# Optimizing a Trainium2 kernel written in Bass

```python
import numpy as np
import jax
import jax.numpy as jnp

def _softmax(x, axis=-1):
    return jax.nn.softmax(x, axis=axis)

def _gelu(x):
    return jax.nn.gelu(x, approximate=True)

def _silu(x):
    return jax.nn.silu(x)

def _sigmoid(x):
    return jax.nn.sigmoid(x)

def _layernorm(x, axis=-1, eps=1e-05):
    m = jnp.mean(x, axis=axis, keepdims=True)
    v = jnp.var(x, axis=axis, keepdims=True)
    return (x - m) / jnp.sqrt(v + eps)

def _scatter_add(tgt, idx, src, axis=0):
    return tgt.at[idx].add(src)

def _segment_sum(src, seg, n):
    return jax.ops.segment_sum(src, seg, n)
kernel_name = 'mk_gnn_resnorm_d4_gnn_r8_c5d5e4'

def setup_inputs(seed: int=0):
    np.random.seed(seed)
    _w = jnp.asarray

    def _rec_inputs():
        import jax
        import jax.numpy as jnp
        _gk = jax.random.key(seed)
        x = -0.000202 + 1 * jax.random.normal(jax.random.fold_in(_gk, 1), (6250, 128), jnp.float32)
        src = jax.random.randint(jax.random.fold_in(_gk, 2), (100000,), 0, 6250, jnp.int32)
        dst = jax.random.randint(jax.random.fold_in(_gk, 3), (100000,), 0, 6250, jnp.int32)
        _o = jnp.argsort(dst, stable=True)
        src = src[_o]
        dst = dst[_o]
        edge_attr_32 = 0.000196303 + 1.00016 * jax.random.normal(jax.random.fold_in(_gk, 11), (100000, 32), jnp.float32)
        edge_type_8 = jax.random.randint(jax.random.fold_in(_gk, 13), (100000,), 0, 8, jnp.int32)
        return (x, src, dst, edge_attr_32, edge_type_8)
    x, src, dst, edge_attr_32, edge_type_8 = _rec_inputs()

    def _L0_gnn_setup():
        import jax, jax.numpy as jnp
        import numpy as np
        import math
        N, E = (6250, 100000)
        HID, EDIM, H = (128, 32, 8)
        D = HID // H
        FFN = 4 * HID
        EPS = 1e-05

        def layer_norm(x, g, b):
            mu = jnp.mean(x, axis=-1, keepdims=True)
            var = jnp.var(x, axis=-1, keepdims=True)
            return (x - mu) * jax.lax.rsqrt(var + EPS) * g + b
        key = jax.random.key(seed)
        ks = jax.random.split(key, 16)
        s = 1.0 / math.sqrt(HID)
        inp = {'x': jax.random.normal(ks[0], (N, HID), jnp.float32), 'edge_index': jax.random.randint(ks[1], (2, E), 0, N, jnp.int32), 'edge_attr': jax.random.normal(ks[2], (E, EDIM), jnp.float32), 'qW': jax.random.normal(ks[3], (HID, HID), jnp.float32) * s, 'qb': jnp.zeros((HID,), jnp.float32), 'kW': jax.random.normal(ks[4], (HID, HID), jnp.float32) * s, 'kb': jnp.zeros((HID,), jnp.float32), 'vW': jax.random.normal(ks[5], (HID, HID), jnp.float32) * s, 'vb': jnp.zeros((HID,), jnp.float32), 'eW': jax.random.normal(ks[6], (EDIM, H), jnp.float32) / math.sqrt(EDIM), 'eb': jnp.zeros((H,), jnp.float32), 'oW': jax.random.normal(ks[7], (HID, HID), jnp.float32) * s, 'ob': jnp.zeros((HID,), jnp.float32), 'ln1_g': jnp.ones((HID,), jnp.float32), 'ln1_b': jnp.zeros((HID,), jnp.float32), 'f1W': jax.random.normal(ks[8], (HID, FFN), jnp.float32) * s, 'f1b': jnp.zeros((FFN,), jnp.float32), 'lnf_g': jnp.ones((FFN,), jnp.float32), 'lnf_b': jnp.zeros((FFN,), jnp.float32), 'f2W': jax.random.normal(ks[9], (FFN, HID), jnp.float32) / math.sqrt(FFN), 'f2b': jnp.zeros((HID,), jnp.float32), 'ln2_g': jnp.ones((HID,), jnp.float32), 'ln2_b': jnp.zeros((HID,), jnp.float32)}
        return inp
    _L0_gnn_all = _L0_gnn_setup()
    _L0_gnn_in = {k: v for k, v in _L0_gnn_all.items() if k in ('qW', 'qb', 'kW', 'kb', 'vW', 'vb', 'eW', 'eb', 'oW', 'ob', 'ln1_g', 'ln1_b', 'f1W', 'f1b', 'lnf_g', 'lnf_b', 'f2W', 'f2b', 'ln2_g', 'ln2_b')}
    del _L0_gnn_all

    def _L1_gnn_setup():
        import jax, jax.numpy as jnp
        import numpy as np
        K = 5
        ALPHA = 0.8
        N_NODES = 6250
        N_EDGES = 100000
        D_FEAT = 128
        key = jax.random.key(seed)
        k1, k2 = jax.random.split(key)
        x = jax.random.normal(k1, (N_NODES, D_FEAT), dtype=jnp.float32)
        edge_index = jax.random.randint(k2, (2, N_EDGES), 0, N_NODES, dtype=jnp.int32)
        return {'x': x, 'edge_index': edge_index}
    _L1_gnn_all = _L1_gnn_setup()
    _L1_gnn_in = {k: v for k, v in _L1_gnn_all.items() if k in ()}
    del _L1_gnn_all

    def _L2_gnn_setup():
        import jax, jax.numpy as jnp
        import numpy as np
        N = 3750
        E = 60000
        IN_DIM = 128
        HID = 32
        HEADS = 4
        OUT_DIM = 128
        NEG_SLOPE = 0.2
        EPS = 1e-16

        def _gat_conv(x, src, dst, W, a_src, a_dst, bias, heads, ch, concat):
            n = x.shape[0]
            h = (x @ W).reshape(n, heads, ch)
            alpha_s = jnp.einsum('nhc,hc->nh', h, a_src)
            alpha_d = jnp.einsum('nhc,hc->nh', h, a_dst)
            e = jax.nn.leaky_relu(alpha_s[src] + alpha_d[dst], NEG_SLOPE)
            m = jax.ops.segment_max(e, dst, num_segments=n)
            m = jnp.where(jnp.isfinite(m), m, 0.0)
            ex = jnp.exp(e - m[dst])
            denom = jax.ops.segment_sum(ex, dst, num_segments=n)
            alpha = ex / (denom[dst] + EPS)
            out = jax.ops.segment_sum(h[src] * alpha[:, :, None], dst, num_segments=n)
            if concat:
                out = out.reshape(n, heads * ch)
            else:
                out = out.mean(axis=1)
            return out + bias
        key = jax.random.key(seed)
        ks = jax.random.split(key, 12)
        x = jax.random.normal(ks[0], (N, IN_DIM), dtype=jnp.float32)
        edge_index = jax.random.randint(ks[1], (2, E), 0, N, dtype=jnp.int32)

        def glorot(k, shape, fan_in):
            return jax.random.normal(k, shape, dtype=jnp.float32) / np.sqrt(fan_in)
        W1 = glorot(ks[2], (IN_DIM, HEADS * HID), IN_DIM)
        a_src1 = glorot(ks[3], (HEADS, HID), HID)
        a_dst1 = glorot(ks[4], (HEADS, HID), HID)
        b1 = jnp.zeros((HEADS * HID,), dtype=jnp.float32)
        W2 = glorot(ks[5], (HEADS * HID, OUT_DIM), HEADS * HID)
        a_src2 = glorot(ks[6], (1, OUT_DIM), OUT_DIM)
        a_dst2 = glorot(ks[7], (1, OUT_DIM), OUT_DIM)
        b2 = jnp.zeros((OUT_DIM,), dtype=jnp.float32)
        return {'x': x, 'edge_index': edge_index, 'W1': W1, 'a_src1': a_src1, 'a_dst1': a_dst1, 'b1': b1, 'W2': W2, 'a_src2': a_src2, 'a_dst2': a_dst2, 'b2': b2}
    _L2_gnn_all = _L2_gnn_setup()
    _L2_gnn_in = {k: v for k, v in _L2_gnn_all.items() if k in ('W1', 'a_src1', 'a_dst1', 'b1', 'W2', 'a_src2', 'a_dst2', 'b2')}
    del _L2_gnn_all

    def _L3_gnn_setup():
        import jax, jax.numpy as jnp
        import numpy as np
        N_NODES = 6250
        N_EDGES = 100000
        IN_DIM = 128
        OUT_DIM = 128
        N_REL = 8
        key = jax.random.key(seed)
        k1, k2, k3, k4, k5, k6 = jax.random.split(key, 6)
        x = jax.random.normal(k1, (N_NODES, IN_DIM), dtype=jnp.float32)
        edge_index = jax.random.randint(k2, (2, N_EDGES), 0, N_NODES, dtype=jnp.int64)
        edge_type = jax.random.randint(k3, (N_EDGES,), 0, N_REL, dtype=jnp.int64)
        scale = 1.0 / np.sqrt(IN_DIM)
        weight = jax.random.normal(k4, (N_REL, IN_DIM, OUT_DIM), dtype=jnp.float32) * scale
        root = jax.random.normal(k5, (IN_DIM, OUT_DIM), dtype=jnp.float32) * scale
        bias = jax.random.normal(k6, (OUT_DIM,), dtype=jnp.float32) * 0.01
        return {'x': x, 'edge_index': edge_index, 'edge_type': edge_type, 'weight': weight, 'root': root, 'bias': bias}
    _L3_gnn_all = _L3_gnn_setup()
    _L3_gnn_in = {k: v for k, v in _L3_gnn_all.items() if k in ('weight', 'root', 'bias')}
    del _L3_gnn_all
    return {'x': x, 'src': src, 'dst': dst, 'edge_attr_32': edge_attr_32, 'edge_type_8': edge_type_8, 'L0_gnn_qW': _L0_gnn_in['qW'], 'L0_gnn_qb': _L0_gnn_in['qb'], 'L0_gnn_kW': _L0_gnn_in['kW'], 'L0_gnn_kb': _L0_gnn_in['kb'], 'L0_gnn_vW': _L0_gnn_in['vW'], 'L0_gnn_vb': _L0_gnn_in['vb'], 'L0_gnn_eW': _L0_gnn_in['eW'], 'L0_gnn_eb': _L0_gnn_in['eb'], 'L0_gnn_oW': _L0_gnn_in['oW'], 'L0_gnn_ob': _L0_gnn_in['ob'], 'L0_gnn_ln1_g': _L0_gnn_in['ln1_g'], 'L0_gnn_ln1_b': _L0_gnn_in['ln1_b'], 'L0_gnn_f1W': _L0_gnn_in['f1W'], 'L0_gnn_f1b': _L0_gnn_in['f1b'], 'L0_gnn_lnf_g': _L0_gnn_in['lnf_g'], 'L0_gnn_lnf_b': _L0_gnn_in['lnf_b'], 'L0_gnn_f2W': _L0_gnn_in['f2W'], 'L0_gnn_f2b': _L0_gnn_in['f2b'], 'L0_gnn_ln2_g': _L0_gnn_in['ln2_g'], 'L0_gnn_ln2_b': _L0_gnn_in['ln2_b'], 'L2_gnn_W1': _L2_gnn_in['W1'], 'L2_gnn_a_src1': _L2_gnn_in['a_src1'], 'L2_gnn_a_dst1': _L2_gnn_in['a_dst1'], 'L2_gnn_b1': _L2_gnn_in['b1'], 'L2_gnn_W2': _L2_gnn_in['W2'], 'L2_gnn_a_src2': _L2_gnn_in['a_src2'], 'L2_gnn_a_dst2': _L2_gnn_in['a_dst2'], 'L2_gnn_b2': _L2_gnn_in['b2'], 'L3_gnn_weight': _L3_gnn_in['weight'], 'L3_gnn_root': _L3_gnn_in['root'], 'L3_gnn_bias': _L3_gnn_in['bias']}

def reference(x, src, dst, edge_attr_32, edge_type_8, L0_gnn_qW, L0_gnn_qb, L0_gnn_kW, L0_gnn_kb, L0_gnn_vW, L0_gnn_vb, L0_gnn_eW, L0_gnn_eb, L0_gnn_oW, L0_gnn_ob, L0_gnn_ln1_g, L0_gnn_ln1_b, L0_gnn_f1W, L0_gnn_f1b, L0_gnn_lnf_g, L0_gnn_lnf_b, L0_gnn_f2W, L0_gnn_f2b, L0_gnn_ln2_g, L0_gnn_ln2_b, L2_gnn_W1, L2_gnn_a_src1, L2_gnn_a_dst1, L2_gnn_b1, L2_gnn_W2, L2_gnn_a_src2, L2_gnn_a_dst2, L2_gnn_b2, L3_gnn_weight, L3_gnn_root, L3_gnn_bias):
    import jax
    import jax.numpy as jnp

    def _L0_gnn_ref(x, edge_index, edge_attr, qW, qb, kW, kb, vW, vb, eW, eb, oW, ob, ln1_g, ln1_b, f1W, f1b, lnf_g, lnf_b, f2W, f2b, ln2_g, ln2_b):
        import jax, jax.numpy as jnp
        import numpy as np
        import math
        N, E = (6250, 100000)
        HID, EDIM, H = (128, 32, 8)
        D = HID // H
        FFN = 4 * HID
        EPS = 1e-05

        def layer_norm(x, g, b):
            mu = jnp.mean(x, axis=-1, keepdims=True)
            var = jnp.var(x, axis=-1, keepdims=True)
            return (x - mu) * jax.lax.rsqrt(var + EPS) * g + b
        src, dst = (edge_index[0], edge_index[1])
        q = (x @ qW + qb).reshape(N, H, D)
        k = (x @ kW + kb).reshape(N, H, D)
        v = (x @ vW + vb).reshape(N, H, D)
        edge_bias = edge_attr @ eW + eb
        scores = jnp.sum(q[src] * k[dst], axis=-1) / math.sqrt(D) + edge_bias
        mx = jax.ops.segment_max(scores, dst, num_segments=N)
        mx = jnp.where(jnp.isinf(mx), jnp.zeros_like(mx), mx)
        ex = jnp.exp(scores - mx[dst])
        den = jax.ops.segment_sum(ex, dst, num_segments=N)
        den = jnp.maximum(den, 1e-08)
        attn = ex / den[dst]
        wv = v[src] * attn[:, :, None]
        out = jax.ops.segment_sum(wv, dst, num_segments=N)
        out = out.reshape(N, HID) @ oW + ob
        x = layer_norm(x + out, ln1_g, ln1_b)
        h = x @ f1W + f1b
        h = jax.nn.gelu(layer_norm(h, lnf_g, lnf_b), approximate=False)
        h = h @ f2W + f2b
        x = layer_norm(x + h, ln2_g, ln2_b)
        return x

    def _L1_gnn_ref(x, edge_index):
        import jax, jax.numpy as jnp
        import numpy as np
        K = 5
        ALPHA = 0.8
        N_NODES = 6250
        N_EDGES = 100000
        D_FEAT = 128
        'APPNP propagation: x_{k+1} = (1-alpha) * A_hat @ x_k + alpha * x_0,\n            with A_hat the GCN-normalized adjacency (self-loops added, D^-1/2 A D^-1/2).'
        n = x.shape[0]
        row, col = (edge_index[0], edge_index[1])
        loop = jnp.arange(n, dtype=edge_index.dtype)
        row = jnp.concatenate([row, loop])
        col = jnp.concatenate([col, loop])
        ones = jnp.ones(row.shape[0], dtype=x.dtype)
        deg = jax.ops.segment_sum(ones, col, num_segments=n)
        dinv = jnp.where(deg > 0, jax.lax.rsqrt(deg), 0.0).astype(x.dtype)
        norm = (dinv[row] * dinv[col])[:, None]
        h = x
        for _ in range(K):
            msg = norm * h[row]
            agg = jax.ops.segment_sum(msg, col, num_segments=n)
            h = (1.0 - ALPHA) * agg + ALPHA * x
        return h

    def _L2_gnn_ref(x, edge_index, W1, a_src1, a_dst1, b1, W2, a_src2, a_dst2, b2):
        import jax, jax.numpy as jnp
        import numpy as np
        N = 3750
        E = 60000
        IN_DIM = 128
        HID = 32
        HEADS = 4
        OUT_DIM = 128
        NEG_SLOPE = 0.2
        EPS = 1e-16

        def _gat_conv(x, src, dst, W, a_src, a_dst, bias, heads, ch, concat):
            n = x.shape[0]
            h = (x @ W).reshape(n, heads, ch)
            alpha_s = jnp.einsum('nhc,hc->nh', h, a_src)
            alpha_d = jnp.einsum('nhc,hc->nh', h, a_dst)
            e = jax.nn.leaky_relu(alpha_s[src] + alpha_d[dst], NEG_SLOPE)
            m = jax.ops.segment_max(e, dst, num_segments=n)
            m = jnp.where(jnp.isfinite(m), m, 0.0)
            ex = jnp.exp(e - m[dst])
            denom = jax.ops.segment_sum(ex, dst, num_segments=n)
            alpha = ex / (denom[dst] + EPS)
            out = jax.ops.segment_sum(h[src] * alpha[:, :, None], dst, num_segments=n)
            if concat:
                out = out.reshape(n, heads * ch)
            else:
                out = out.mean(axis=1)
            return out + bias
        loops = jnp.arange(N, dtype=edge_index.dtype)
        src = jnp.concatenate([edge_index[0], loops])
        dst = jnp.concatenate([edge_index[1], loops])
        h = _gat_conv(x, src, dst, W1, a_src1, a_dst1, b1, HEADS, HID, concat=True)
        h = jax.nn.elu(h)
        out = _gat_conv(h, src, dst, W2, a_src2, a_dst2, b2, 1, OUT_DIM, concat=False)
        return out

    def _L3_gnn_ref(x, edge_index, edge_type, weight, root, bias):
        import jax, jax.numpy as jnp
        import numpy as np
        N_NODES = 6250
        N_EDGES = 100000
        IN_DIM = 128
        OUT_DIM = 128
        N_REL = 8
        src, dst = (edge_index[0], edge_index[1])
        h_src = x[src]
        out = x @ root + bias
        for r in range(N_REL):
            mask = (edge_type == r).astype(x.dtype)
            msg = h_src * mask[:, None] @ weight[r]
            agg = jax.ops.segment_sum(msg, dst, num_segments=N_NODES)
            cnt = jax.ops.segment_sum(mask, dst, num_segments=N_NODES)
            out = out + agg / jnp.maximum(cnt, 1.0)[:, None]
        return out
    edge_index = jnp.stack([src, dst])
    x = _layernorm(x + _L0_gnn_ref(x, edge_index, edge_attr_32, L0_gnn_qW, L0_gnn_qb, L0_gnn_kW, L0_gnn_kb, L0_gnn_vW, L0_gnn_vb, L0_gnn_eW, L0_gnn_eb, L0_gnn_oW, L0_gnn_ob, L0_gnn_ln1_g, L0_gnn_ln1_b, L0_gnn_f1W, L0_gnn_f1b, L0_gnn_lnf_g, L0_gnn_lnf_b, L0_gnn_f2W, L0_gnn_f2b, L0_gnn_ln2_g, L0_gnn_ln2_b), axis=-1)
    x = _layernorm(x + _L1_gnn_ref(x, edge_index), axis=-1)
    x = _layernorm(x + _L2_gnn_ref(x, edge_index, L2_gnn_W1, L2_gnn_a_src1, L2_gnn_a_dst1, L2_gnn_b1, L2_gnn_W2, L2_gnn_a_src2, L2_gnn_a_dst2, L2_gnn_b2), axis=-1)
    x = _layernorm(x + _L3_gnn_ref(x, edge_index, edge_type_8, L3_gnn_weight, L3_gnn_root, L3_gnn_bias), axis=-1)
    return x

_drawn_inputs = setup_inputs


def setup_inputs(seed=0):
    import zlib

    import numpy as np

    out = dict(_drawn_inputs(seed))
    spreads = {'L0_gnn_qb': (0.0, 0.8),
     'L0_gnn_kb': (0.0, 0.466),
     'L0_gnn_vb': (0.0, 0.1),
     'L0_gnn_eb': (0.0, 0.8),
     'L0_gnn_ob': (0.0, 0.1),
     'L0_gnn_ln1_g': (1.0, 0.2),
     'L0_gnn_ln1_b': (0.0, 0.1),
     'L0_gnn_f1b': (0.0, 0.1),
     'L0_gnn_lnf_g': (1.0, 0.2),
     'L0_gnn_lnf_b': (0.0, 0.1),
     'L0_gnn_f2b': (0.0, 0.1),
     'L0_gnn_ln2_g': (1.0, 0.2),
     'L0_gnn_ln2_b': (0.0, 0.1),
     'L2_gnn_b1': (0.0, 0.1),
     'L2_gnn_b2': (0.0, 0.1)}
    factors = {'L2_gnn_a_dst1': 3.218, 'L2_gnn_a_src2': 3.216, 'L2_gnn_a_dst2': 8.0, 'L3_gnn_bias': 8.0}
    for name, (base, spread) in spreads.items():
        noise = np.random.default_rng([zlib.crc32(name.encode()), seed]).standard_normal(out[name].shape)
        drawn = base * np.exp(spread * noise) if base else spread * noise
        out[name] = jnp.asarray(drawn.astype(out[name].dtype))
    for name, factor in factors.items():
        out[name] = (out[name] * factor).astype(out[name].dtype)
    return out
```

```python
from contextlib import ExitStack, contextmanager

import concourse.bass as bass
from concourse import mybir
from concourse.alu_op_type import AluOpType as ALU

ACT = mybir.ActivationFunctionType
AX = mybir.AxisListType.X
F32 = mybir.dt.float32
I32 = mybir.dt.int32
ENG = mybir.EngineType

P = 128
N, E, D, FFN, EDIM, NREL = 6250, 100000, 128, 512, 32, 8
H0 = 8
SELF_LOOPS = 3750
FULL, TAIL = N // P, N % P
TILES = FULL + 1
NT = TILES + TILES % 2
NP = NT * P
U = 4
NCH = -(-((E + TILES * (P - 1)) // P) // (2 * U)) * (2 * U)
NG = NCH // U
PADC = NCH + U
EP, EC = 125, E // 125
RECW = 12
R_SRC, R_DST, R_TYP, R_NEXT, R_BIAS = 0, 1, 2, 3, 4
ROUND = 16
BIG = 1.0e30
EPS = 1e-5


class Core:
    pass


def after(eng, sem, value):
    if isinstance(value, int) and value <= 0:
        return
    eng.wait_ge(sem, value)


def apart(eng, sem, value):
    if isinstance(value, int) and value <= 0:
        return
    eng.wait_ge(sem, value)
    eng.nop(nofuse=True)


def in_pairs(eng, n, body):
    body(0, 0, 0)
    body(1, 1, 0)
    with eng.Fori(1, n // 2) as i:
        body(i * 2, 0, i)
        body(i * 2 + 1, 1, i)


def tiles_of_chunks(nc, m, engine, j):
    _, tiles = nc.values_load_multi_w_load_instructions(
        m.chunk_tile[0:1, bass.ds(j * U, U)], engines=[engine], min_val=0, max_val=TILES - 1)
    return tiles


def cols(j, n=U):
    return bass.ds(j * n, n)


@contextmanager
def semaphores(nc):
    with ExitStack() as ctx:
        handles = []

        def sem(name):
            handles.append(ctx.enter_context(nc.semaphore(name)))
            return handles[-1]

        yield sem
        with nc.Block() as block:
            @block.gpsimd
            def _(pool):
                for handle in handles:
                    pool.sem_clear(handle)


def load_constants(nc, m, A, sem):
    s_w, s_z, s_id = sem("weights_loaded"), sem("constants_zeroed"), sem("constants_made")
    s_i, s_row = sem("iota_done"), sem("rows_loaded")
    with nc.Block() as block:
        @block.sync
        def _(sp):
            n = 0

            def load(dst, src):
                nonlocal n
                sp.dma_start(dst, src).then_inc(s_w, 16)
                n += 16

            sp.wait_ge(s_z, 3)
            load(m.X[:, 0:FULL, :], A["x"][0:FULL * P, :].rearrange("(t p) d -> p t d", p=P))
            load(m.X[0:TAIL, FULL, :], A["x"][FULL * P:N, :])
            for e in range(P // EDIM):
                load(m.edge_w[e * EDIM:(e + 1) * EDIM, e * H0:(e + 1) * H0], A["L0_gnn_eW"])
            load(m.w_vqk[:, 0:D], A["L0_gnn_vW"])
            load(m.w_vqk[:, D:2 * D], A["L0_gnn_qW"])
            load(m.w_vqk[:, 2 * D:3 * D], A["L0_gnn_kW"])
            load(m.w_o[:, :], A["L0_gnn_oW"])
            load(m.w_f1[:, :], A["L0_gnn_f1W"])
            load(m.w_f2[:, :, :], A["L0_gnn_f2W"].rearrange("(c k) n -> k c n", k=P))
            load(m.w_g1[:, :], A["L2_gnn_W1"])
            load(m.w_g2[:, :], A["L2_gnn_W2"])
            load(m.w_rel[:, 0:NREL, :], A["L3_gnn_weight"].rearrange("r k n -> k r n"))
            load(m.w_rel[:, NREL, :], A["L3_gnn_root"])
            sp.wait_ge(s_w, n)

        @block.scalar
        def _(act):
            rows = [(m.b_vqk[:, 0:D], A["L0_gnn_vb"]), (m.b_vqk[:, D:2 * D], A["L0_gnn_qb"]),
                    (m.b_vqk[:, 2 * D:3 * D], A["L0_gnn_kb"]), (m.b_edge[:, :], A["L0_gnn_eb"]),
                    (m.b_o[:, :], A["L0_gnn_ob"]), (m.g_ln1[:, :], A["L0_gnn_ln1_g"]),
                    (m.b_ln1[:, :], A["L0_gnn_ln1_b"]), (m.b_f1[:, :], A["L0_gnn_f1b"]),
                    (m.g_lnf[:, :], A["L0_gnn_lnf_g"]), (m.b_lnf[:, :], A["L0_gnn_lnf_b"]),
                    (m.b_f2[:, :], A["L0_gnn_f2b"]), (m.g_ln2[:, :], A["L0_gnn_ln2_g"]),
                    (m.b_ln2[:, :], A["L0_gnn_ln2_b"]), (m.b_g1[:, :], A["L2_gnn_b1"]),
                    (m.b_g2[:, :], A["L2_gnn_b2"]), (m.b_rel[:, :], A["L3_gnn_bias"]),
                    (m.a_src1[:, :], A["L2_gnn_a_src1"].rearrange("h c -> (h c)")),
                    (m.a_dst1[:, :], A["L2_gnn_a_dst1"].rearrange("h c -> (h c)")),
                    (m.a_src2[:, :], A["L2_gnn_a_src2"].rearrange("h c -> (h c)")),
                    (m.a_dst2[:, :], A["L2_gnn_a_dst2"].rearrange("h c -> (h c)"))]
            for dst, src in rows:
                act.dma_start(dst, src.partition_broadcast(P)).then_inc(s_row, 16)
            act.wait_ge(s_row, 16 * len(rows))

        @block.vector
        def _(dve):
            dve.memset(m.X[:, :, :], 0.0).then_inc(s_z, 1)
            dve.memset(m.edge_w[:, :], 0.0).then_inc(s_z, 1)
            dve.memset(m.ident[:, :], 0.0).then_inc(s_z, 1)
            dve.memset(m.ones[:, :], 1.0).then_inc(s_z, 1)
            dve.memset(m.minus_half[:, :], -0.5)
            dve.wait_ge(s_i, 3)
            dve.tensor_copy(m.node_ramp[:, :], m.node_ramp_i[:, :]).then_inc(s_id, 1)
            dve.tensor_copy(m.node_id[:, :], m.node_i[:, :]).then_inc(s_id, 1)
            dve.tensor_copy(m.slot[:, :], m.slot_i[:, :]).then_inc(s_id, 1)
            dve.wait_ge(s_id, 5)
            dve.tensor_scalar(m.has_loop[:, :], m.node_id[:, :], float(SELF_LOOPS), None,
                              ALU.is_lt).then_inc(s_id, 1)

        @block.gpsimd
        def _(pool):
            pool.iota(m.node_ramp_i[:, :], [[1, P]], base=0, channel_multiplier=0).then_inc(s_i, 1)
            pool.iota(m.node_i[:, :], [[P, NT]], base=0, channel_multiplier=1).then_inc(s_i, 1)
            pool.iota(m.slot_i[:, :], [[0, 1]], base=0, channel_multiplier=1).then_inc(s_i, 1)
            pool.wait_ge(s_z, 4)
            pool.affine_select(out=m.ident[:, :], in_=m.ident[:, :], compare_op=ALU.not_equal, fill=1.0,
                               base=0, pattern=[[-1, P]], channel_multiplier=1).then_inc(s_id, 1)
            pool.affine_select(out=m.upto[:, :], in_=m.ones[:, 0:TILES], compare_op=ALU.is_ge, fill=0.0,
                               base=0, pattern=[[1, TILES]], channel_multiplier=-1).then_inc(s_id, 1)


def build_records(nc, m, A, sem):
    s_e, s_nextz = sem("edge_lists_loaded"), sem("next_dst_cleared")
    s_attr = [sem(f"attr_loaded{k}") for k in range(2)]
    s_rec_out = m.s_gather
    s_tr, s_trc, s_bias, s_rec = sem("attr_turned"), sem("attr_turned_copied"), sem("bias_made"), sem("record_made")
    s_pad, s_padout, s_cnt = sem("pad_made"), sem("pad_stored"), sem("edges_counted")
    rounds = EC // ROUND
    with ExitStack() as ctx:
        def sb(name, shape, dt=F32):
            return ctx.enter_context(nc.sbuf_tensor(name, shape, dt))

        room = m.own[0:EP, :, :].rearrange("p t d -> p (t d)")
        src_i, dst_i, typ_i, next_i = (room[:, k * EC:(k + 1) * EC].bitcast(I32) for k in range(4))
        dst_f, below = (room[:, k * EC:(k + 1) * EC] for k in (4, 5))
        edges_below = sb("edges_below", [EP, TILES + 1])
        attr = sb("attr", [EP, 2, ROUND * EDIM])
        attr_t = sb("attr_t", [P, 2, 4, P])
        rec = sb("rec", [EP, 2, ROUND, RECW])
        pad = sb("pad", [P, RECW])
        rec_i = rec[:, :, :, :].bitcast(I32)
        attr_d = A["edge_attr_32"].rearrange("(p i) k -> p (i k)", p=EP)
        rec_d = m.rec_dram[0:E, :].rearrange("(p i) w -> p i w", p=EP)

        with nc.Block() as block:
            @block.sync
            def _(sp):
                flat = lambda a: a.rearrange("(p i) -> p i", p=EP)
                sp.dma_start(dst_i[:, :], flat(A["dst"])).then_inc(s_e, 16)
                sp.dma_start(src_i[:, :], flat(A["src"])).then_inc(s_e, 16)
                sp.dma_start(typ_i[:, :], flat(A["edge_type_8"])).then_inc(s_e, 16)
                sp.wait_ge(s_nextz, 1)
                sp.dma_start(next_i[0:EP - 1, :], A["dst"][1:1 + (EP - 1) * EC].rearrange(
                    "(p i) -> p i", i=EC)).then_inc(s_e, 16)
                sp.dma_start(next_i[EP - 1:EP, 0:EC - 1], A["dst"][1 + (EP - 1) * EC:E].rearrange(
                    "(a i) -> a i", a=1)).then_inc(s_e, 16)

                def load(r, k, i):
                    after(sp, s_tr, r - 1)
                    sp.dma_start(attr[:, k, :], attr_d[:, bass.ds(r * (ROUND * EDIM), ROUND * EDIM)]
                                 ).then_inc(s_attr[k], 16)
                in_pairs(sp, rounds, load)
                sp.wait_ge(s_pad, 2)
                sp.dma_start(m.rec_dram[E:E + P, :], pad[:, :]).then_inc(s_padout, 16)
                sp.wait_ge(s_padout, 16)

            @block.tensor
            def _(pe):
                def turn(r, k, i):
                    pe.wait_ge(s_attr[k], i * 16 + 16)
                    for q in range(4):
                        last = pe.transpose(m.ps_t[:, k, q * P:q * P + EP], attr[:, k, q * P:(q + 1) * P],
                                            m.ident[0:EP, 0:EP])
                    last.then_inc(s_tr, 1)
                    pe.wait_ge(s_trc, r + 1)
                    after(pe, s_rec, r - 1)
                    for q in range(4):
                        last = pe.matmul(m.ps_k[0:EP, k, q * EDIM:(q + 1) * EDIM], attr_t[:, k, q, 0:EP],
                                         m.edge_w[:, :], start=True, stop=True)
                    last.then_inc(s_bias, 1)
                in_pairs(pe, rounds, turn)

            @block.scalar
            def _(act):
                def copy(r, k, i):
                    after(act, s_bias, r - 1)
                    act.wait_ge(s_tr, r + 1)
                    act.copy(attr_t[:, k, :, 0:EP], m.ps_t[:, k, :].rearrange("p (q e) -> p q e", q=4)[:, :, 0:EP]
                             ).then_inc(s_trc, 1)
                in_pairs(act, rounds, copy)

            @block.vector
            def _(dve):
                dve.memset(next_i[:, :], -1).then_inc(s_nextz, 1)
                dve.memset(pad[:, :], 0.0).then_inc(s_pad, 1)
                dve.wait_ge(s_pad, 1)
                dve.memset(pad[:, R_DST:R_DST + 1], 1.0e7).then_inc(s_pad, 1)
                dve.wait_ge(s_e, 16 * 5)
                dve.tensor_copy(dst_f[:, :], dst_i[:, :]).then_inc(s_cnt, 1)
                dve.memset(edges_below[:, 0:1], 0.0).then_inc(s_cnt, 1)
                dve.wait_ge(s_cnt, 2)
                for t in range(TILES):
                    dve.tensor_scalar(below[:, :], dst_f[:, :], float((t + 1) * P), None, ALU.is_lt
                                      ).then_inc(s_cnt, 1)
                    dve.wait_ge(s_cnt, 3 + 2 * t)
                    dve.tensor_reduce(edges_below[:, t + 1:t + 2], below[:, :], AX, ALU.add).then_inc(s_cnt, 1)
                    dve.wait_ge(s_cnt, 4 + 2 * t)
                dve.tensor_tensor(m.tile_edges[:, :], edges_below[:, 1:TILES + 1], edges_below[:, 0:TILES],
                                  ALU.subtract).then_inc(s_cnt, 1)

                def record(r, k, i):
                    after(dve, s_rec_out[k], i * 16)
                    dve.wait_ge(s_bias, r + 1)
                    at = bass.ds(r * ROUND, ROUND)
                    dve.tensor_copy(rec_i[:, k, :, R_SRC], src_i[:, at])
                    dve.tensor_copy(rec[:, k, :, R_DST], dst_i[:, at])
                    dve.tensor_copy(rec[:, k, :, R_TYP], typ_i[:, at])
                    dve.tensor_copy(rec[:, k, :, R_NEXT], next_i[:, at])
                    dve.tensor_tensor(rec[:, k, :, R_BIAS:R_BIAS + H0],
                                      m.ps_k[0:EP, k, 0:4 * EDIM].rearrange("p (e h) -> p e h", h=H0),
                                      m.b_edge[0:EP, :].unsqueeze(1).broadcast_to([EP, ROUND, H0]),
                                      ALU.add).then_inc(s_rec, 1)
                in_pairs(dve, rounds, record)

            @block.gpsimd
            def _(pool):
                def store(r, k, i):
                    apart(pool, s_rec, r + 1)
                    pool.dma_start(rec_d[:, bass.ds(r * ROUND, ROUND), :], rec[:, k, :, :]).then_inc(s_rec_out[k], 16)
                in_pairs(pool, rounds, store)
                for k in range(2):
                    pool.wait_ge(s_rec_out[k], 16 * (rounds // 2))
    m.gathered += 16 * (rounds // 2)


def plan_chunks(nc, m, A, sem):
    s_pe, s_v, s_plan, s_r = sem("plan_products"), sem("plan_steps"), sem("plan_made"), [
        sem("records_in_sp"), sem("records_in_act")]
    s_ramp = sem("chunk_ramp_made")
    half = NCH // 2
    with ExitStack() as ctx:
        def sb(name, shape, dt=F32):
            return ctx.enter_context(nc.sbuf_tensor(name, shape, dt))

        cnt, cnt_i, nch = sb("cnt", [TILES, 1]), sb("cnt_i", [TILES, 1], I32), sb("nch", [TILES, 1])
        slack, last = sb("slack", [TILES, 1]), sb("last_chunk", [TILES, 1])
        past, first = sb("past", [TILES, NCH]), sb("first_edge", [1, NCH])
        first_i = sb("first_edge_i", [1, NCH], I32)
        tile_f = sb("tile_f", [P, NCH])
        ramp = sb("chunk_ramp", [TILES, NCH])
        with nc.Block() as block:
            @block.tensor
            def _(pe):
                pe.matmul(m.ps_t[0:TILES, 0, 0:1], m.tile_edges[:, :], m.ones[0:EP, 0:1], start=True, stop=True
                          ).then_inc(s_pe, 1)
                pe.wait_ge(s_v, 6)
                pe.matmul(m.ps_k[0:TILES, 0, 0:1], m.upto[0:TILES, :], nch[:, :], start=True, stop=True
                          ).then_inc(s_pe, 1)
                pe.wait_ge(s_v, 9)
                for h in range(2):
                    part = past[:, h * half:(h + 1) * half]
                    pe.matmul(m.ps_o[:, 0, h, 0:half], m.ones[0:TILES, :], part, start=True, stop=True)
                    pe.matmul(m.ps_o[0:1, 1, h, 0:half], slack[:, :], part, start=True, stop=True
                              ).then_inc(s_pe, 1)

            @block.vector
            def _(dve):
                n = 0

                def step(ins):
                    nonlocal n
                    n += 1
                    ins.then_inc(s_v, 1)
                    dve.wait_ge(s_v, n)

                dve.wait_ge(s_ramp, 1)
                step(dve.tensor_copy(ramp[:, :], m.dst_slot[0:TILES, 0:NCH].bitcast(I32)))
                dve.wait_ge(s_pe, 1)
                step(dve.tensor_copy(cnt[:, :], m.ps_t[0:TILES, 0, 0:1]))
                step(dve.tensor_scalar(cnt_i[:, :], cnt[:, :], float(P - 1), None, ALU.add))
                step(dve.tensor_scalar(cnt_i[:, :], cnt_i[:, :], 7, None, ALU.arith_shift_right))
                step(dve.tensor_copy(nch[:, :], cnt_i[:, :]))
                step(dve.scalar_tensor_tensor(slack[:, :], nch[:, :], -float(P), cnt[:, :], ALU.mult, ALU.add))
                dve.wait_ge(s_pe, 2)
                step(dve.tensor_copy(last[:, :], m.ps_k[0:TILES, 0, 0:1]))
                step(dve.tensor_scalar(past[:, :], ramp[:, :], last[:, 0:1], None, ALU.is_ge))
                step(dve.memset(m.dst_slot[:, :], -1.0))
                dve.wait_ge(s_pe, 4)
                step(dve.tensor_scalar(tile_f[:, :].rearrange("p (h c) -> p h c", h=2), m.ps_o[:, 0, :, 0:half],
                                       float(TILES - 1), None, ALU.min))
                step(dve.memset(m.chunk_tile[:, :], 0))
                step(dve.tensor_copy(m.chunk_tile[0:1, 0:NCH], tile_f[0:1, :]))
                step(dve.scalar_tensor_tensor(first[:, :].rearrange("p (h c) -> p h c", h=2),
                                              ramp[0:1, :].rearrange("p (h c) -> p h c", h=2), float(P),
                                              m.ps_o[0:1, 1, :, 0:half], ALU.mult, ALU.add))
                step(dve.tensor_scalar(first_i[:, :], first[:, :], float(E), None, ALU.min))
                dve.sem_inc(s_plan, 1)
                for c in range(2):
                    dve.wait_ge(s_r[c], 16 * half)
                step(dve.tensor_scalar(tile_f[:, :], tile_f[:, :], -float(P), None, ALU.mult))
                step(dve.tensor_tensor(m.dst_slot[:, 0:NCH], m.R[:, :, R_DST], tile_f[:, :], ALU.add))
                step(dve.memset(m.etype[:, :], 0.0))
                step(dve.memset(m.src_idx[:, :], 0))
                step(dve.memset(m.rel_idx[:, :], 0))
                step(dve.memset(m.rel_w[:, :], 0.0))
                step(dve.tensor_copy(m.etype[:, 0:NCH], m.R[:, :, R_TYP]))
                step(dve.tensor_copy(m.src_idx[:, 0:NCH], m.R[:, :, R_SRC].bitcast(I32)))
                step(dve.scalar_tensor_tensor(m.rel_idx[:, 0:NCH], m.src_idx[:, 0:NCH], float(NREL),
                                              m.etype[:, 0:NCH], ALU.mult, ALU.add))
                step(dve.tensor_tensor(m.is_last[:, :], m.R[:, :, R_DST], m.R[:, :, R_NEXT], ALU.not_equal))
                step(dve.tensor_scalar(m.at_end[:, :], m.slot[:, :], float(P - 1), None, ALU.is_equal))
                step(dve.tensor_scalar(m.is_last[:, :], m.is_last[:, :], m.at_end[:, 0:1], None, ALU.max))

            @block.gpsimd
            def _(pool):
                pool.iota(m.dst_slot[0:TILES, 0:NCH].bitcast(I32), [[1, NCH]], base=0, channel_multiplier=0
                          ).then_inc(s_ramp, 1)

            def load_half(eng, engine, c):
                eng.wait_ge(s_plan, 1)
                with eng.Fori(0, half // 4) as i:
                    _, at = nc.values_load_multi_w_load_instructions(
                        first_i[0:1, bass.ds(i * 4 + c * half, 4)], engines=[engine], min_val=0, max_val=E)
                    for u in range(4):
                        eng.dma_start(m.R[:, bass.ds(i * 4 + (c * half + u), 1), :],
                                      m.rec_dram[bass.ds(at[u], P), :].unsqueeze(1)).then_inc(s_r[c], 16)

            @block.sync
            def _(sp):
                load_half(sp, ENG.SP, 0)

            @block.scalar
            def _(act):
                load_half(act, ENG.Activation, 1)


def allocate(nc, ctx):
    def sb(name, shape, dt=F32):
        return ctx.enter_context(nc.sbuf_tensor(name, shape, dt))

    m = Core()
    m.ident, m.ones, m.upto = sb("ident", [P, P]), sb("ones", [P, P]), sb("upto", [P, TILES])
    m.node_i, m.node_id, m.has_loop = sb("node_i", [P, NT], I32), sb("node_id", [P, NT]), sb("has_loop", [P, NT])
    m.slot_i, m.slot, m.at_end = sb("slot_i", [P, 1], I32), sb("slot", [P, 1]), sb("at_end", [P, 1])
    m.edge_w = sb("edge_w", [P, EDIM])
    m.w_vqk, m.b_vqk = sb("w_vqk", [P, 3 * D]), sb("b_vqk", [P, 3 * D])
    m.b_edge = sb("b_edge", [P, H0])
    m.w_o, m.w_f1, m.w_f2 = sb("w_o", [P, D]), sb("w_f1", [P, FFN]), sb("w_f2", [P, FFN // P, D])
    m.w_g1, m.w_g2, m.w_rel = sb("w_g1", [P, D]), sb("w_g2", [P, D]), sb("w_rel", [P, NREL + 1, D])
    m.b_o, m.g_ln1, m.b_ln1, m.b_f2 = sb("b_o", [P, D]), sb("g_ln1", [P, D]), sb("b_ln1", [P, D]), sb("b_f2", [P, D])
    m.g_ln2, m.b_ln2, m.b_g1, m.b_g2 = sb("g_ln2", [P, D]), sb("b_ln2", [P, D]), sb("b_g1", [P, D]), sb("b_g2", [P, D])
    m.b_rel, m.a_src1, m.a_dst1 = sb("b_rel", [P, D]), sb("a_src1", [P, D]), sb("a_dst1", [P, D])
    m.a_src2, m.a_dst2 = sb("a_src2", [P, D]), sb("a_dst2", [P, D])
    m.b_f1, m.g_lnf, m.b_lnf = sb("b_f1", [P, FFN]), sb("g_lnf", [P, FFN]), sb("b_lnf", [P, FFN])
    m.X = sb("X", [P, NT, D])
    m.own = sb("own", [P, NT, D])
    m.acc = sb("acc", [P, NT, D + H0])
    m.R = sb("R", [P, NCH, RECW])
    m.top = sb("top", [P, NT, 2 * H0])
    m.cnt = sb("cnt_rel", [P, NT, NREL])
    m.dinv = sb("dinv", [P, NT])
    m.a_s, m.a_d = sb("a_s", [P, NT, 4]), sb("a_d", [P, NT, 4])
    m.tile_edges = sb("tile_edges", [EP, TILES])
    m.dst_slot, m.etype, m.rel_w = sb("dst_slot", [P, PADC]), sb("etype", [P, PADC]), sb("rel_w", [P, PADC])
    m.src_idx, m.rel_idx = sb("src_idx", [P, PADC], I32), sb("rel_idx", [P, PADC], I32)
    m.is_last = sb("is_last", [P, NCH])
    m.chunk_tile = sb("chunk_tile", [1, PADC], I32)
    m.node_ramp_i, m.node_ramp = sb("node_ramp_i", [P, P], I32), sb("node_ramp", [P, P])
    m.minus_half = sb("minus_half", [P, NT])
    m.tmp = sb("tmp", [P, D])
    m.loop_off = sb("loop_off", [P, NT])
    m.ps_t = ctx.enter_context(nc.psum_tensor("ps_t", [P, 2, 512], F32))
    m.ps_k = ctx.enter_context(nc.psum_tensor("ps_k", [P, 2, 512], F32))
    m.ps_o = ctx.enter_context(nc.psum_tensor("ps_o", [P, 2, 2, 512], F32))
    m.scratch = m.acc[:, :, :].rearrange("p t w -> p (t w)")
    m.table_vq = nc.dram_tensor("table_vq", (NP, 2 * D), F32).ap()
    m.table_h = nc.dram_tensor("table_h", (NP, D), F32).ap()
    m.table_g = nc.dram_tensor("table_g", (NP, D + 4), F32).ap()
    m.table_r = nc.dram_tensor("table_r", (NP * NREL, D), F32).ap()
    m.rows_dram = nc.dram_tensor("rows_dram", (P, NCH, D), F32).ap()
    m.rec_dram = nc.dram_tensor("rec_dram", (E + P, RECW), F32).ap()
    return m


def project(nc, sem, m, tag, prepare, weight, width, finish, table=None, table_width=0):
    s_in, s_tr, s_trc = sem(tag + "_staged"), sem(tag + "_turned"), sem(tag + "_turned_copied")
    s_mm, s_out = sem(tag + "_product"), sem(tag + "_out")
    s_store = [sem(f"{tag}_stored{k}") for k in range(2)]
    banks = -(-width // 512)
    step = width // banks
    with ExitStack() as ctx:
        staged = ctx.enter_context(nc.sbuf_tensor(tag + "_in", [P, 2, D], F32))
        rows_t = ctx.enter_context(nc.sbuf_tensor(tag + "_t", [P, 2, D], F32))
        out = ctx.enter_context(nc.sbuf_tensor(tag + "_o", [P, 2, width], F32))
        with nc.Block() as block:
            @block.vector
            def _(dve):
                def stage(t, k):
                    after(dve, s_tr, t - 1)
                    prepare(dve, staged[:, k, :], t)
                    dve.drain().then_inc(s_in, 1)

                def end(t, k, i):
                    if table is not None:
                        after(dve, s_store[k], i * 16)
                    dve.wait_ge(s_mm, t + 1)
                    finish(dve, out[:, k, :], m.ps_o[:, k, 0:banks, 0:step], t)
                    dve.drain().then_inc(s_out, 1)

                stage(0, 0)
                stage(1, 1)
                end(0, 0, 0)
                stage(2, 0)
                end(1, 1, 0)
                with dve.Fori(1, NT // 2 - 1) as i:
                    stage(i * 2 + 1, 1)
                    end(i * 2, 0, i)
                    stage(i * 2 + 2, 0)
                    end(i * 2 + 1, 1, i)
                stage(NT - 1, 1)
                end(NT - 2, 0, NT // 2 - 1)
                end(NT - 1, 1, NT // 2 - 1)

            @block.tensor
            def _(pe):
                def body(t, k, i):
                    pe.wait_ge(s_in, t + 1)
                    pe.transpose(m.ps_t[:, k, 0:P], staged[:, k, :], m.ident[:, :]).then_inc(s_tr, 1)
                    pe.wait_ge(s_trc, t + 1)
                    after(pe, s_out, t - 1)
                    for b in range(banks):
                        last = pe.matmul(m.ps_o[:, k, b, 0:step], rows_t[:, k, :],
                                         weight[:, b * step:(b + 1) * step], start=True, stop=True)
                    last.then_inc(s_mm, 1)
                in_pairs(pe, NT, body)

            @block.scalar
            def _(act):
                def body(t, k, i):
                    act.wait_ge(s_tr, t + 1)
                    after(act, s_mm, t - 1)
                    act.copy(rows_t[:, k, :], m.ps_t[:, k, 0:P]).then_inc(s_trc, 1)
                in_pairs(act, NT, body)

            if table is not None:
                @block.sync
                def _(sp):
                    def body(t, k, i):
                        sp.wait_ge(s_out, t + 1)
                        sp.dma_start(table[bass.ds(t * P, P), :], out[:, k, 0:table_width]).then_inc(s_store[k], 16)
                    in_pairs(sp, NT, body)
                    for k in range(2):
                        sp.wait_ge(s_store[k], 16 * (NT // 2))


def layer_norm(nc, sem, m, tag, rows, gain=None, shift=None, add=None):
    s_var, s_rstd = sem(tag + "_variance"), sem(tag + "_rstd")
    with ExitStack() as ctx:
        def sb(name, shape):
            return ctx.enter_context(nc.sbuf_tensor(tag + name, shape, F32))

        stats = sb("_stats", [P, NT, 6])
        mean, var, rstd, diff = (sb(n, [P, NT]) for n in ("_mean", "_var", "_rstd", "_diff"))
        with nc.Block() as block:
            @block.vector
            def _(dve):
                if add is not None:
                    dve.tensor_tensor(rows, rows, add, ALU.add)
                    dve.drain()
                with dve.Fori(0, NT // 2) as i:
                    for k in range(2):
                        dve.bn_stats(stats[:, bass.ds(i * 2 + k, 1), :], rows[:, bass.ds(i * 2 + k, 1), :])
                dve.drain()
                dve.tensor_tensor(mean[:, :], stats[:, :, 1], stats[:, :, 4], ALU.add)
                dve.tensor_tensor(diff[:, :], stats[:, :, 1], stats[:, :, 4], ALU.subtract)
                dve.tensor_tensor(var[:, :], stats[:, :, 2], stats[:, :, 5], ALU.add)
                dve.drain()
                dve.tensor_scalar(mean[:, :], mean[:, :], 0.5, None, ALU.mult)
                dve.tensor_tensor(diff[:, :], diff[:, :], diff[:, :], ALU.mult)
                dve.tensor_scalar(var[:, :], var[:, :], 1.0 / D, None, ALU.mult)
                dve.drain()
                dve.scalar_tensor_tensor(var[:, :], diff[:, :], 0.25, var[:, :], ALU.mult, ALU.add)
                dve.drain()
                dve.tensor_scalar(var[:, :], var[:, :], EPS, None, ALU.add).then_inc(s_var, 1)
                dve.wait_ge(s_rstd, 1)
                with dve.Fori(0, NT // 2) as i:
                    for k in range(2):
                        t = bass.ds(i * 2 + k, 1)
                        dve.tensor_scalar(rows[:, t, :], rows[:, t, :], mean[:, t], rstd[:, t], ALU.subtract, ALU.mult)
                    if gain is not None:
                        two = bass.ds(i * 2, 2)
                        dve.drain()
                        dve.tensor_tensor(rows[:, two, :], rows[:, two, :], gain.unsqueeze(1).broadcast_to([P, 2, D]), ALU.mult)
                        dve.drain()
                        dve.tensor_tensor(rows[:, two, :], rows[:, two, :], shift.unsqueeze(1).broadcast_to([P, 2, D]), ALU.add)

            @block.gpsimd
            def _(pool):
                pool.wait_ge(s_var, 1)
                pool.tensor_tensor(rstd[:, :], var[:, :], m.minus_half[:, 0:var.shape[1]], ALU.pow).then_inc(s_rstd, 1)


def score_pass(nc, sem, m, tag, table, width, heads, dot):
    s_idx, s_oh = sem(tag + "_indices"), sem(tag + "_one_hot")
    s_gather, base = m.s_gather, m.gathered
    s_spill = [sem(f"{tag}_spilled{k}") for k in range(2)]
    s_tr, s_trc, s_ex = sem(tag + "_turned"), sem(tag + "_turned_copied"), sem(tag + "_spread")
    s_cnt, s_used = sem(tag + "_counted"), sem(tag + "_used")
    own = heads if not dot else D
    with ExitStack() as ctx:
        def sb(name, shape, dt=F32):
            return ctx.enter_context(nc.sbuf_tensor(tag + name, shape, dt))

        idx = sb("_idx", [P, 2, U], I32)
        got = sb("_got", [P, 2, U, width])
        hot, hot_t = sb("_hot", [P, 2, U, P]), sb("_hot_t", [P, 2, U, P])
        kind = sb("_kind", [P, 2, U, NREL])
        dots = sb("_dots", [P, 2, U, heads])
        with nc.Block() as block:
            @block.gpsimd
            def _(pool):
                def body(j, k, i):
                    apart(pool, s_idx, j + 1)
                    apart(pool, s_used, j - 1)
                    apart(pool, s_spill[k], i * 16)
                    for u in range(U):
                        pool.indirect_dma_start(got[:, k, u, :], None, table, bass.IndirectOffsetOnAxis(
                            ap=idx[:, k, u:u + 1], axis=0)).then_inc(s_gather[k], 16)
                in_pairs(pool, NG, body)

            @block.sync
            def _(sp):
                def body(j, k, i):
                    sp.wait_ge(s_gather[k], i * (16 * U) + (base + 16 * U))
                    sp.dma_start(m.rows_dram[:, cols(j), :], got[:, k, :, 0:D]).then_inc(s_spill[k], 16)
                in_pairs(sp, NG, body)
                for k in range(2):
                    sp.wait_ge(s_spill[k], 16 * (NG // 2))

            @block.tensor
            def _(pe):
                def body(j, k, i):
                    pe.wait_ge(s_oh, j + 1)
                    for u in range(U):
                        last = pe.transpose(m.ps_t[:, k, u * P:(u + 1) * P], hot[:, k, u, :], m.ident[:, :])
                    last.then_inc(s_tr, 1)
                    after(pe, s_used, j - 1)
                    if dot:
                        for u in range(U):
                            last = pe.matmul(m.ps_o[:, k, 0, u * NREL:(u + 1) * NREL], hot[:, k, u, :],
                                             kind[:, k, u, :], start=True, stop=True)
                        last.then_inc(s_cnt, 1)
                    tiles = tiles_of_chunks(nc, m, ENG.PE, j)
                    pe.wait_ge(s_trc, j + 1)
                    for u in range(U):
                        rows = (m.own if dot else m.a_d)[:, bass.ds(tiles[u], 1), 0:own]
                        last = pe.matmul(m.ps_k[:, k, u * own:(u + 1) * own], hot_t[:, k, u, :], rows,
                                         start=True, stop=True)
                    last.then_inc(s_ex, 1)
                in_pairs(pe, NG, body)

            @block.scalar
            def _(act):
                def body(j, k, i):
                    act.wait_ge(s_tr, j + 1)
                    after(act, s_ex, j - 1)
                    act.copy(hot_t[:, k, :, :], m.ps_t[:, k, :].rearrange("p (u e) -> p u e", u=U)).then_inc(s_trc, 1)
                in_pairs(act, NG, body)

            @block.vector
            def _(dve):
                def stage(j, k):
                    after(dve, s_ex, j - 1)
                    if dot:
                        after(dve, s_cnt, j - 1)
                        dve.tensor_tensor(kind[:, k, :, :], m.node_ramp[:, 0:NREL].unsqueeze(1).broadcast_to([P, U, NREL]),
                                          m.etype[:, cols(j)].unsqueeze(2).broadcast_to([P, U, NREL]), ALU.is_equal)
                    dve.tensor_copy(idx[:, k, :], m.src_idx[:, cols(j)]).then_inc(s_idx, 1)
                    dve.tensor_tensor(hot[:, k, :, :], m.node_ramp[:, :].unsqueeze(1).broadcast_to([P, U, P]),
                                      m.dst_slot[:, cols(j)].unsqueeze(2).broadcast_to([P, U, P]),
                                      ALU.is_equal).then_inc(s_oh, 1)

                def score(j, k, i):
                    if dot:
                        tiles = tiles_of_chunks(nc, m, ENG.DVE, j)
                    dve.wait_ge(s_ex, j + 1)
                    dve.wait_ge(s_gather[k], i * (16 * U) + (base + 16 * U))
                    at = m.R[:, cols(j), R_BIAS:R_BIAS + heads]
                    if not dot:
                        dve.tensor_tensor(dots[:, k, :, :], got[:, k, :, D:D + heads],
                                          m.ps_k[:, k, 0:U * own].rearrange("p (u h) -> p u h", u=U), ALU.add)
                        dve.drain()
                        dve.scalar_tensor_tensor(at, dots[:, k, :, :], 0.2, dots[:, k, :, :], ALU.mult, ALU.max)
                        dve.drain().then_inc(s_used, 1)
                        return
                    q = got[:, k, :, D:2 * D]
                    dve.tensor_tensor(q, q, m.ps_k[:, k, :].rearrange("p (u d) -> p u d", u=U), ALU.mult)
                    dve.wait_ge(s_cnt, j + 1)
                    for u in range(U):
                        c = m.cnt[:, bass.ds(tiles[u], 1), :]
                        dve.tensor_tensor(c, c, m.ps_o[:, k, 0, u * NREL:(u + 1) * NREL].unsqueeze(1), ALU.add)
                        dve.drain()
                    for u in range(U):
                        dve.tensor_reduce(dots[:, k, u, :], got[:, k, u, D:2 * D].rearrange("p (h c) -> p h c", h=heads),
                                          AX, ALU.add)
                    dve.drain()
                    dve.scalar_tensor_tensor(at, dots[:, k, :, :], float(D // heads) ** -0.5, at, ALU.mult, ALU.add)
                    dve.drain().then_inc(s_used, 1)

                def body(j, k, i):
                    stage(j + 1, 1 - k)
                    score(j, k, i)
                if dot:
                    dve.memset(m.cnt[:, :, :], 0.0)
                stage(0, 0)
                in_pairs(dve, NG, body)
    m.gathered += 16 * U * (NG // 2)


def score_maximum(nc, sem, m, tag, heads):
    G = min(P // heads, 64)
    rows, quads, steps = G * heads, G // U, NCH // G
    s_st, s_tr, s_run, s_bk = sem(tag + "_staged"), sem(tag + "_turned"), sem(tag + "_run"), sem(tag + "_back")
    s_fl, s_oh, s_mm = sem(tag + "_flagged"), sem(tag + "_one_hot"), sem(tag + "_sent")
    assert steps * G == NCH and steps % 2 == 0 or heads == 1
    with ExitStack() as ctx:
        def sb(name, shape):
            return ctx.enter_context(nc.sbuf_tensor(tag + name, shape, F32))

        value, last = sb("_value", [P, G, heads]), sb("_last", [P, G, heads])
        cut, run = sb("_cut", [rows, P]), sb("_run", [rows, P])
        sent, present = sb("_sent", [P, G, heads + 1]), sb("_present", [P, G])
        found = sb("_found", [P, G, heads])
        hot = sb("_hot", [P, 2, U, P])
        w = heads + 1
        with nc.Block() as block:
            @block.vector
            def _(dve):
                dve.memset(cut[:, :], 0.0)
                dve.drain()
                with dve.Fori(0, steps) as g:
                    here = bass.ds(g * G, G)
                    flags = m.is_last[:, here].unsqueeze(2).broadcast_to([P, G, heads])
                    dve.tensor_copy(value[:, :, :], m.R[:, here, R_BIAS:R_BIAS + heads])
                    dve.tensor_copy(last[:, :, :], flags)
                    dve.drain().then_inc(s_st, 1)
                    dve.wait_ge(s_tr, g + 1)
                    dve.tensor_scalar(cut[:, 1:P], m.ps_t[0:rows, 1, 0:P - 1], -BIG, None, ALU.mult)
                    dve.drain()
                    dve.tensor_tensor_scan(run[:, :], cut[:, :], m.ps_t[0:rows, 0, 0:P], -BIG, ALU.add, ALU.max)
                    dve.drain().then_inc(s_run, 1)
                    dve.wait_ge(s_bk, g + 1)
                    dve.tensor_tensor(sent[:, :, 0:heads], m.ps_k[:, 0, 0:rows].rearrange("p (g h) -> p g h", g=G),
                                      last[:, :, :], ALU.mult)
                    dve.tensor_copy(sent[:, :, heads], m.is_last[:, here])
                    dve.drain().then_inc(s_fl, 1)
                    for q in range(quads):
                        if q >= 2:
                            dve.wait_ge(s_mm, g * quads + (q - 1))
                        dve.tensor_tensor(hot[:, q % 2, :, :], m.node_ramp[:, :].unsqueeze(1).broadcast_to([P, U, P]),
                                          m.dst_slot[:, bass.ds(g * G + q * U, U)].unsqueeze(2).broadcast_to([P, U, P]),
                                          ALU.is_equal).then_inc(s_oh, 1)
                    dve.wait_ge(s_mm, g * quads + quads)
                    res = m.ps_o[:, 0, 0, 0:G * w].rearrange("p (g w) -> p g w", g=G)
                    dve.tensor_scalar(present[:, :], res[:, :, heads], BIG, -BIG, ALU.mult, ALU.add)
                    dve.drain()
                    dve.tensor_tensor(found[:, :, :], res[:, :, 0:heads],
                                      present[:, :].unsqueeze(2).broadcast_to([P, G, heads]), ALU.add)
                    for q in range(quads):
                        _, tiles = nc.values_load_multi_w_load_instructions(
                            m.chunk_tile[0:1, bass.ds(g * G + q * U, U)], engines=[ENG.DVE], min_val=0,
                            max_val=TILES - 1)
                        for u in range(U):
                            top = m.top[:, bass.ds(tiles[u], 1), 0:heads]
                            dve.drain()
                            dve.tensor_tensor(top, top, found[:, q * U + u, :].unsqueeze(1), ALU.max)
                    dve.drain()

            @block.tensor
            def _(pe):
                with pe.Fori(0, steps) as g:
                    apart(pe, s_st, g + 1)
                    pe.transpose(m.ps_t[0:rows, 0, 0:P], value[:, :, :].rearrange("p g h -> p (g h)"), m.ident[:, :])
                    pe.transpose(m.ps_t[0:rows, 1, 0:P], last[:, :, :].rearrange("p g h -> p (g h)"), m.ident[:, :]
                                 ).then_inc(s_tr, 1)
                    apart(pe, s_run, g + 1)
                    pe.transpose(m.ps_k[:, 0, 0:rows], run[:, :], m.ident[0:rows, 0:rows]).then_inc(s_bk, 1)
                    apart(pe, s_fl, g + 1)
                    for q in range(quads):
                        pe.wait_ge(s_oh, g * quads + (q + 1))
                        for u in range(U):
                            c = q * U + u
                            mm = pe.matmul(m.ps_o[:, 0, 0, c * w:(c + 1) * w], hot[:, q % 2, u, :], sent[:, c, :],
                                           start=True, stop=True)
                        mm.then_inc(s_mm, 1)


def value_pass(nc, sem, m, tag, heads, relations):
    s_oh, s_rows = sem(tag + "_one_hot"), [sem(f"{tag}_rows{k}") for k in range(2)]
    s_tr, s_trc, s_ex = sem(tag + "_turned"), sem(tag + "_turned_copied"), sem(tag + "_spread")
    s_d, s_p, s_wr = sem(tag + "_differences"), sem(tag + "_weights"), sem(tag + "_weighted")
    s_sum, s_acc = sem(tag + "_summed"), sem(tag + "_added")
    W = D + heads
    span = 2 * H0 if relations else heads
    with ExitStack() as ctx:
        def sb(name, shape):
            return ctx.enter_context(nc.sbuf_tensor(tag + name, shape, F32))

        hot, hot_t = sb("_hot", [P, 2, U, P]), sb("_hot_t", [P, 2, U, P])
        kind = sb("_kind", [P, 2, U, NREL])
        diff = sb("_diff", [P, 2, U, heads])
        rows = sb("_rows", [P, 2, U, D])
        weighted = sb("_weighted", [P, 2, U, W])
        with nc.Block() as block:
            @block.sync
            def _(sp):
                def body(j, k, i):
                    after(sp, s_wr, j - 1)
                    sp.dma_start(rows[:, k, :, :], m.rows_dram[:, cols(j), :]).then_inc(s_rows[k], 16)
                in_pairs(sp, NG, body)

            @block.tensor
            def _(pe):
                def total(j, k):
                    pe.wait_ge(s_wr, j + 1)
                    after(pe, s_acc, j - 1)
                    for u in range(U):
                        last = pe.matmul(m.ps_o[:, k, u // 2, (u % 2) * W:(u % 2 + 1) * W], hot[:, k, u, :],
                                         weighted[:, k, u, :], start=True, stop=True)
                    last.then_inc(s_sum, 1)

                def body(j, k, i):
                    pe.wait_ge(s_oh, j + 1)
                    for u in range(U):
                        last = pe.transpose(m.ps_t[:, k, u * P:(u + 1) * P], hot[:, k, u, :], m.ident[:, :])
                    last.then_inc(s_tr, 1)
                    tiles = tiles_of_chunks(nc, m, ENG.PE, j)
                    pe.wait_ge(s_trc, j + 1)
                    after(pe, s_d, j - 1)
                    for u in range(U):
                        last = pe.matmul(m.ps_k[:, k, u * span:(u + 1) * span], hot_t[:, k, u, :],
                                         m.top[:, bass.ds(tiles[u], 1), 0:span], start=True, stop=True)
                    last.then_inc(s_ex, 1)
                    if not (isinstance(j, int) and j == 0):
                        total(j - 1, 1 - k)
                in_pairs(pe, NG, body)
                total(NG - 1, 1)

            @block.scalar
            def _(act):
                def body(j, k, i):
                    act.wait_ge(s_tr, j + 1)
                    after(act, s_ex, j - 1)
                    act.copy(hot_t[:, k, :, :], m.ps_t[:, k, :].rearrange("p (u e) -> p u e", u=U)).then_inc(s_trc, 1)
                    after(act, s_sum, j - 1)
                    act.wait_ge(s_d, j + 1)
                    act.activation(weighted[:, k, :, D:W], diff[:, k, :, :], ACT.Exp).then_inc(s_p, 1)
                in_pairs(act, NG, body)

            @block.vector
            def _(dve):
                def stage(j, k):
                    after(dve, s_sum, j - 1)
                    if relations:
                        dve.tensor_tensor(kind[:, k, :, :], m.node_ramp[:, 0:NREL].unsqueeze(1).broadcast_to([P, U, NREL]),
                                          m.etype[:, cols(j)].unsqueeze(2).broadcast_to([P, U, NREL]), ALU.is_equal)
                    dve.tensor_tensor(hot[:, k, :, :], m.node_ramp[:, :].unsqueeze(1).broadcast_to([P, U, P]),
                                      m.dst_slot[:, cols(j)].unsqueeze(2).broadcast_to([P, U, P]),
                                      ALU.is_equal).then_inc(s_oh, 1)

                def differences(j, k):
                    dve.wait_ge(s_ex, j + 1)
                    after(dve, s_p, j - 1)
                    spread = m.ps_k[:, k, 0:U * span].rearrange("p (u h) -> p u h", u=U)
                    dve.tensor_tensor(diff[:, k, :, :], m.R[:, cols(j), R_BIAS:R_BIAS + heads], spread[:, :, 0:heads],
                                      ALU.subtract)
                    if relations:
                        dve.tensor_tensor(kind[:, k, :, :], kind[:, k, :, :], spread[:, :, H0:2 * H0], ALU.mult)
                    dve.drain().then_inc(s_d, 1)
                    if relations:
                        dve.tensor_reduce(m.rel_w[:, cols(j)], kind[:, k, :, :], AX, ALU.add)

                def weigh(j, k, i):
                    dve.wait_ge(s_rows[k], i * 16 + 16)
                    dve.wait_ge(s_p, j + 1)
                    c = D // heads
                    for u in range(U):
                        dve.tensor_tensor(weighted[:, k, u, 0:D].rearrange("p (h c) -> p h c", h=heads),
                                          rows[:, k, u, :].rearrange("p (h c) -> p h c", h=heads),
                                          weighted[:, k, u, D:W].unsqueeze(2).broadcast_to([P, heads, c]), ALU.mult)
                    dve.drain().then_inc(s_wr, 1)

                def add(j, k):
                    tiles = tiles_of_chunks(nc, m, ENG.DVE, j)
                    dve.wait_ge(s_sum, j + 1)
                    for u in range(U):
                        a = m.acc[:, bass.ds(tiles[u], 1), 0:W]
                        dve.tensor_tensor(a, a, m.ps_o[:, k, u // 2, (u % 2) * W:(u % 2 + 1) * W].unsqueeze(1), ALU.add)
                        dve.drain()
                    dve.sem_inc(s_acc, 1)

                def body(j, k, i):
                    differences(j, k)
                    if not (isinstance(j, int) and j == 0):
                        add(j - 1, 1 - k)
                    stage(j + 1, 1 - k)
                    weigh(j, k, i)
                stage(0, 0)
                in_pairs(dve, NG, body)
                add(NG - 1, 1)


def sum_pass(nc, sem, m, tag, table, indices, edge_weight=None):
    s_idx, s_oh, s_sum, s_acc = (sem(tag + n) for n in ("_indices", "_one_hot", "_summed", "_added"))
    s_gather, base = m.s_gather, m.gathered
    with ExitStack() as ctx:
        def sb(name, shape, dt=F32):
            return ctx.enter_context(nc.sbuf_tensor(tag + name, shape, dt))

        idx, got, hot = sb("_idx", [P, 2, U], I32), sb("_got", [P, 2, U, D]), sb("_hot", [P, 2, U, P])
        with nc.Block() as block:
            @block.gpsimd
            def _(pool):
                def body(j, k, i):
                    apart(pool, s_idx, j + 1)
                    for u in range(U):
                        pool.indirect_dma_start(got[:, k, u, :], None, table, bass.IndirectOffsetOnAxis(
                            ap=idx[:, k, u:u + 1], axis=0)).then_inc(s_gather[k], 16)
                in_pairs(pool, NG, body)

            @block.tensor
            def _(pe):
                def body(j, k, i):
                    pe.wait_ge(s_oh, j + 1)
                    after(pe, s_acc, j - 1)
                    pe.wait_ge(s_gather[k], i * (16 * U) + (base + 16 * U))
                    for u in range(U):
                        last = pe.matmul(m.ps_o[:, k, 0, u * D:(u + 1) * D], hot[:, k, u, :], got[:, k, u, :],
                                         start=True, stop=True)
                    last.then_inc(s_sum, 1)
                in_pairs(pe, NG, body)

            @block.vector
            def _(dve):
                def stage(j, k):
                    after(dve, s_sum, j - 1)
                    dve.tensor_copy(idx[:, k, :], indices[:, cols(j)]).then_inc(s_idx, 1)
                    to = hot[:, k, :, :]
                    ins = dve.tensor_tensor(to, m.node_ramp[:, :].unsqueeze(1).broadcast_to([P, U, P]),
                                            m.dst_slot[:, cols(j)].unsqueeze(2).broadcast_to([P, U, P]), ALU.is_equal)
                    if edge_weight is not None:
                        dve.drain()
                        ins = dve.tensor_tensor(to, to, edge_weight[:, cols(j)].unsqueeze(2).broadcast_to([P, U, P]),
                                                ALU.mult)
                    ins.then_inc(s_oh, 1)

                def add(j, k, i):
                    tiles = tiles_of_chunks(nc, m, ENG.DVE, j)
                    dve.wait_ge(s_sum, j + 1)
                    for u in range(U):
                        a = m.acc[:, bass.ds(tiles[u], 1), 0:D]
                        dve.tensor_tensor(a, a, m.ps_o[:, k, 0, u * D:(u + 1) * D].unsqueeze(1), ALU.add)
                        dve.drain()
                    dve.sem_inc(s_acc, 1)

                def body(j, k, i):
                    if not (isinstance(j, int) and j == 0):
                        add(j - 1, 1 - k, i)
                    stage(j + 1, 1 - k)
                stage(0, 0)
                in_pairs(dve, NG, body)
                add(NG - 1, 1, 0)
    m.gathered += 16 * U * (NG // 2)


def store_rows(nc, sem, m, tag, rows, dram):
    s = sem(tag + "_stored")
    with nc.Block() as block:
        @block.sync
        def _(sp):
            sp.dma_start(dram.rearrange("(t p) d -> p t d", p=P), rows).then_inc(s, 16)
            sp.wait_ge(s, 16)


def feed_forward(nc, sem, m, rows, out):
    B = 5
    s_in, s_tr, s_trc, s_h = sem("ff_staged"), sem("ff_turned"), sem("ff_turned_copied"), sem("ff_hidden")
    s_var, s_rstd, s_n, s_g = sem("ff_variance"), sem("ff_rstd"), sem("ff_normed"), sem("ff_gelu")
    s_gt, s_gtc, s_y, s_out = sem("ff_gelu_turned"), sem("ff_gelu_copied"), sem("ff_product"), sem("ff_out")
    C = FFN // P
    banks = [m.ps_o[:, 0, 0, :], m.ps_o[:, 0, 1, :], m.ps_o[:, 1, 0, :], m.ps_o[:, 1, 1, :], m.ps_k[:, 0, :]]
    with ExitStack() as ctx:
        def sb(name, shape):
            return ctx.enter_context(nc.sbuf_tensor("ff_" + name, shape, F32))

        x = sb("x", [P, B, D])
        hid = m.scratch[:, 0:B * FFN].rearrange("p (b f) -> p b f", b=B)
        hid_t = m.scratch[:, B * FFN:2 * B * FFN].rearrange("p (b c n) -> p b c n", b=B, c=C)
        x_t = sb("x_t", [P, B, P])
        stats, mean, var, rstd, diff = sb("stats", [P, B, 6]), *(sb(n, [P, B]) for n in ("mean", "var", "rstd", "diff"))
        with nc.Block() as block:
            @block.vector
            def _(dve):
                with dve.Fori(0, NT // B) as i:
                    dve.tensor_copy(x[:, :, :], rows[:, bass.ds(i * B, B), :])
                    dve.drain().then_inc(s_in, 1)
                    for b in range(B):
                        dve.wait_ge(s_h, i * B + (b + 1))
                        dve.tensor_tensor(hid[:, b, :], banks[b], m.b_f1[:, :], ALU.add)
                    dve.drain()
                    for b in range(B):
                        dve.bn_stats(stats[:, b, :], hid[:, b, :])
                    dve.drain()
                    dve.tensor_tensor(mean[:, :], stats[:, :, 1], stats[:, :, 4], ALU.add)
                    dve.tensor_tensor(diff[:, :], stats[:, :, 1], stats[:, :, 4], ALU.subtract)
                    dve.tensor_tensor(var[:, :], stats[:, :, 2], stats[:, :, 5], ALU.add)
                    dve.drain()
                    dve.tensor_scalar(mean[:, :], mean[:, :], 0.5, None, ALU.mult)
                    dve.tensor_tensor(diff[:, :], diff[:, :], diff[:, :], ALU.mult)
                    dve.tensor_scalar(var[:, :], var[:, :], 1.0 / FFN, None, ALU.mult)
                    dve.drain()
                    dve.scalar_tensor_tensor(var[:, :], diff[:, :], 0.25, var[:, :], ALU.mult, ALU.add)
                    dve.drain()
                    dve.tensor_scalar(var[:, :], var[:, :], EPS, None, ALU.add).then_inc(s_var, 1)
                    dve.wait_ge(s_rstd, i + 1)
                    for b in range(B):
                        dve.tensor_scalar(hid[:, b, :], hid[:, b, :], mean[:, b:b + 1], rstd[:, b:b + 1],
                                          ALU.subtract, ALU.mult)
                    dve.drain()
                    dve.tensor_tensor(hid, hid, m.g_lnf[:, :].unsqueeze(1).broadcast_to([P, B, FFN]), ALU.mult)
                    dve.drain()
                    dve.tensor_tensor(hid, hid, m.b_lnf[:, :].unsqueeze(1).broadcast_to([P, B, FFN]), ALU.add
                                      ).then_inc(s_n, 1)
                    dve.tensor_tensor(x[:, :, :], x[:, :, :], m.b_f2[:, :].unsqueeze(1).broadcast_to([P, B, D]), ALU.add)
                    dve.drain()
                    dve.wait_ge(s_y, i + 1)
                    dve.tensor_tensor(out[:, bass.ds(i * B, 4), :], x[:, 0:4, :],
                                      m.ps_t[:, 0, :].rearrange("p (b d) -> p b d", b=4), ALU.add)
                    dve.tensor_tensor(out[:, bass.ds(i * B + 4, 1), :], x[:, 4:5, :], m.ps_t[:, 1, 0:D].unsqueeze(1), ALU.add)
                    dve.drain()

            @block.gpsimd
            def _(pool):
                with pool.Fori(0, NT // B) as i:
                    apart(pool, s_var, i + 1)
                    pool.tensor_tensor(rstd[:, :], var[:, :], m.minus_half[:, 0:var.shape[1]], ALU.pow).then_inc(s_rstd, 1)

            @block.tensor
            def _(pe):
                with pe.Fori(0, NT // B) as i:
                    pe.wait_ge(s_in, i + 1)
                    for b in range(B):
                        mm = pe.transpose(m.ps_t[:, b // 4, (b % 4) * P:(b % 4 + 1) * P], x[:, b, :], m.ident[:, :])
                    mm.then_inc(s_tr, 1)
                    pe.wait_ge(s_trc, i * 2 + 2)
                    for b in range(B):
                        pe.matmul(banks[b], x_t[:, b, :], m.w_f1[:, :], start=True, stop=True).then_inc(s_h, 1)
                    for b in range(B):
                        pe.wait_ge(s_g, i * B + (b + 1))
                        for c in range(C):
                            mm = pe.transpose(banks[b][:, c * P:(c + 1) * P], hid[:, b, c * P:(c + 1) * P], m.ident[:, :])
                        mm.then_inc(s_gt, 1)
                    for b in range(B):
                        pe.wait_ge(s_gtc, i * B + (b + 1))
                        for c in range(C):
                            mm = pe.matmul(m.ps_t[:, b // 4, (b % 4) * D:(b % 4 + 1) * D], hid_t[:, b, c, :],
                                           m.w_f2[:, c, :], start=(c == 0), stop=(c == C - 1))
                    mm.then_inc(s_y, 1)

            @block.scalar
            def _(act):
                with act.Fori(0, NT // B) as i:
                    act.wait_ge(s_tr, i + 1)
                    act.copy(x_t[:, 0:4, :], m.ps_t[:, 0, :].rearrange("p (b n) -> p b n", b=4)).then_inc(s_trc, 1)
                    act.copy(x_t[:, 4, :], m.ps_t[:, 1, 0:P]).then_inc(s_trc, 1)
                    act.wait_ge(s_n, i + 1)
                    for b in range(B):
                        act.activation(hid[:, b, :], hid[:, b, :], ACT.Gelu).then_inc(s_g, 1)
                    for b in range(B):
                        act.wait_ge(s_gt, i * B + (b + 1))
                        act.copy(hid_t[:, b, :, :], banks[b].rearrange("p (c n) -> p c n", c=C)).then_inc(s_gtc, 1)


def attention_layer(nc, sem, m):
    def prepare(dve, staged, t):
        dve.tensor_copy(staged.unsqueeze(1), m.X[:, bass.ds(t, 1), :])

    def finish(dve, out, product, t):
        dve.tensor_tensor(out.unsqueeze(1), product, m.b_vqk[:, :].unsqueeze(1), ALU.add)
        dve.drain()
        dve.tensor_copy(m.own[:, bass.ds(t, 1), :], out[:, 2 * D:3 * D].unsqueeze(1))

    project(nc, sem, m, "vqk", prepare, m.w_vqk[:, :], 3 * D, finish, m.table_vq, 2 * D)
    score_pass(nc, sem, m, "a0", m.table_vq, 2 * D, H0, True)

    s_deg = sem("degrees")
    with nc.Block() as block:
        @block.vector
        def _(dve):
            dve.memset(m.top[:, :, :], -BIG)
            dve.memset(m.acc[:, :, :], 0.0)
            dve.tensor_reduce(m.dinv[:, :], m.cnt[:, :, :], AX, ALU.add)
            dve.drain()
            dve.tensor_scalar(m.dinv[:, :], m.dinv[:, :], 1.0, None, ALU.add).then_inc(s_deg, 1)
            dve.tensor_scalar(m.cnt[:, :, :], m.cnt[:, :, :], 1.0, None, ALU.max)
            dve.drain()
            dve.reciprocal(m.top[:, :, H0:2 * H0], m.cnt[:, :, :])

        @block.gpsimd
        def _(pool):
            pool.wait_ge(s_deg, 1)
            pool.tensor_tensor(m.dinv[:, :], m.dinv[:, :], m.minus_half[:, :], ALU.pow)

    score_maximum(nc, sem, m, "m0", H0)
    value_pass(nc, sem, m, "v0", H0, True)

    with nc.Block() as block:
        @block.vector
        def _(dve):
            den = m.acc[:, :, D:D + H0]
            dve.tensor_scalar(den, den, 1e-8, None, ALU.max)
            dve.drain()
            dve.reciprocal(den, den)

    def normalised(dve, staged, t):
        dve.tensor_tensor(staged.rearrange("p (h c) -> p h c", h=H0),
                          m.acc[:, bass.ds(t, 1), 0:D].rearrange("p t (h c) -> p (t h) c", h=H0),
                          m.acc[:, bass.ds(t, 1), D:D + H0].rearrange("p t h -> p (t h)").unsqueeze(2)
                          .broadcast_to([P, H0, D // H0]), ALU.mult)

    def residual(dve, out, product, t):
        dve.tensor_tensor(out.unsqueeze(1), product, m.b_o[:, :].unsqueeze(1), ALU.add)
        dve.drain()
        dve.tensor_tensor(m.own[:, bass.ds(t, 1), :], out.unsqueeze(1), m.X[:, bass.ds(t, 1), :], ALU.add)

    project(nc, sem, m, "oproj", normalised, m.w_o[:, :], D, residual)
    layer_norm(nc, sem, m, "ln1", m.own[:, :, :], m.g_ln1[:, :], m.b_ln1[:, :])
    feed_forward(nc, sem, m, m.own, m.own)
    layer_norm(nc, sem, m, "ln2", m.own[:, :, :], m.g_ln2[:, :], m.b_ln2[:, :])
    layer_norm(nc, sem, m, "ln_l0", m.X[:, :, :], add=m.own[:, :, :])


def appnp_layer(nc, m):
    dinv = m.dinv[:, :].unsqueeze(2).broadcast_to([P, NT, D])
    h = m.acc[:, :, 0:D]
    with nc.Block() as block:
        @block.vector
        def _(dve):
            dve.tensor_tensor(m.own[:, :, :], m.X[:, :, :], dinv, ALU.mult)
            dve.memset(m.acc[:, :, :], 0.0)
    for hop in range(5):
        with semaphores(nc) as sem:
            store_rows(nc, sem, m, f"hop{hop}", m.own[:, :, :], m.table_h)
            sum_pass(nc, sem, m, f"p{hop}", m.table_h, m.src_idx)
        with nc.Block() as block:
            @block.vector
            def _(dve):
                dve.tensor_tensor(h, h, m.own[:, :, :], ALU.add)
                dve.drain()
                dve.tensor_tensor(h, h, dinv, ALU.mult)
                dve.drain()
                dve.tensor_scalar(h, h, 1.0 - 0.8, None, ALU.mult)
                dve.drain()
                dve.scalar_tensor_tensor(h, m.X[:, :, :], 0.8, h, ALU.mult, ALU.add)
                dve.drain()
                if hop < 4:
                    dve.tensor_tensor(m.own[:, :, :], h, dinv, ALU.mult)
                    dve.drain()
                    dve.memset(h, 0.0)
    with semaphores(nc) as sem:
        layer_norm(nc, sem, m, "ln_l1", m.X[:, :, :], add=h)


def gat_conv(nc, sem, m, tag, prepare, weight, a_src, a_dst, heads):
    c = D // heads

    def finish(dve, out, product, t):
        dve.tensor_copy(out[:, 0:D].unsqueeze(1), product)
        dve.drain()
        dve.tensor_copy(m.own[:, bass.ds(t, 1), :], out[:, 0:D].unsqueeze(1))
        for a, to in ((a_src, m.a_s), (a_dst, m.a_d)):
            dve.tensor_tensor(m.tmp[:, :], out[:, 0:D], a[:, :], ALU.mult)
            dve.drain()
            dve.tensor_reduce(to[:, bass.ds(t, 1), 0:heads], m.tmp[:, :].rearrange("p (t h c) -> p t h c", t=1, h=heads),
                              AX, ALU.add)
            dve.drain()

    project(nc, sem, m, tag + "w", prepare, weight[:, :], D, finish)
    s_tab, s_exp, s_self = sem(tag + "_table"), sem(tag + "_self_exp"), sem(tag + "_self")
    with nc.Block() as block:
        @block.sync
        def _(sp):
            rows = m.table_g.rearrange("(t p) d -> p t d", p=P)
            sp.dma_start(rows[:, :, 0:D], m.own[:, :, :]).then_inc(s_tab, 16)
            sp.dma_start(rows[:, :, D:D + 4], m.a_s[:, :, :]).then_inc(s_tab, 16)
            sp.wait_ge(s_tab, 32)
    own_score = m.cnt[:, :, 0:heads]
    loop = m.has_loop[:, :].unsqueeze(2).broadcast_to([P, NT, heads])
    with nc.Block() as block:
        @block.vector
        def _(dve):
            top = m.top[:, :, 0:heads]
            dve.tensor_tensor(top, m.a_s[:, :, 0:heads], m.a_d[:, :, 0:heads], ALU.add)
            dve.drain()
            dve.scalar_tensor_tensor(own_score, top, 0.2, top, ALU.mult, ALU.max)
            dve.tensor_scalar(m.loop_off[:, :], m.has_loop[:, :], BIG, -BIG, ALU.mult, ALU.add)
            dve.drain()
            dve.tensor_tensor(top, own_score, loop, ALU.mult)
            dve.drain()
            dve.tensor_tensor(top, top, m.loop_off[:, :].unsqueeze(2).broadcast_to([P, NT, heads]), ALU.add)
    score_pass(nc, sem, m, tag + "s", m.table_g, D + 4, heads, False)
    score_maximum(nc, sem, m, tag + "m", heads)
    with nc.Block() as block:
        @block.vector
        def _(dve):
            den = m.acc[:, :, D:D + heads]
            dve.tensor_tensor(own_score, own_score, m.top[:, :, 0:heads], ALU.subtract)
            dve.drain()
            dve.tensor_scalar(own_score, own_score, 0.0, None, ALU.min)
            dve.drain().then_inc(s_self, 1)
            dve.wait_ge(s_exp, 1)
            dve.tensor_tensor(den, own_score, loop, ALU.mult)
            dve.drain()
            with dve.Fori(0, NT) as t:
                dve.tensor_tensor(m.acc[:, bass.ds(t, 1), 0:D].rearrange("p t (h c) -> p (t h) c", h=heads),
                                  m.own[:, bass.ds(t, 1), :].rearrange("p t (h c) -> p (t h) c", h=heads),
                                  m.acc[:, bass.ds(t, 1), D:D + heads].rearrange("p t h -> p (t h)").unsqueeze(2)
                                  .broadcast_to([P, heads, c]), ALU.mult)

        @block.scalar
        def _(act):
            act.wait_ge(s_self, 1)
            act.activation(own_score, own_score, ACT.Exp).then_inc(s_exp, 1)
    value_pass(nc, sem, m, tag + "v", heads, False)
    with nc.Block() as block:
        @block.vector
        def _(dve):
            den = m.acc[:, :, D:D + heads]
            dve.tensor_scalar(den, den, 1e-16, None, ALU.add)
            dve.drain()
            dve.reciprocal(den, den)


def gat_layer(nc, m):
    def prepare_x(dve, staged, t):
        dve.tensor_copy(staged.unsqueeze(1), m.X[:, bass.ds(t, 1), :])

    with semaphores(nc) as sem:
        gat_conv(nc, sem, m, "g1", prepare_x, m.w_g1, m.a_src1, m.a_dst1, 4)

    def finish_rows(heads, bias):
        def tile(dve, to, t):
            dve.tensor_tensor(to.rearrange("p (h c) -> p h c", h=heads),
                              m.acc[:, bass.ds(t, 1), 0:D].rearrange("p t (h c) -> p (t h) c", h=heads),
                              m.acc[:, bass.ds(t, 1), D:D + heads].rearrange("p t h -> p (t h)").unsqueeze(2)
                              .broadcast_to([P, heads, D // heads]), ALU.mult)
            dve.drain()
            dve.tensor_tensor(to, to, bias[:, :], ALU.add)
            dve.drain()
        return tile

    with semaphores(nc) as sem:
        s_m, s_e = sem("elu_min"), sem("elu_exp")
        first = finish_rows(4, m.b_g1)
        with nc.Block() as block:
            @block.vector
            def _(dve):
                with dve.Fori(0, NT) as t:
                    first(dve, m.tmp[:, :], t)
                    dve.tensor_copy(m.own[:, bass.ds(t, 1), :], m.tmp[:, :].unsqueeze(1))
                    dve.tensor_scalar(m.acc[:, bass.ds(t, 1), 0:D], m.tmp[:, :].unsqueeze(1), 0.0, None, ALU.min)
                    dve.drain()
                dve.drain().then_inc(s_m, 1)
                dve.wait_ge(s_e, 1)
                dve.scalar_tensor_tensor(m.own[:, :, :], m.acc[:, :, 0:D], -1.0, m.own[:, :, :], ALU.add, ALU.max)

            @block.scalar
            def _(act):
                act.wait_ge(s_m, 1)
                act.activation(m.acc[:, :, 0:D], m.acc[:, :, 0:D], ACT.Exp).then_inc(s_e, 1)

    def prepare_h(dve, staged, t):
        dve.tensor_copy(staged.unsqueeze(1), m.own[:, bass.ds(t, 1), :])

    with semaphores(nc) as sem:
        gat_conv(nc, sem, m, "g2", prepare_h, m.w_g2, m.a_src2, m.a_dst2, 1)
    second = finish_rows(1, m.b_g2)
    with nc.Block() as block:
        @block.vector
        def _(dve):
            with dve.Fori(0, NT) as t:
                second(dve, m.tmp[:, :], t)
                dve.tensor_tensor(m.X[:, bass.ds(t, 1), :], m.X[:, bass.ds(t, 1), :], m.tmp[:, :].unsqueeze(1), ALU.add)
                dve.drain()
    with semaphores(nc) as sem:
        layer_norm(nc, sem, m, "ln_l2", m.X[:, :, :])


def relational_layer(nc, sem, m):
    def prepare(dve, staged, t):
        dve.tensor_copy(staged.unsqueeze(1), m.X[:, bass.ds(t, 1), :])

    def per_relation(dve, out, product, t):
        dve.tensor_copy(out.rearrange("p (b n) -> p b n", b=2), product)

    def root(dve, out, product, t):
        dve.tensor_tensor(m.acc[:, bass.ds(t, 1), 0:D], product, m.b_rel[:, :].unsqueeze(1), ALU.add)

    project(nc, sem, m, "rel", prepare, m.w_rel[:, 0:NREL, :].rearrange("k r n -> k (r n)"), NREL * D, per_relation,
            m.table_r.rearrange("(n r) d -> n (r d)", r=NREL), NREL * D)
    project(nc, sem, m, "root", prepare, m.w_rel[:, NREL, :], D, root)
    sum_pass(nc, sem, m, "r", m.table_r, m.rel_idx, m.rel_w)
    layer_norm(nc, sem, m, "ln_l3", m.X[:, :, :], add=m.acc[:, :, 0:D])


def store_output(nc, sem, m, out):
    s_out = sem("output_stored")
    with nc.Block() as block:
        @block.sync
        def _(sp):
            sp.dma_start(out[0:FULL * P, :].rearrange("(t p) d -> p t d", p=P), m.X[:, 0:FULL, :]).then_inc(s_out, 16)
            sp.dma_start(out[FULL * P:N, :], m.X[0:TAIL, FULL, :]).then_inc(s_out, 16)
            sp.wait_ge(s_out, 32)


def build(nc, A, out, stages=4):
    with ExitStack() as ctx:
        m = allocate(nc, ctx)
        m.s_gather = [ctx.enter_context(nc.semaphore(f"gathered{k}")) for k in range(2)]
        m.gathered = 0
        with semaphores(nc) as sem:
            load_constants(nc, m, A, sem)
            build_records(nc, m, A, sem)
            plan_chunks(nc, m, A, sem)
        with semaphores(nc) as sem:
            attention_layer(nc, sem, m)
        if stages > 1:
            appnp_layer(nc, m)
        if stages > 2:
            gat_layer(nc, m)
        if stages > 3:
            with semaphores(nc) as sem:
                relational_layer(nc, sem, m)
        with semaphores(nc) as sem:
            store_output(nc, sem, m, out)


_INS = ['x', 'src', 'dst', 'edge_attr_32', 'edge_type_8', 'L0_gnn_qW', 'L0_gnn_qb', 'L0_gnn_kW', 'L0_gnn_kb',
        'L0_gnn_vW', 'L0_gnn_vb', 'L0_gnn_eW', 'L0_gnn_eb', 'L0_gnn_oW', 'L0_gnn_ob', 'L0_gnn_ln1_g',
        'L0_gnn_ln1_b', 'L0_gnn_f1W', 'L0_gnn_f1b', 'L0_gnn_lnf_g', 'L0_gnn_lnf_b', 'L0_gnn_f2W', 'L0_gnn_f2b',
        'L0_gnn_ln2_g', 'L0_gnn_ln2_b', 'L2_gnn_W1', 'L2_gnn_a_src1', 'L2_gnn_a_dst1', 'L2_gnn_b1', 'L2_gnn_W2',
        'L2_gnn_a_src2', 'L2_gnn_a_dst2', 'L2_gnn_b2', 'L3_gnn_weight', 'L3_gnn_root', 'L3_gnn_bias']
_OUTS = [((N, D), 'float32')]


def kernel(**inputs):
    import numpy as _np
    import concourse.bacc as _bacc
    from concourse import mybir as _mybir
    from concourse.bass_utils import run_bass_kernel_spmd as _run

    nc = _bacc.Bacc("TRN2", target_bir_lowering=False, num_devices=1)
    arrays, args = {}, {}
    for name in _INS:
        a = _np.ascontiguousarray(inputs[name])
        arrays[f"in_{name}_dram"] = a
        args[name] = nc.dram_tensor(f"in_{name}_dram", a.shape, _mybir.dt.from_np(a.dtype), kind="ExternalInput").ap()
    outs = []
    for i, (shape, dtype) in enumerate(_OUTS):
        dt = _mybir.dt.from_np(_np.dtype(dtype))
        outs.append(nc.dram_tensor(f"out_{i}_dram", shape, dt, kind="ExternalOutput").ap())
    build(nc, args, outs[0])
    r = _run(nc, [arrays], core_ids=[0])
    got = tuple(r.results[0][f"out_{i}_dram"] for i in range(len(_OUTS)))
    return got[0]
```

```python
from contextlib import ExitStack, contextmanager

import concourse.bass as bass
from concourse import mybir
from concourse.alu_op_type import AluOpType as ALU

ACT = mybir.ActivationFunctionType
AX = mybir.AxisListType.X
F32 = mybir.dt.float32
I32 = mybir.dt.int32
ENG = mybir.EngineType

P = 128
N, E, D, FFN, EDIM, NREL = 6250, 100000, 128, 512, 32, 8
H0 = 8
SELF_LOOPS = 3750
FULL, TAIL = N // P, N % P
TILES = FULL + 1
NT = TILES + TILES % 2
NP = NT * P
U = 4
NCH = -(-((E + TILES * (P - 1)) // P) // (2 * U)) * (2 * U)
NG = NCH // U
RING = 4
EP, EC = 125, E // 125
RECW = 12
R_SRC, R_DST, R_TYP, R_NEXT, R_BIAS = 0, 1, 2, 3, 4
ROUND = 16
BIG = 1.0e30
EPS = 1e-5


class Core:
    pass


def after(eng, sem, value):
    if isinstance(value, int) and value <= 0:
        return
    eng.wait_ge(sem, value)


def apart(eng, sem, value):
    if isinstance(value, int) and value <= 0:
        return
    eng.wait_ge(sem, value)
    eng.nop(nofuse=True)


def in_pairs(eng, n, body):
    body(0, 0, 0)
    body(1, 1, 0)
    with eng.Fori(1, n // 2) as i:
        body(i * 2, 0, i)
        body(i * 2 + 1, 1, i)


def in_rounds(eng, n, ring, body):
    for s in range(ring):
        body(s, s, 0)
    with eng.Fori(1, n // ring - 1) as i:
        for s in range(ring):
            body(i * ring + s, s, i)
    for s in range(ring):
        body(n - ring + s, s, n // ring - 1)


def within(step, n=NG):
    return not isinstance(step, int) or step < n


def began(step):
    return not isinstance(step, int) or step >= 0


def count_gathers(m):
    m.gathered = [g + 16 * U * (NG // RING) for g in m.gathered]


def one_hot(dve, m, to, chunks, n):
    return dve.tensor_tensor(to, m.node_ramp[:, :].unsqueeze(1).broadcast_to([P, n, P]),
                             m.dst_slot[:, chunks].unsqueeze(2).broadcast_to([P, n, P]), ALU.is_equal)


def kinds(dve, m, to, j):
    return dve.tensor_tensor(to, m.node_ramp[:, 0:NREL].unsqueeze(1).broadcast_to([P, U, NREL]),
                             m.etype[:, cols(j)].unsqueeze(2).broadcast_to([P, U, NREL]), ALU.is_equal)


def tiles_of_chunks(nc, m, engine, j):
    return tiles_at(nc, m, engine, cols(j))


def tiles_at(nc, m, engine, chunks):
    _, tiles = nc.values_load_multi_w_load_instructions(
        m.chunk_tile[0:1, chunks], engines=[engine], min_val=0, max_val=TILES - 1,
        skip_runtime_bounds_check_because="plan_chunks clamps the table")
    return tiles


def cols(j, n=U):
    return bass.ds(j * n, n)


@contextmanager
def semaphores(nc):
    with ExitStack() as ctx:
        handles = []

        def sem(name):
            handles.append(ctx.enter_context(nc.semaphore(name)))
            return handles[-1]

        yield sem
        with nc.Block() as block:
            @block.gpsimd
            def _(pool):
                for handle in handles:
                    pool.sem_clear(handle)


def load_constants(nc, m, A, sem):
    s_w, s_z, s_id = sem("weights_loaded"), sem("constants_zeroed"), sem("constants_made")
    s_i, s_row = sem("iota_done"), sem("rows_loaded")
    with nc.Block() as block:
        @block.sync
        def _(sp):
            n = 0

            def load(dst, src):
                nonlocal n
                sp.dma_start(dst, src).then_inc(s_w, 16)
                n += 16

            sp.wait_ge(s_z, 3)
            load(m.X[:, 0:FULL, :], A["x"][0:FULL * P, :].rearrange("(t p) d -> p t d", p=P))
            load(m.X[0:TAIL, FULL, :], A["x"][FULL * P:N, :])
            for e in range(P // EDIM):
                load(m.edge_w[e * EDIM:(e + 1) * EDIM, e * H0:(e + 1) * H0], A["L0_gnn_eW"])
            load(m.w_vqk[:, 0:D], A["L0_gnn_vW"])
            load(m.w_vqk[:, D:2 * D], A["L0_gnn_qW"])
            load(m.w_vqk[:, 2 * D:3 * D], A["L0_gnn_kW"])
            load(m.w_o[:, :], A["L0_gnn_oW"])
            load(m.w_f1[:, :], A["L0_gnn_f1W"])
            load(m.w_f2[:, :, :], A["L0_gnn_f2W"].rearrange("(c k) n -> k c n", k=P))
            load(m.w_g1[:, :], A["L2_gnn_W1"])
            load(m.w_g2[:, :], A["L2_gnn_W2"])
            load(m.w_rel[:, 0:NREL, :], A["L3_gnn_weight"].rearrange("r k n -> k r n"))
            load(m.w_rel[:, NREL, :], A["L3_gnn_root"])
            sp.wait_ge(s_w, n)

        @block.scalar
        def _(act):
            rows = [(m.b_vqk[:, 0:D], A["L0_gnn_vb"]), (m.b_vqk[:, D:2 * D], A["L0_gnn_qb"]),
                    (m.b_vqk[:, 2 * D:3 * D], A["L0_gnn_kb"]), (m.b_edge[:, :], A["L0_gnn_eb"]),
                    (m.b_o[:, :], A["L0_gnn_ob"]), (m.g_ln1[:, :], A["L0_gnn_ln1_g"]),
                    (m.b_ln1[:, :], A["L0_gnn_ln1_b"]), (m.b_f1[:, :], A["L0_gnn_f1b"]),
                    (m.g_lnf[:, :], A["L0_gnn_lnf_g"]), (m.b_lnf[:, :], A["L0_gnn_lnf_b"]),
                    (m.b_f2[:, :], A["L0_gnn_f2b"]), (m.g_ln2[:, :], A["L0_gnn_ln2_g"]),
                    (m.b_ln2[:, :], A["L0_gnn_ln2_b"]), (m.b_g1[:, :], A["L2_gnn_b1"]),
                    (m.b_g2[:, :], A["L2_gnn_b2"]), (m.b_rel[:, :], A["L3_gnn_bias"]),
                    (m.a_src1[:, :], A["L2_gnn_a_src1"].rearrange("h c -> (h c)")),
                    (m.a_dst1[:, :], A["L2_gnn_a_dst1"].rearrange("h c -> (h c)")),
                    (m.a_src2[:, :], A["L2_gnn_a_src2"].rearrange("h c -> (h c)")),
                    (m.a_dst2[:, :], A["L2_gnn_a_dst2"].rearrange("h c -> (h c)"))]
            for dst, src in rows:
                act.dma_start(dst, src.partition_broadcast(P)).then_inc(s_row, 16)
            act.wait_ge(s_row, 16 * len(rows))

        @block.vector
        def _(dve):
            dve.memset(m.X[:, :, :], 0.0).then_inc(s_z, 1)
            dve.memset(m.edge_w[:, :], 0.0).then_inc(s_z, 1)
            dve.memset(m.ident[:, :], 0.0).then_inc(s_z, 1)
            dve.memset(m.ones[:, :], 1.0).then_inc(s_z, 1)
            dve.memset(m.minus_half[:, :], -0.5)
            dve.wait_ge(s_i, 3)
            dve.tensor_copy(m.node_ramp[:, :], m.node_ramp_i[:, :]).then_inc(s_id, 1)
            dve.tensor_copy(m.node_id[:, :], m.node_i[:, :]).then_inc(s_id, 1)
            dve.tensor_copy(m.slot[:, :], m.slot_i[:, :]).then_inc(s_id, 1)
            dve.wait_ge(s_id, 5)
            dve.tensor_scalar(m.has_loop[:, :], m.node_id[:, :], float(SELF_LOOPS), None,
                              ALU.is_lt).then_inc(s_id, 1)

        @block.gpsimd
        def _(pool):
            pool.iota(m.node_ramp_i[:, :], [[1, P]], base=0, channel_multiplier=0).then_inc(s_i, 1)
            pool.iota(m.node_i[:, :], [[P, NT]], base=0, channel_multiplier=1).then_inc(s_i, 1)
            pool.iota(m.slot_i[:, :], [[0, 1]], base=0, channel_multiplier=1).then_inc(s_i, 1)
            pool.wait_ge(s_z, 4)
            pool.affine_select(out=m.ident[:, :], in_=m.ident[:, :], compare_op=ALU.not_equal, fill=1.0,
                               base=0, pattern=[[-1, P]], channel_multiplier=1).then_inc(s_id, 1)
            pool.affine_select(out=m.upto[:, :], in_=m.ones[:, 0:TILES], compare_op=ALU.is_ge, fill=0.0,
                               base=0, pattern=[[1, TILES]], channel_multiplier=-1).then_inc(s_id, 1)


def build_records(nc, m, A, sem):
    s_e, s_nextz = sem("edge_lists_loaded"), sem("next_dst_cleared")
    s_attr = [sem(f"attr_loaded{k}") for k in range(2)]
    s_rec_out = m.s_gather
    s_tr, s_trc, s_bias, s_rec = sem("attr_turned"), sem("attr_turned_copied"), sem("bias_made"), sem("record_made")
    s_pad, s_padout, s_cnt = sem("pad_made"), sem("pad_stored"), sem("edges_counted")
    rounds = EC // ROUND
    with ExitStack() as ctx:
        def sb(name, shape, dt=F32):
            return ctx.enter_context(nc.sbuf_tensor(name, shape, dt))

        room = m.own[0:EP, :, :].rearrange("p t d -> p (t d)")
        src_i, dst_i, typ_i, next_i = (room[:, k * EC:(k + 1) * EC].bitcast(I32) for k in range(4))
        dst_f, below = (room[:, k * EC:(k + 1) * EC] for k in (4, 5))
        edges_below = sb("edges_below", [EP, TILES + 1])
        attr = sb("attr", [EP, 2, ROUND * EDIM])
        attr_t = sb("attr_t", [P, 2, 4, P])
        rec = sb("rec", [EP, 2, ROUND, RECW])
        pad = sb("pad", [P, RECW])
        rec_i = rec[:, :, :, :].bitcast(I32)
        attr_d = A["edge_attr_32"].rearrange("(p i) k -> p (i k)", p=EP)
        rec_d = m.rec_dram[0:E, :].rearrange("(p i) w -> p i w", p=EP)

        with nc.Block() as block:
            @block.sync
            def _(sp):
                flat = lambda a: a.rearrange("(p i) -> p i", p=EP)
                sp.dma_start(dst_i[:, :], flat(A["dst"])).then_inc(s_e, 16)
                sp.dma_start(src_i[:, :], flat(A["src"])).then_inc(s_e, 16)
                sp.dma_start(typ_i[:, :], flat(A["edge_type_8"])).then_inc(s_e, 16)
                sp.wait_ge(s_nextz, 1)
                sp.dma_start(next_i[0:EP - 1, :], A["dst"][1:1 + (EP - 1) * EC].rearrange(
                    "(p i) -> p i", i=EC)).then_inc(s_e, 16)
                sp.dma_start(next_i[EP - 1:EP, 0:EC - 1], A["dst"][1 + (EP - 1) * EC:E].rearrange(
                    "(a i) -> a i", a=1)).then_inc(s_e, 16)

                def load(r, k, i):
                    after(sp, s_tr, r - 1)
                    sp.dma_start(attr[:, k, :], attr_d[:, bass.ds(r * (ROUND * EDIM), ROUND * EDIM)]
                                 ).then_inc(s_attr[k], 16)
                in_pairs(sp, rounds, load)
                sp.wait_ge(s_pad, 2)
                sp.dma_start(m.rec_dram[E:E + P, :], pad[:, :]).then_inc(s_padout, 16)
                sp.wait_ge(s_padout, 16)

            @block.tensor
            def _(pe):
                def turn(r, k, i):
                    pe.wait_ge(s_attr[k], i * 16 + 16)
                    for q in range(4):
                        last = pe.transpose(m.ps_t[:, k, q * P:q * P + EP], attr[:, k, q * P:(q + 1) * P],
                                            m.ident[0:EP, 0:EP])
                    last.then_inc(s_tr, 1)
                    pe.wait_ge(s_trc, r + 1)
                    after(pe, s_rec, r - 1)
                    for q in range(4):
                        last = pe.matmul(m.ps_k[0:EP, k, q * EDIM:(q + 1) * EDIM], attr_t[:, k, q, 0:EP],
                                         m.edge_w[:, :], start=True, stop=True)
                    last.then_inc(s_bias, 1)
                in_pairs(pe, rounds, turn)

            @block.scalar
            def _(act):
                def copy(r, k, i):
                    after(act, s_bias, r - 1)
                    act.wait_ge(s_tr, r + 1)
                    act.copy(attr_t[:, k, :, 0:EP], m.ps_t[:, k, :].rearrange("p (q e) -> p q e", q=4)[:, :, 0:EP]
                             ).then_inc(s_trc, 1)
                in_pairs(act, rounds, copy)

            @block.vector
            def _(dve):
                dve.memset(next_i[:, :], -1).then_inc(s_nextz, 1)
                dve.memset(pad[:, :], 0.0).then_inc(s_pad, 1)
                dve.wait_ge(s_pad, 1)
                dve.memset(pad[:, R_DST:R_DST + 1], 1.0e7).then_inc(s_pad, 1)
                dve.wait_ge(s_e, 16 * 5)
                dve.tensor_copy(dst_f[:, :], dst_i[:, :]).then_inc(s_cnt, 1)
                dve.memset(edges_below[:, 0:1], 0.0).then_inc(s_cnt, 1)
                dve.wait_ge(s_cnt, 2)
                for t in range(TILES):
                    dve.tensor_scalar(below[:, :], dst_f[:, :], float((t + 1) * P), None, ALU.is_lt
                                      ).then_inc(s_cnt, 1)
                    dve.wait_ge(s_cnt, 3 + 2 * t)
                    dve.tensor_reduce(edges_below[:, t + 1:t + 2], below[:, :], AX, ALU.add).then_inc(s_cnt, 1)
                    dve.wait_ge(s_cnt, 4 + 2 * t)
                dve.tensor_tensor(m.tile_edges[:, :], edges_below[:, 1:TILES + 1], edges_below[:, 0:TILES],
                                  ALU.subtract).then_inc(s_cnt, 1)

                def record(r, k, i):
                    after(dve, s_rec_out[k], i * 16)
                    dve.wait_ge(s_bias, r + 1)
                    at = bass.ds(r * ROUND, ROUND)
                    dve.tensor_copy(rec_i[:, k, :, R_SRC], src_i[:, at])
                    dve.tensor_copy(rec[:, k, :, R_DST], dst_i[:, at])
                    dve.tensor_copy(rec[:, k, :, R_TYP], typ_i[:, at])
                    dve.tensor_copy(rec[:, k, :, R_NEXT], next_i[:, at])
                    dve.tensor_tensor(rec[:, k, :, R_BIAS:R_BIAS + H0],
                                      m.ps_k[0:EP, k, 0:4 * EDIM].rearrange("p (e h) -> p e h", h=H0),
                                      m.b_edge[0:EP, :].unsqueeze(1).broadcast_to([EP, ROUND, H0]),
                                      ALU.add).then_inc(s_rec, 1)
                in_pairs(dve, rounds, record)

            @block.gpsimd
            def _(pool):
                def store(r, k, i):
                    apart(pool, s_rec, r + 1)
                    pool.dma_start(rec_d[:, bass.ds(r * ROUND, ROUND), :], rec[:, k, :, :]).then_inc(s_rec_out[k], 16)
                in_pairs(pool, rounds, store)
                for k in range(2):
                    pool.wait_ge(s_rec_out[k], 16 * (rounds // 2))
    for k in range(2):
        m.gathered[k] += 16 * (rounds // 2)


def plan_chunks(nc, m, A, sem):
    s_pe, s_v, s_plan, s_r = sem("plan_products"), sem("plan_steps"), sem("plan_made"), [
        sem("records_in_sp"), sem("records_in_act")]
    s_ramp = sem("chunk_ramp_made")
    half = NCH // 2
    with ExitStack() as ctx:
        def sb(name, shape, dt=F32):
            return ctx.enter_context(nc.sbuf_tensor(name, shape, dt))

        cnt, cnt_i, nch = sb("cnt", [TILES, 1]), sb("cnt_i", [TILES, 1], I32), sb("nch", [TILES, 1])
        slack, last = sb("slack", [TILES, 1]), sb("last_chunk", [TILES, 1])
        past, first = sb("past", [TILES, NCH]), sb("first_edge", [1, NCH])
        first_i = sb("first_edge_i", [1, NCH], I32)
        tile_f = sb("tile_f", [P, NCH])
        ramp = sb("chunk_ramp", [TILES, NCH])
        with nc.Block() as block:
            @block.tensor
            def _(pe):
                pe.matmul(m.ps_t[0:TILES, 0, 0:1], m.tile_edges[:, :], m.ones[0:EP, 0:1], start=True, stop=True
                          ).then_inc(s_pe, 1)
                pe.wait_ge(s_v, 6)
                pe.matmul(m.ps_k[0:TILES, 0, 0:1], m.upto[0:TILES, :], nch[:, :], start=True, stop=True
                          ).then_inc(s_pe, 1)
                pe.wait_ge(s_v, 9)
                for h in range(2):
                    part = past[:, h * half:(h + 1) * half]
                    pe.matmul(m.ps_o[:, 0, h, 0:half], m.ones[0:TILES, :], part, start=True, stop=True)
                    pe.matmul(m.ps_o[0:1, 1, h, 0:half], slack[:, :], part, start=True, stop=True
                              ).then_inc(s_pe, 1)

            @block.vector
            def _(dve):
                n = 0

                def step(ins):
                    nonlocal n
                    n += 1
                    ins.then_inc(s_v, 1)
                    dve.wait_ge(s_v, n)

                dve.wait_ge(s_ramp, 1)
                step(dve.tensor_copy(ramp[:, :], m.dst_slot[0:TILES, 0:NCH].bitcast(I32)))
                dve.wait_ge(s_pe, 1)
                step(dve.tensor_copy(cnt[:, :], m.ps_t[0:TILES, 0, 0:1]))
                step(dve.tensor_scalar(cnt_i[:, :], cnt[:, :], float(P - 1), None, ALU.add))
                step(dve.tensor_scalar(cnt_i[:, :], cnt_i[:, :], 7, None, ALU.arith_shift_right))
                step(dve.tensor_copy(nch[:, :], cnt_i[:, :]))
                step(dve.scalar_tensor_tensor(slack[:, :], nch[:, :], -float(P), cnt[:, :], ALU.mult, ALU.add))
                dve.wait_ge(s_pe, 2)
                step(dve.tensor_copy(last[:, :], m.ps_k[0:TILES, 0, 0:1]))
                step(dve.tensor_scalar(past[:, :], ramp[:, :], last[:, 0:1], None, ALU.is_ge))
                step(dve.memset(m.dst_slot[:, :], -1.0))
                dve.wait_ge(s_pe, 4)
                step(dve.tensor_scalar(tile_f[:, :].rearrange("p (h c) -> p h c", h=2), m.ps_o[:, 0, :, 0:half],
                                       float(TILES - 1), None, ALU.min))
                step(dve.memset(m.chunk_tile[:, :], 0))
                step(dve.tensor_copy(m.chunk_tile[0:1, 0:NCH], tile_f[0:1, :]))
                step(dve.scalar_tensor_tensor(first[:, :].rearrange("p (h c) -> p h c", h=2),
                                              ramp[0:1, :].rearrange("p (h c) -> p h c", h=2), float(P),
                                              m.ps_o[0:1, 1, :, 0:half], ALU.mult, ALU.add))
                step(dve.tensor_scalar(first_i[:, :], first[:, :], float(E), None, ALU.min))
                dve.sem_inc(s_plan, 1)
                for c in range(2):
                    dve.wait_ge(s_r[c], 16 * half)
                step(dve.tensor_scalar(tile_f[:, :], tile_f[:, :], -float(P), None, ALU.mult))
                step(dve.tensor_tensor(m.dst_slot[:, 0:NCH], m.R[:, :, R_DST], tile_f[:, :], ALU.add))
                step(dve.memset(m.etype[:, :], 0.0))
                step(dve.memset(m.src_idx[:, :], 0))
                step(dve.memset(m.rel_idx[:, :], 0))
                step(dve.memset(m.rel_w[:, :], 0.0))
                step(dve.tensor_copy(m.etype[:, 0:NCH], m.R[:, :, R_TYP]))
                step(dve.tensor_copy(m.src_idx[:, 0:NCH], m.R[:, :, R_SRC].bitcast(I32)))
                step(dve.scalar_tensor_tensor(m.rel_idx[:, 0:NCH], m.src_idx[:, 0:NCH], float(NREL),
                                              m.etype[:, 0:NCH], ALU.mult, ALU.add))
                step(dve.tensor_tensor(m.is_last[:, :], m.R[:, :, R_DST], m.R[:, :, R_NEXT], ALU.not_equal))
                step(dve.tensor_scalar(m.at_end[:, :], m.slot[:, :], float(P - 1), None, ALU.is_equal))
                step(dve.tensor_scalar(m.is_last[:, :], m.is_last[:, :], m.at_end[:, 0:1], None, ALU.max))

            @block.gpsimd
            def _(pool):
                pool.iota(m.dst_slot[0:TILES, 0:NCH].bitcast(I32), [[1, NCH]], base=0, channel_multiplier=0
                          ).then_inc(s_ramp, 1)

            def load_half(eng, engine, c):
                eng.wait_ge(s_plan, 1)
                with eng.Fori(0, half // 4) as i:
                    _, at = nc.values_load_multi_w_load_instructions(
                        first_i[0:1, bass.ds(i * 4 + c * half, 4)], engines=[engine], min_val=0, max_val=E,
                        skip_runtime_bounds_check_because="clamped above")
                    for u in range(4):
                        eng.dma_start(m.R[:, bass.ds(i * 4 + (c * half + u), 1), :],
                                      m.rec_dram[bass.ds(at[u], P), :].unsqueeze(1)).then_inc(s_r[c], 16)

            @block.sync
            def _(sp):
                load_half(sp, ENG.SP, 0)

            @block.scalar
            def _(act):
                load_half(act, ENG.Activation, 1)


def allocate(nc, ctx):
    def sb(name, shape, dt=F32):
        return ctx.enter_context(nc.sbuf_tensor(name, shape, dt))

    m = Core()
    m.ident, m.ones, m.upto = sb("ident", [P, P]), sb("ones", [P, P]), sb("upto", [P, TILES])
    m.node_i, m.node_id, m.has_loop = sb("node_i", [P, NT], I32), sb("node_id", [P, NT]), sb("has_loop", [P, NT])
    m.slot_i, m.slot, m.at_end = sb("slot_i", [P, 1], I32), sb("slot", [P, 1]), sb("at_end", [P, 1])
    m.edge_w = sb("edge_w", [P, EDIM])
    m.w_vqk, m.b_vqk = sb("w_vqk", [P, 3 * D]), sb("b_vqk", [P, 3 * D])
    m.b_edge = sb("b_edge", [P, H0])
    m.w_o, m.w_f1, m.w_f2 = sb("w_o", [P, D]), sb("w_f1", [P, FFN]), sb("w_f2", [P, FFN // P, D])
    m.w_g1, m.w_g2, m.w_rel = sb("w_g1", [P, D]), sb("w_g2", [P, D]), sb("w_rel", [P, NREL + 1, D])
    m.b_o, m.g_ln1, m.b_ln1, m.b_f2 = sb("b_o", [P, D]), sb("g_ln1", [P, D]), sb("b_ln1", [P, D]), sb("b_f2", [P, D])
    m.g_ln2, m.b_ln2, m.b_g1, m.b_g2 = sb("g_ln2", [P, D]), sb("b_ln2", [P, D]), sb("b_g1", [P, D]), sb("b_g2", [P, D])
    m.b_rel, m.a_src1, m.a_dst1 = sb("b_rel", [P, D]), sb("a_src1", [P, D]), sb("a_dst1", [P, D])
    m.a_src2, m.a_dst2 = sb("a_src2", [P, D]), sb("a_dst2", [P, D])
    m.b_f1, m.g_lnf, m.b_lnf = sb("b_f1", [P, FFN]), sb("g_lnf", [P, FFN]), sb("b_lnf", [P, FFN])
    m.X = sb("X", [P, NT, D])
    m.own = sb("own", [P, NT, D])
    m.acc = sb("acc", [P, NT, D + H0 + NREL])
    m.R = sb("R", [P, NCH, RECW])
    m.top = sb("top", [P, NT, 2 * H0])
    m.dinv = sb("dinv", [P, NT])
    m.a_s, m.a_d = sb("a_s", [P, NT, 4]), sb("a_d", [P, NT, 4])
    m.tile_edges = sb("tile_edges", [EP, TILES])
    m.dst_slot, m.etype, m.rel_w = sb("dst_slot", [P, NCH]), sb("etype", [P, NCH]), sb("rel_w", [P, NCH])
    m.src_idx, m.rel_idx = sb("src_idx", [P, NCH], I32), sb("rel_idx", [P, NCH], I32)
    m.is_last = sb("is_last", [P, NCH])
    m.chunk_tile = sb("chunk_tile", [1, NCH], I32)
    m.node_ramp_i, m.node_ramp = sb("node_ramp_i", [P, P], I32), sb("node_ramp", [P, P])
    m.minus_half = sb("minus_half", [P, NT])
    m.tmp = sb("tmp", [P, D])
    m.loop_off = sb("loop_off", [P, NT])
    m.ps_t = ctx.enter_context(nc.psum_tensor("ps_t", [P, 2, 512], F32))
    m.ps_k = ctx.enter_context(nc.psum_tensor("ps_k", [P, 2, 512], F32))
    m.ps_o = ctx.enter_context(nc.psum_tensor("ps_o", [P, 2, 2, 512], F32))
    m.scratch = m.acc[:, :, :].rearrange("p t w -> p (t w)")
    m.table_vq = nc.dram_tensor("table_vq", (NP, 2 * D), F32).ap()
    m.table_h = nc.dram_tensor("table_h", (NP, D), F32).ap()
    m.table_g = nc.dram_tensor("table_g", (NP, D + 4), F32).ap()
    m.table_r = nc.dram_tensor("table_r", (NP * NREL, D), F32).ap()
    m.rows_dram = nc.dram_tensor("rows_dram", (P, NCH, D), F32).ap()
    m.rec_dram = nc.dram_tensor("rec_dram", (E + P, RECW), F32).ap()
    return m


def project(nc, sem, m, tag, prepare, weight, width, finish, table=None, table_width=0):
    s_in, s_tr, s_trc = sem(tag + "_staged"), sem(tag + "_turned"), sem(tag + "_turned_copied")
    s_mm, s_out = sem(tag + "_product"), sem(tag + "_out")
    s_store = [sem(f"{tag}_stored{k}") for k in range(2)]
    banks = -(-width // 512)
    step = width // banks
    with ExitStack() as ctx:
        staged = ctx.enter_context(nc.sbuf_tensor(tag + "_in", [P, 2, D], F32))
        rows_t = ctx.enter_context(nc.sbuf_tensor(tag + "_t", [P, 2, D], F32))
        out = ctx.enter_context(nc.sbuf_tensor(tag + "_o", [P, 2, width], F32))
        with nc.Block() as block:
            @block.vector
            def _(dve):
                def stage(t, k):
                    after(dve, s_tr, t - 1)
                    prepare(dve, staged[:, k, :], t)
                    dve.drain().then_inc(s_in, 1)

                def end(t, k, i):
                    if table is not None:
                        after(dve, s_store[k], i * 16)
                    dve.wait_ge(s_mm, t + 1)
                    finish(dve, out[:, k, :], m.ps_o[:, k, 0:banks, 0:step], t)
                    dve.drain().then_inc(s_out, 1)

                stage(0, 0)
                stage(1, 1)
                end(0, 0, 0)
                stage(2, 0)
                end(1, 1, 0)
                with dve.Fori(1, NT // 2 - 1) as i:
                    stage(i * 2 + 1, 1)
                    end(i * 2, 0, i)
                    stage(i * 2 + 2, 0)
                    end(i * 2 + 1, 1, i)
                stage(NT - 1, 1)
                end(NT - 2, 0, NT // 2 - 1)
                end(NT - 1, 1, NT // 2 - 1)

            @block.tensor
            def _(pe):
                def body(t, k, i):
                    pe.wait_ge(s_in, t + 1)
                    pe.transpose(m.ps_t[:, k, 0:P], staged[:, k, :], m.ident[:, :]).then_inc(s_tr, 1)
                    pe.wait_ge(s_trc, t + 1)
                    after(pe, s_out, t - 1)
                    for b in range(banks):
                        last = pe.matmul(m.ps_o[:, k, b, 0:step], rows_t[:, k, :],
                                         weight[:, b * step:(b + 1) * step], start=True, stop=True)
                    last.then_inc(s_mm, 1)
                in_pairs(pe, NT, body)

            @block.scalar
            def _(act):
                def body(t, k, i):
                    act.wait_ge(s_tr, t + 1)
                    after(act, s_mm, t - 1)
                    act.copy(rows_t[:, k, :], m.ps_t[:, k, 0:P]).then_inc(s_trc, 1)
                in_pairs(act, NT, body)

            if table is not None:
                @block.sync
                def _(sp):
                    def body(t, k, i):
                        sp.wait_ge(s_out, t + 1)
                        sp.dma_start(table[bass.ds(t * P, P), :], out[:, k, 0:table_width]).then_inc(s_store[k], 16)
                    in_pairs(sp, NT, body)
                    for k in range(2):
                        sp.wait_ge(s_store[k], 16 * (NT // 2))


def layer_norm(nc, sem, m, tag, rows, gain=None, shift=None, add=None):
    s_var, s_rstd = sem(tag + "_variance"), sem(tag + "_rstd")
    with ExitStack() as ctx:
        def sb(name, shape):
            return ctx.enter_context(nc.sbuf_tensor(tag + name, shape, F32))

        stats = sb("_stats", [P, NT, 6])
        mean, var, rstd, diff = (sb(n, [P, NT]) for n in ("_mean", "_var", "_rstd", "_diff"))
        with nc.Block() as block:
            @block.vector
            def _(dve):
                if add is not None:
                    dve.tensor_tensor(rows, rows, add, ALU.add)
                    dve.drain()
                with dve.Fori(0, NT // 2) as i:
                    for k in range(2):
                        dve.bn_stats(stats[:, bass.ds(i * 2 + k, 1), :], rows[:, bass.ds(i * 2 + k, 1), :])
                dve.drain()
                dve.tensor_tensor(mean[:, :], stats[:, :, 1], stats[:, :, 4], ALU.add)
                dve.tensor_tensor(diff[:, :], stats[:, :, 1], stats[:, :, 4], ALU.subtract)
                dve.tensor_tensor(var[:, :], stats[:, :, 2], stats[:, :, 5], ALU.add)
                dve.drain()
                dve.tensor_scalar(mean[:, :], mean[:, :], 0.5, None, ALU.mult)
                dve.tensor_tensor(diff[:, :], diff[:, :], diff[:, :], ALU.mult)
                dve.tensor_scalar(var[:, :], var[:, :], 1.0 / D, None, ALU.mult)
                dve.drain()
                dve.scalar_tensor_tensor(var[:, :], diff[:, :], 0.25, var[:, :], ALU.mult, ALU.add)
                dve.drain()
                dve.tensor_scalar(var[:, :], var[:, :], EPS, None, ALU.add).then_inc(s_var, 1)
                dve.wait_ge(s_rstd, 1)
                with dve.Fori(0, NT // 2) as i:
                    for k in range(2):
                        t = bass.ds(i * 2 + k, 1)
                        dve.tensor_scalar(rows[:, t, :], rows[:, t, :], mean[:, t], rstd[:, t], ALU.subtract, ALU.mult)
                    if gain is not None:
                        two = bass.ds(i * 2, 2)
                        dve.drain()
                        dve.tensor_tensor(rows[:, two, :], rows[:, two, :], gain.unsqueeze(1).broadcast_to([P, 2, D]), ALU.mult)
                        dve.drain()
                        dve.tensor_tensor(rows[:, two, :], rows[:, two, :], shift.unsqueeze(1).broadcast_to([P, 2, D]), ALU.add)

            @block.gpsimd
            def _(pool):
                pool.wait_ge(s_var, 1)
                pool.tensor_tensor(rstd[:, :], var[:, :], m.minus_half[:, 0:var.shape[1]], ALU.pow).then_inc(s_rstd, 1)


def score_pass(nc, sem, m, tag, table, width, heads, dot):
    s_idx, s_oh = sem(tag + "_indices"), sem(tag + "_one_hot")
    s_gather, base = m.s_gather, list(m.gathered)
    s_spill = [sem(f"{tag}_spilled{s}") for s in range(RING)]
    s_tr, s_trc, s_ex = sem(tag + "_turned"), sem(tag + "_turned_copied"), sem(tag + "_spread")
    s_used = sem(tag + "_used")
    own = heads if not dot else D
    with ExitStack() as ctx:
        def sb(name, shape, dt=F32):
            return ctx.enter_context(nc.sbuf_tensor(tag + name, shape, dt))

        idx = sb("_idx", [P, RING, U], I32)
        got = sb("_got", [P, RING, U, width])
        hot, hot_t = sb("_hot", [P, 2, U, P]), sb("_hot_t", [P, 2, U, P])
        dots = sb("_dots", [P, U, heads])
        with nc.Block() as block:
            @block.gpsimd
            def _(pool):
                def body(j, s, i):
                    apart(pool, s_idx, j + 1)
                    apart(pool, s_spill[s], i * 16)
                    for u in range(U):
                        pool.indirect_dma_start(got[:, s, u, :], None, table, bass.IndirectOffsetOnAxis(
                            ap=idx[:, s, u:u + 1], axis=0)).then_inc(s_gather[s], 16)
                in_rounds(pool, NG, RING, body)

            @block.sync
            def _(sp):
                def body(j, s, i):
                    sp.wait_ge(s_gather[s], i * (16 * U) + (base[s] + 16 * U))
                    sp.dma_start(m.rows_dram[:, cols(j), :], got[:, s, :, 0:D]).then_inc(s_spill[s], 16)
                in_rounds(sp, NG, RING, body)
                for s in range(RING):
                    sp.wait_ge(s_spill[s], 16 * (NG // RING))

            @block.tensor
            def _(pe):
                def body(j, s, i):
                    k = s % 2
                    pe.wait_ge(s_oh, j + 1)
                    for u in range(U):
                        last = pe.transpose(m.ps_t[:, k, u * P:(u + 1) * P], hot[:, k, u, :], m.ident[:, :])
                    last.then_inc(s_tr, 1)
                    tiles = tiles_of_chunks(nc, m, ENG.PE, j)
                    after(pe, s_used, j - 1)
                    pe.wait_ge(s_trc, j + 1)
                    for u in range(U):
                        rows = (m.own if dot else m.a_d)[:, bass.ds(tiles[u], 1), 0:own]
                        last = pe.matmul(m.ps_k[:, k, u * own:(u + 1) * own], hot_t[:, k, u, :], rows,
                                         start=True, stop=True)
                    last.then_inc(s_ex, 1)
                in_rounds(pe, NG, RING, body)

            @block.scalar
            def _(act):
                def body(j, s, i):
                    k = s % 2
                    act.wait_ge(s_tr, j + 1)
                    after(act, s_ex, j - 1)
                    act.copy(hot_t[:, k, :, :], m.ps_t[:, k, :].rearrange("p (u e) -> p u e", u=U)).then_inc(s_trc, 1)
                in_rounds(act, NG, RING, body)

            @block.vector
            def _(dve):
                def stage_indices(j, s):
                    dve.tensor_copy(idx[:, s, :], m.src_idx[:, cols(j)]).then_inc(s_idx, 1)

                def stage_one_hot(j, k):
                    after(dve, s_tr, j - 1)
                    one_hot(dve, m, hot[:, k, :, :], cols(j), U).then_inc(s_oh, 1)

                def score(j, s, i):
                    k = s % 2
                    dve.wait_ge(s_ex, j + 1)
                    dve.wait_ge(s_gather[s], i * (16 * U) + (base[s] + 16 * U))
                    at = m.R[:, cols(j), R_BIAS:R_BIAS + heads]
                    if not dot:
                        dve.tensor_tensor(dots[:, :, :], got[:, s, :, D:D + heads],
                                          m.ps_k[:, k, 0:U * own].rearrange("p (u h) -> p u h", u=U), ALU.add)
                        dve.drain()
                        dve.scalar_tensor_tensor(at, dots[:, :, :], 0.2, dots[:, :, :], ALU.mult, ALU.max)
                        dve.drain().then_inc(s_used, 1)
                        return
                    q = got[:, s, :, D:2 * D]
                    dve.tensor_tensor(q, q, m.ps_k[:, k, :].rearrange("p (u d) -> p u d", u=U), ALU.mult)
                    dve.drain()
                    dve.tensor_reduce(dots[:, :, :], q.rearrange("p u (h c) -> p u h c", h=heads), AX, ALU.add)
                    dve.drain()
                    dve.scalar_tensor_tensor(at, dots[:, :, :], float(D // heads) ** -0.5, at, ALU.mult, ALU.add)
                    dve.drain().then_inc(s_used, 1)

                def body(j, s, i):
                    if within(j + 3):
                        stage_indices(j + 3, (s + 3) % RING)
                    if within(j + 1):
                        stage_one_hot(j + 1, (s + 1) % 2)
                    score(j, s, i)
                for j in range(3):
                    stage_indices(j, j)
                stage_one_hot(0, 0)
                in_rounds(dve, NG, RING, body)
    count_gathers(m)


def score_maximum(nc, sem, m, tag, heads):
    G = min(P // heads, 32)
    rows, quads, steps = G * heads, G // U, NCH // G
    s_st, s_tr, s_run, s_bk = sem(tag + "_staged"), sem(tag + "_turned"), sem(tag + "_run"), sem(tag + "_back")
    s_fl, s_oh, s_mm, s_top = sem(tag + "_flagged"), sem(tag + "_one_hot"), sem(tag + "_sent"), sem(tag + "_taken")
    assert steps * G == NCH and steps % 2 == 0 and quads % 2 == 0
    w = heads + 1
    with ExitStack() as ctx:
        def sb(name, shape):
            return ctx.enter_context(nc.sbuf_tensor(tag + name, shape, F32))

        value, last = sb("_value", [P, 2, G, heads]), sb("_last", [P, 2, G, heads])
        cut, run = sb("_cut", [rows, P]), sb("_run", [rows, 2, P])
        sent, present = sb("_sent", [P, 2, G, w]), sb("_present", [P, G])
        found = sb("_found", [P, G, heads])
        tops = sb("_tops", [P, U, NT, heads])
        hot = sb("_hot", [P, 2, U, P])
        with nc.Block() as block:
            @block.vector
            def _(dve):
                def stage(g, k):
                    here = bass.ds(g * G, G)
                    dve.tensor_copy(value[:, k, :, :], m.R[:, here, R_BIAS:R_BIAS + heads])
                    dve.tensor_copy(last[:, k, :, :], m.is_last[:, here].unsqueeze(2).broadcast_to([P, G, heads]))
                    dve.drain().then_inc(s_st, 1)

                def scan(g, k):
                    dve.wait_ge(s_tr, g + 1)
                    dve.tensor_scalar(cut[:, 1:P], m.ps_t[0:rows, k, P:2 * P - 1], -BIG, None, ALU.mult)
                    dve.drain()
                    dve.tensor_tensor_scan(run[:, k, :], cut[:, :], m.ps_t[0:rows, k, 0:P], -BIG, ALU.add, ALU.max)
                    dve.drain().then_inc(s_run, 1)

                def flag(g, k):
                    dve.wait_ge(s_bk, g + 1)
                    after(dve, s_mm, (g - 1) * quads)
                    dve.tensor_tensor(sent[:, k, :, 0:heads], m.ps_k[:, k, 0:rows].rearrange("p (g h) -> p g h", g=G),
                                      last[:, k, :, :], ALU.mult)
                    dve.tensor_copy(sent[:, k, :, heads], m.is_last[:, bass.ds(g * G, G)])
                    dve.drain().then_inc(s_fl, 1)

                def one_hots(g):
                    for q in range(quads):
                        after(dve, s_mm, g * quads + (q - 1))
                        one_hot(dve, m, hot[:, q % 2, :, :], bass.ds(g * G + q * U, U), U).then_inc(s_oh, 1)

                def take(g, k):
                    dve.wait_ge(s_mm, g * quads + quads)
                    res = m.ps_o[:, k, 0, 0:G * w].rearrange("p (g w) -> p g w", g=G)
                    dve.tensor_scalar(present[:, :], res[:, :, heads], BIG, -BIG, ALU.mult, ALU.add)
                    dve.drain()
                    dve.tensor_tensor(found[:, :, :], res[:, :, 0:heads],
                                      present[:, :].unsqueeze(2).broadcast_to([P, G, heads]), ALU.add)
                    for q in range(quads):
                        tiles = tiles_at(nc, m, ENG.DVE, bass.ds(g * G + q * U, U))
                        dve.drain()
                        for u in range(U):
                            top = tops[:, u, bass.ds(tiles[u], 1), :]
                            dve.tensor_tensor(top, top, found[:, q * U + u, :].unsqueeze(1), ALU.max)
                    dve.drain().then_inc(s_top, 1)

                def body(g, k, i):
                    if within(g + 1, steps):
                        scan(g + 1, 1 - k)
                    flag(g, k)
                    if within(g + 2, steps):
                        stage(g + 2, k)
                    one_hots(g)
                    if began(g - 1):
                        take(g - 1, 1 - k)

                dve.memset(cut[:, :], 0.0)
                dve.memset(tops[:, :, :, :], -BIG)
                stage(0, 0)
                stage(1, 1)
                scan(0, 0)
                in_rounds(dve, steps, 2, body)
                take(steps - 1, 1)
                dve.tensor_tensor(tops[:, 0:2, :, :], tops[:, 0:2, :, :], tops[:, 2:4, :, :], ALU.max)
                dve.drain()
                dve.tensor_tensor(tops[:, 0, :, :], tops[:, 0, :, :], tops[:, 1, :, :], ALU.max)
                dve.drain()
                dve.tensor_tensor(m.top[:, :, 0:heads], m.top[:, :, 0:heads], tops[:, 0, :, :], ALU.max)

            @block.tensor
            def _(pe):
                def turn(g, k):
                    apart(pe, s_st, g + 1)
                    apart(pe, s_run, g - 1)
                    pe.transpose(m.ps_t[0:rows, k, 0:P], value[:, k, :, :].rearrange("p g h -> p (g h)"),
                                 m.ident[:, :])
                    pe.transpose(m.ps_t[0:rows, k, P:2 * P], last[:, k, :, :].rearrange("p g h -> p (g h)"),
                                 m.ident[:, :]).then_inc(s_tr, 1)

                def back(g, k):
                    apart(pe, s_run, g + 1)
                    apart(pe, s_fl, g - 1)
                    pe.transpose(m.ps_k[:, k, 0:rows], run[:, k, :], m.ident[0:rows, 0:rows]).then_inc(s_bk, 1)

                def body(g, k, i):
                    if within(g + 1, steps):
                        back(g + 1, 1 - k)
                    if within(g + 2, steps):
                        turn(g + 2, k)
                    apart(pe, s_fl, g + 1)
                    apart(pe, s_top, g - 1)
                    for q in range(quads):
                        pe.wait_ge(s_oh, g * quads + (q + 1))
                        for u in range(U):
                            c = q * U + u
                            mm = pe.matmul(m.ps_o[:, k, 0, c * w:(c + 1) * w], hot[:, q % 2, u, :], sent[:, k, c, :],
                                           start=True, stop=True)
                        mm.then_inc(s_mm, 1)

                turn(0, 0)
                turn(1, 1)
                back(0, 0)
                in_rounds(pe, steps, 2, body)


def value_pass(nc, sem, m, tag, heads, count=False, pick=False):
    s_oh, s_rows = sem(tag + "_one_hot"), [sem(f"{tag}_rows{k}") for k in range(2)]
    s_tr, s_trc, s_ex = sem(tag + "_turned"), sem(tag + "_turned_copied"), sem(tag + "_spread")
    s_d, s_p, s_wr = sem(tag + "_differences"), sem(tag + "_weights"), sem(tag + "_weighted")
    s_sum, s_acc = sem(tag + "_summed"), sem(tag + "_added")
    W = D + heads + (NREL if count else 0)
    span = 2 * H0 if pick else heads
    with ExitStack() as ctx:
        def sb(name, shape):
            return ctx.enter_context(nc.sbuf_tensor(tag + name, shape, F32))

        hot, hot_t = sb("_hot", [P, RING, U, P]), sb("_hot_t", [P, 2, U, P])
        kind = sb("_kind", [P, RING, U, NREL])
        diff = sb("_diff", [P, 2, U, heads])
        rows = sb("_rows", [P, 2, U, D])
        weighted = sb("_weighted", [P, 2, U, W])
        with nc.Block() as block:
            @block.sync
            def _(sp):
                def body(j, s, i):
                    after(sp, s_wr, j - 1)
                    sp.dma_start(rows[:, s % 2, :, :], m.rows_dram[:, cols(j), :]).then_inc(s_rows[s % 2], 16)
                in_rounds(sp, NG, RING, body)

            @block.tensor
            def _(pe):
                def total(j, s):
                    k = s % 2
                    pe.wait_ge(s_wr, j + 1)
                    after(pe, s_acc, j - 1)
                    for u in range(U):
                        last = pe.matmul(m.ps_o[:, k, u // 2, (u % 2) * W:(u % 2 + 1) * W], hot[:, s, u, :],
                                         weighted[:, k, u, :], start=True, stop=True)
                    last.then_inc(s_sum, 1)

                def body(j, s, i):
                    k = s % 2
                    pe.wait_ge(s_oh, j + 1)
                    for u in range(U):
                        last = pe.transpose(m.ps_t[:, k, u * P:(u + 1) * P], hot[:, s, u, :], m.ident[:, :])
                    last.then_inc(s_tr, 1)
                    if began(j - 2):
                        total(j - 2, (s + 2) % RING)
                    tiles = tiles_of_chunks(nc, m, ENG.PE, j)
                    pe.wait_ge(s_trc, j + 1)
                    after(pe, s_d, j - 1)
                    for u in range(U):
                        last = pe.matmul(m.ps_k[:, k, u * span:(u + 1) * span], hot_t[:, k, u, :],
                                         m.top[:, bass.ds(tiles[u], 1), 0:span], start=True, stop=True)
                    last.then_inc(s_ex, 1)
                in_rounds(pe, NG, RING, body)
                total(NG - 2, RING - 2)
                total(NG - 1, RING - 1)

            @block.scalar
            def _(act):
                def copy(j, k):
                    act.wait_ge(s_tr, j + 1)
                    after(act, s_ex, j - 1)
                    act.copy(hot_t[:, k, :, :], m.ps_t[:, k, :].rearrange("p (u e) -> p u e", u=U)).then_inc(s_trc, 1)

                def body(j, s, i):
                    k = s % 2
                    if within(j + 1):
                        copy(j + 1, 1 - k)
                    after(act, s_sum, j - 1)
                    act.wait_ge(s_d, j + 1)
                    act.activation(weighted[:, k, :, D:D + heads], diff[:, k, :, :], ACT.Exp).then_inc(s_p, 1)
                copy(0, 0)
                in_rounds(act, NG, RING, body)

            @block.vector
            def _(dve):
                def stage(j, s):
                    after(dve, s_sum, j - 3)
                    if pick:
                        kinds(dve, m, kind[:, s, :, :], j)
                    one_hot(dve, m, hot[:, s, :, :], cols(j), U).then_inc(s_oh, 1)

                def differences(j, s):
                    k = s % 2
                    dve.wait_ge(s_ex, j + 1)
                    after(dve, s_p, j - 1)
                    spread = m.ps_k[:, k, 0:U * span].rearrange("p (u h) -> p u h", u=U)
                    dve.tensor_tensor(diff[:, k, :, :], m.R[:, cols(j), R_BIAS:R_BIAS + heads], spread[:, :, 0:heads],
                                      ALU.subtract)
                    if pick:
                        dve.tensor_tensor(kind[:, s, :, :], kind[:, s, :, :], spread[:, :, H0:2 * H0], ALU.mult)
                    dve.drain().then_inc(s_d, 1)
                    if pick:
                        dve.tensor_reduce(m.rel_w[:, cols(j)], kind[:, s, :, :], AX, ALU.add)

                def weigh(j, s, i):
                    k = s % 2
                    dve.wait_ge(s_rows[k], i * (16 * RING // 2) + 16 * (s // 2 + 1))
                    dve.wait_ge(s_p, j + 1)
                    if count:
                        kinds(dve, m, weighted[:, k, :, D + heads:W], j)
                    dve.tensor_tensor(weighted[:, k, :, 0:D].rearrange("p u (h c) -> p u h c", h=heads),
                                      rows[:, k, :, :].rearrange("p u (h c) -> p u h c", h=heads),
                                      weighted[:, k, :, D:D + heads].unsqueeze(3).broadcast_to([P, U, heads, D // heads]),
                                      ALU.mult)
                    dve.drain().then_inc(s_wr, 1)

                def add(j, k):
                    tiles = tiles_of_chunks(nc, m, ENG.DVE, j)
                    dve.wait_ge(s_sum, j + 1)
                    for u in range(U):
                        a = m.acc[:, bass.ds(tiles[u], 1), 0:W]
                        dve.tensor_tensor(a, a, m.ps_o[:, k, u // 2, (u % 2) * W:(u % 2 + 1) * W].unsqueeze(1), ALU.add)
                        dve.drain()
                    dve.sem_inc(s_acc, 1)

                def body(j, s, i):
                    if within(j + 2):
                        stage(j + 2, (s + 2) % RING)
                    weigh(j, s, i)
                    if within(j + 1):
                        differences(j + 1, (s + 1) % RING)
                    if began(j - 1):
                        add(j - 1, (s + 1) % 2)
                stage(0, 0)
                stage(1, 1)
                dve.drain()
                differences(0, 0)
                in_rounds(dve, NG, RING, body)
                add(NG - 1, 1)


def sum_pass(nc, sem, m, tag, table, indices, edge_weight=None):
    s_idx, s_oh, s_sum, s_acc = (sem(tag + n) for n in ("_indices", "_one_hot", "_summed", "_added"))
    s_gather, base = m.s_gather, list(m.gathered)
    with ExitStack() as ctx:
        def sb(name, shape, dt=F32):
            return ctx.enter_context(nc.sbuf_tensor(tag + name, shape, dt))

        idx, got, hot = sb("_idx", [P, RING, U], I32), sb("_got", [P, RING, U, D]), sb("_hot", [P, 2, U, P])
        with nc.Block() as block:
            @block.gpsimd
            def _(pool):
                def body(j, s, i):
                    apart(pool, s_idx, j + 1)
                    for u in range(U):
                        pool.indirect_dma_start(got[:, s, u, :], None, table, bass.IndirectOffsetOnAxis(
                            ap=idx[:, s, u:u + 1], axis=0)).then_inc(s_gather[s], 16)
                in_rounds(pool, NG, RING, body)

            @block.tensor
            def _(pe):
                def body(j, s, i):
                    k = s % 2
                    pe.wait_ge(s_oh, j + 1)
                    after(pe, s_acc, j - 1)
                    pe.wait_ge(s_gather[s], i * (16 * U) + (base[s] + 16 * U))
                    for u in range(U):
                        last = pe.matmul(m.ps_o[:, k, 0, u * D:(u + 1) * D], hot[:, k, u, :], got[:, s, u, :],
                                         start=True, stop=True)
                    last.then_inc(s_sum, 1)
                in_rounds(pe, NG, RING, body)

            @block.vector
            def _(dve):
                def stage_indices(j, s):
                    after(dve, s_sum, j - 3)
                    dve.tensor_copy(idx[:, s, :], indices[:, cols(j)]).then_inc(s_idx, 1)

                def stage_one_hot(j, k):
                    after(dve, s_sum, j - 1)
                    ins = one_hot(dve, m, hot[:, k, :, :], cols(j), U)
                    if edge_weight is not None:
                        dve.drain()
                        ins = dve.tensor_tensor(hot[:, k, :, :], hot[:, k, :, :],
                                                edge_weight[:, cols(j)].unsqueeze(2).broadcast_to([P, U, P]), ALU.mult)
                    ins.then_inc(s_oh, 1)

                def add(j, k):
                    tiles = tiles_of_chunks(nc, m, ENG.DVE, j)
                    dve.wait_ge(s_sum, j + 1)
                    for u in range(U):
                        a = m.acc[:, bass.ds(tiles[u], 1), 0:D]
                        dve.tensor_tensor(a, a, m.ps_o[:, k, 0, u * D:(u + 1) * D].unsqueeze(1), ALU.add)
                        dve.drain()
                    dve.sem_inc(s_acc, 1)

                def body(j, s, i):
                    if within(j + 3):
                        stage_indices(j + 3, (s + 3) % RING)
                    if within(j + 1):
                        stage_one_hot(j + 1, (s + 1) % 2)
                    add(j, s % 2)
                for j in range(3):
                    stage_indices(j, j)
                stage_one_hot(0, 0)
                in_rounds(dve, NG, RING, body)
    count_gathers(m)


def store_rows(nc, sem, m, tag, rows, dram):
    s = sem(tag + "_stored")
    with nc.Block() as block:
        @block.sync
        def _(sp):
            sp.dma_start(dram.rearrange("(t p) d -> p t d", p=P), rows).then_inc(s, 16)
            sp.wait_ge(s, 16)


def feed_forward(nc, sem, m, rows, out):
    B = 5
    s_in, s_tr, s_trc, s_h = sem("ff_staged"), sem("ff_turned"), sem("ff_turned_copied"), sem("ff_hidden")
    s_var, s_rstd, s_n, s_g = sem("ff_variance"), sem("ff_rstd"), sem("ff_normed"), sem("ff_gelu")
    s_gt, s_gtc, s_y, s_out = sem("ff_gelu_turned"), sem("ff_gelu_copied"), sem("ff_product"), sem("ff_out")
    C = FFN // P
    banks = [m.ps_o[:, 0, 0, :], m.ps_o[:, 0, 1, :], m.ps_o[:, 1, 0, :], m.ps_o[:, 1, 1, :], m.ps_k[:, 0, :]]
    with ExitStack() as ctx:
        def sb(name, shape):
            return ctx.enter_context(nc.sbuf_tensor("ff_" + name, shape, F32))

        x = sb("x", [P, B, D])
        hid = m.scratch[:, 0:B * FFN].rearrange("p (b f) -> p b f", b=B)
        hid_t = m.scratch[:, B * FFN:2 * B * FFN].rearrange("p (b c n) -> p b c n", b=B, c=C)
        x_t = sb("x_t", [P, B, P])
        stats, mean, var, rstd, diff = sb("stats", [P, B, 6]), *(sb(n, [P, B]) for n in ("mean", "var", "rstd", "diff"))
        with nc.Block() as block:
            @block.vector
            def _(dve):
                with dve.Fori(0, NT // B) as i:
                    dve.tensor_copy(x[:, :, :], rows[:, bass.ds(i * B, B), :])
                    dve.drain().then_inc(s_in, 1)
                    for b in range(B):
                        dve.wait_ge(s_h, i * B + (b + 1))
                        dve.tensor_tensor(hid[:, b, :], banks[b], m.b_f1[:, :], ALU.add)
                    dve.drain()
                    for b in range(B):
                        dve.bn_stats(stats[:, b, :], hid[:, b, :])
                    dve.drain()
                    dve.tensor_tensor(mean[:, :], stats[:, :, 1], stats[:, :, 4], ALU.add)
                    dve.tensor_tensor(diff[:, :], stats[:, :, 1], stats[:, :, 4], ALU.subtract)
                    dve.tensor_tensor(var[:, :], stats[:, :, 2], stats[:, :, 5], ALU.add)
                    dve.drain()
                    dve.tensor_scalar(mean[:, :], mean[:, :], 0.5, None, ALU.mult)
                    dve.tensor_tensor(diff[:, :], diff[:, :], diff[:, :], ALU.mult)
                    dve.tensor_scalar(var[:, :], var[:, :], 1.0 / FFN, None, ALU.mult)
                    dve.drain()
                    dve.scalar_tensor_tensor(var[:, :], diff[:, :], 0.25, var[:, :], ALU.mult, ALU.add)
                    dve.drain()
                    dve.tensor_scalar(var[:, :], var[:, :], EPS, None, ALU.add).then_inc(s_var, 1)
                    dve.wait_ge(s_rstd, i + 1)
                    for b in range(B):
                        dve.tensor_scalar(hid[:, b, :], hid[:, b, :], mean[:, b:b + 1], rstd[:, b:b + 1],
                                          ALU.subtract, ALU.mult)
                    dve.drain()
                    dve.tensor_tensor(hid, hid, m.g_lnf[:, :].unsqueeze(1).broadcast_to([P, B, FFN]), ALU.mult)
                    dve.drain()
                    dve.tensor_tensor(hid, hid, m.b_lnf[:, :].unsqueeze(1).broadcast_to([P, B, FFN]), ALU.add
                                      ).then_inc(s_n, 1)
                    dve.tensor_tensor(x[:, :, :], x[:, :, :], m.b_f2[:, :].unsqueeze(1).broadcast_to([P, B, D]), ALU.add)
                    dve.drain()
                    dve.wait_ge(s_y, i + 1)
                    dve.tensor_tensor(out[:, bass.ds(i * B, 4), :], x[:, 0:4, :],
                                      m.ps_t[:, 0, :].rearrange("p (b d) -> p b d", b=4), ALU.add)
                    dve.tensor_tensor(out[:, bass.ds(i * B + 4, 1), :], x[:, 4:5, :], m.ps_t[:, 1, 0:D].unsqueeze(1), ALU.add)
                    dve.drain()

            @block.gpsimd
            def _(pool):
                with pool.Fori(0, NT // B) as i:
                    apart(pool, s_var, i + 1)
                    pool.tensor_tensor(rstd[:, :], var[:, :], m.minus_half[:, 0:var.shape[1]], ALU.pow).then_inc(s_rstd, 1)

            @block.tensor
            def _(pe):
                with pe.Fori(0, NT // B) as i:
                    pe.wait_ge(s_in, i + 1)
                    for b in range(B):
                        mm = pe.transpose(m.ps_t[:, b // 4, (b % 4) * P:(b % 4 + 1) * P], x[:, b, :], m.ident[:, :])
                    mm.then_inc(s_tr, 1)
                    pe.wait_ge(s_trc, i * 2 + 2)
                    for b in range(B):
                        pe.matmul(banks[b], x_t[:, b, :], m.w_f1[:, :], start=True, stop=True).then_inc(s_h, 1)
                    for b in range(B):
                        pe.wait_ge(s_g, i * B + (b + 1))
                        for c in range(C):
                            mm = pe.transpose(banks[b][:, c * P:(c + 1) * P], hid[:, b, c * P:(c + 1) * P], m.ident[:, :])
                        mm.then_inc(s_gt, 1)
                    for b in range(B):
                        pe.wait_ge(s_gtc, i * B + (b + 1))
                        for c in range(C):
                            mm = pe.matmul(m.ps_t[:, b // 4, (b % 4) * D:(b % 4 + 1) * D], hid_t[:, b, c, :],
                                           m.w_f2[:, c, :], start=(c == 0), stop=(c == C - 1))
                    mm.then_inc(s_y, 1)

            @block.scalar
            def _(act):
                with act.Fori(0, NT // B) as i:
                    act.wait_ge(s_tr, i + 1)
                    act.copy(x_t[:, 0:4, :], m.ps_t[:, 0, :].rearrange("p (b n) -> p b n", b=4)).then_inc(s_trc, 1)
                    act.copy(x_t[:, 4, :], m.ps_t[:, 1, 0:P]).then_inc(s_trc, 1)
                    act.wait_ge(s_n, i + 1)
                    for b in range(B):
                        act.activation(hid[:, b, :], hid[:, b, :], ACT.Gelu).then_inc(s_g, 1)
                    for b in range(B):
                        act.wait_ge(s_gt, i * B + (b + 1))
                        act.copy(hid_t[:, b, :, :], banks[b].rearrange("p (c n) -> p c n", c=C)).then_inc(s_gtc, 1)


def attention_layer(nc, sem, m):
    def prepare(dve, staged, t):
        dve.tensor_copy(staged.unsqueeze(1), m.X[:, bass.ds(t, 1), :])

    def finish(dve, out, product, t):
        dve.tensor_tensor(out.unsqueeze(1), product, m.b_vqk[:, :].unsqueeze(1), ALU.add)
        dve.drain()
        dve.tensor_copy(m.own[:, bass.ds(t, 1), :], out[:, 2 * D:3 * D].unsqueeze(1))

    project(nc, sem, m, "vqk", prepare, m.w_vqk[:, :], 3 * D, finish, m.table_vq, 2 * D)
    score_pass(nc, sem, m, "a0", m.table_vq, 2 * D, H0, True)

    with nc.Block() as block:
        @block.vector
        def _(dve):
            dve.memset(m.top[:, :, :], -BIG)
            dve.memset(m.acc[:, :, :], 0.0)
    score_maximum(nc, sem, m, "m0", H0)
    value_pass(nc, sem, m, "v0", H0, count=True)

    s_deg = sem("degrees")
    with nc.Block() as block:
        @block.vector
        def _(dve):
            counts = m.acc[:, :, D + H0:D + H0 + NREL]
            dve.tensor_reduce(m.dinv[:, :], counts, AX, ALU.add)
            dve.drain()
            dve.tensor_scalar(m.dinv[:, :], m.dinv[:, :], 1.0, None, ALU.add).then_inc(s_deg, 1)
            den = m.acc[:, :, D:D + H0]
            dve.tensor_scalar(den, den, 1e-8, None, ALU.max)
            dve.tensor_scalar(counts, counts, 1.0, None, ALU.max)
            dve.drain()
            dve.reciprocal(den, den)
            dve.reciprocal(m.top[:, :, H0:2 * H0], counts)

        @block.gpsimd
        def _(pool):
            pool.wait_ge(s_deg, 1)
            pool.tensor_tensor(m.dinv[:, :], m.dinv[:, :], m.minus_half[:, :], ALU.pow)

    def normalised(dve, staged, t):
        dve.tensor_tensor(staged.rearrange("p (h c) -> p h c", h=H0),
                          m.acc[:, bass.ds(t, 1), 0:D].rearrange("p t (h c) -> p (t h) c", h=H0),
                          m.acc[:, bass.ds(t, 1), D:D + H0].rearrange("p t h -> p (t h)").unsqueeze(2)
                          .broadcast_to([P, H0, D // H0]), ALU.mult)

    def residual(dve, out, product, t):
        dve.tensor_tensor(out.unsqueeze(1), product, m.b_o[:, :].unsqueeze(1), ALU.add)
        dve.drain()
        dve.tensor_tensor(m.own[:, bass.ds(t, 1), :], out.unsqueeze(1), m.X[:, bass.ds(t, 1), :], ALU.add)

    project(nc, sem, m, "oproj", normalised, m.w_o[:, :], D, residual)
    layer_norm(nc, sem, m, "ln1", m.own[:, :, :], m.g_ln1[:, :], m.b_ln1[:, :])
    feed_forward(nc, sem, m, m.own, m.own)
    layer_norm(nc, sem, m, "ln2", m.own[:, :, :], m.g_ln2[:, :], m.b_ln2[:, :])
    layer_norm(nc, sem, m, "ln_l0", m.X[:, :, :], add=m.own[:, :, :])


def appnp_layer(nc, m):
    dinv = m.dinv[:, :].unsqueeze(2).broadcast_to([P, NT, D])
    h = m.acc[:, :, 0:D]
    with nc.Block() as block:
        @block.vector
        def _(dve):
            dve.tensor_tensor(m.own[:, :, :], m.X[:, :, :], dinv, ALU.mult)
            dve.memset(m.acc[:, :, :], 0.0)
    for hop in range(5):
        with semaphores(nc) as sem:
            store_rows(nc, sem, m, f"hop{hop}", m.own[:, :, :], m.table_h)
            sum_pass(nc, sem, m, f"p{hop}", m.table_h, m.src_idx)
        with nc.Block() as block:
            @block.vector
            def _(dve):
                dve.tensor_tensor(h, h, m.own[:, :, :], ALU.add)
                dve.drain()
                dve.tensor_tensor(h, h, dinv, ALU.mult)
                dve.drain()
                dve.tensor_scalar(h, h, 1.0 - 0.8, None, ALU.mult)
                dve.drain()
                dve.scalar_tensor_tensor(h, m.X[:, :, :], 0.8, h, ALU.mult, ALU.add)
                dve.drain()
                if hop < 4:
                    dve.tensor_tensor(m.own[:, :, :], h, dinv, ALU.mult)
                    dve.drain()
                    dve.memset(h, 0.0)
    with semaphores(nc) as sem:
        layer_norm(nc, sem, m, "ln_l1", m.X[:, :, :], add=h)


def gat_conv(nc, sem, m, tag, prepare, weight, a_src, a_dst, heads, pick):
    c = D // heads

    def finish(dve, out, product, t):
        dve.tensor_copy(out[:, 0:D].unsqueeze(1), product)
        dve.drain()
        dve.tensor_copy(m.own[:, bass.ds(t, 1), :], out[:, 0:D].unsqueeze(1))
        for a, to in ((a_src, m.a_s), (a_dst, m.a_d)):
            dve.tensor_tensor(m.tmp[:, :], out[:, 0:D], a[:, :], ALU.mult)
            dve.drain()
            dve.tensor_reduce(to[:, bass.ds(t, 1), 0:heads], m.tmp[:, :].rearrange("p (t h c) -> p t h c", t=1, h=heads),
                              AX, ALU.add)
            dve.drain()

    project(nc, sem, m, tag + "w", prepare, weight[:, :], D, finish)
    s_tab, s_exp, s_self = sem(tag + "_table"), sem(tag + "_self_exp"), sem(tag + "_self")
    with nc.Block() as block:
        @block.sync
        def _(sp):
            rows = m.table_g.rearrange("(t p) d -> p t d", p=P)
            sp.dma_start(rows[:, :, 0:D], m.own[:, :, :]).then_inc(s_tab, 16)
            sp.dma_start(rows[:, :, D:D + 4], m.a_s[:, :, :]).then_inc(s_tab, 16)
            sp.wait_ge(s_tab, 32)
    own_score = m.a_s[:, :, 0:heads]
    loop = m.has_loop[:, :].unsqueeze(2).broadcast_to([P, NT, heads])
    with nc.Block() as block:
        @block.vector
        def _(dve):
            top = m.top[:, :, 0:heads]
            dve.tensor_tensor(top, m.a_s[:, :, 0:heads], m.a_d[:, :, 0:heads], ALU.add)
            dve.drain()
            dve.scalar_tensor_tensor(own_score, top, 0.2, top, ALU.mult, ALU.max)
            dve.tensor_scalar(m.loop_off[:, :], m.has_loop[:, :], BIG, -BIG, ALU.mult, ALU.add)
            dve.drain()
            dve.tensor_tensor(top, own_score, loop, ALU.mult)
            dve.drain()
            dve.tensor_tensor(top, top, m.loop_off[:, :].unsqueeze(2).broadcast_to([P, NT, heads]), ALU.add)
    score_pass(nc, sem, m, tag + "s", m.table_g, D + 4, heads, False)
    score_maximum(nc, sem, m, tag + "m", heads)
    with nc.Block() as block:
        @block.vector
        def _(dve):
            den = m.acc[:, :, D:D + heads]
            dve.tensor_tensor(own_score, own_score, m.top[:, :, 0:heads], ALU.subtract)
            dve.drain()
            dve.tensor_scalar(own_score, own_score, 0.0, None, ALU.min)
            dve.drain().then_inc(s_self, 1)
            dve.wait_ge(s_exp, 1)
            dve.tensor_tensor(den, own_score, loop, ALU.mult)
            dve.drain()
            with dve.Fori(0, NT) as t:
                dve.tensor_tensor(m.acc[:, bass.ds(t, 1), 0:D].rearrange("p t (h c) -> p (t h) c", h=heads),
                                  m.own[:, bass.ds(t, 1), :].rearrange("p t (h c) -> p (t h) c", h=heads),
                                  m.acc[:, bass.ds(t, 1), D:D + heads].rearrange("p t h -> p (t h)").unsqueeze(2)
                                  .broadcast_to([P, heads, c]), ALU.mult)

        @block.scalar
        def _(act):
            act.wait_ge(s_self, 1)
            act.activation(own_score, own_score, ACT.Exp).then_inc(s_exp, 1)
    value_pass(nc, sem, m, tag + "v", heads, pick=pick)
    with nc.Block() as block:
        @block.vector
        def _(dve):
            den = m.acc[:, :, D:D + heads]
            dve.tensor_scalar(den, den, 1e-16, None, ALU.add)
            dve.drain()
            dve.reciprocal(den, den)


def gat_layer(nc, m):
    def prepare_x(dve, staged, t):
        dve.tensor_copy(staged.unsqueeze(1), m.X[:, bass.ds(t, 1), :])

    with semaphores(nc) as sem:
        gat_conv(nc, sem, m, "g1", prepare_x, m.w_g1, m.a_src1, m.a_dst1, 4, True)

    def finish_rows(heads, bias):
        def tile(dve, to, t):
            dve.tensor_tensor(to.rearrange("p (h c) -> p h c", h=heads),
                              m.acc[:, bass.ds(t, 1), 0:D].rearrange("p t (h c) -> p (t h) c", h=heads),
                              m.acc[:, bass.ds(t, 1), D:D + heads].rearrange("p t h -> p (t h)").unsqueeze(2)
                              .broadcast_to([P, heads, D // heads]), ALU.mult)
            dve.drain()
            dve.tensor_tensor(to, to, bias[:, :], ALU.add)
            dve.drain()
        return tile

    with semaphores(nc) as sem:
        s_m, s_e = sem("elu_min"), sem("elu_exp")
        first = finish_rows(4, m.b_g1)
        with nc.Block() as block:
            @block.vector
            def _(dve):
                with dve.Fori(0, NT) as t:
                    first(dve, m.tmp[:, :], t)
                    dve.tensor_copy(m.own[:, bass.ds(t, 1), :], m.tmp[:, :].unsqueeze(1))
                    dve.tensor_scalar(m.acc[:, bass.ds(t, 1), 0:D], m.tmp[:, :].unsqueeze(1), 0.0, None, ALU.min)
                    dve.drain()
                dve.drain().then_inc(s_m, 1)
                dve.wait_ge(s_e, 1)
                dve.scalar_tensor_tensor(m.own[:, :, :], m.acc[:, :, 0:D], -1.0, m.own[:, :, :], ALU.add, ALU.max)

            @block.scalar
            def _(act):
                act.wait_ge(s_m, 1)
                act.activation(m.acc[:, :, 0:D], m.acc[:, :, 0:D], ACT.Exp).then_inc(s_e, 1)

    def prepare_h(dve, staged, t):
        dve.tensor_copy(staged.unsqueeze(1), m.own[:, bass.ds(t, 1), :])

    with semaphores(nc) as sem:
        gat_conv(nc, sem, m, "g2", prepare_h, m.w_g2, m.a_src2, m.a_dst2, 1, False)
    second = finish_rows(1, m.b_g2)
    with nc.Block() as block:
        @block.vector
        def _(dve):
            with dve.Fori(0, NT) as t:
                second(dve, m.tmp[:, :], t)
                dve.tensor_tensor(m.X[:, bass.ds(t, 1), :], m.X[:, bass.ds(t, 1), :], m.tmp[:, :].unsqueeze(1), ALU.add)
                dve.drain()
    with semaphores(nc) as sem:
        layer_norm(nc, sem, m, "ln_l2", m.X[:, :, :])


def relational_layer(nc, sem, m):
    def prepare(dve, staged, t):
        dve.tensor_copy(staged.unsqueeze(1), m.X[:, bass.ds(t, 1), :])

    def per_relation(dve, out, product, t):
        dve.tensor_copy(out.rearrange("p (b n) -> p b n", b=2), product)

    def root(dve, out, product, t):
        dve.tensor_tensor(m.acc[:, bass.ds(t, 1), 0:D], product, m.b_rel[:, :].unsqueeze(1), ALU.add)

    project(nc, sem, m, "rel", prepare, m.w_rel[:, 0:NREL, :].rearrange("k r n -> k (r n)"), NREL * D, per_relation,
            m.table_r.rearrange("(n r) d -> n (r d)", r=NREL), NREL * D)
    project(nc, sem, m, "root", prepare, m.w_rel[:, NREL, :], D, root)
    sum_pass(nc, sem, m, "r", m.table_r, m.rel_idx, m.rel_w)
    layer_norm(nc, sem, m, "ln_l3", m.X[:, :, :], add=m.acc[:, :, 0:D])


def store_output(nc, sem, m, out):
    s_out = sem("output_stored")
    with nc.Block() as block:
        @block.sync
        def _(sp):
            sp.dma_start(out[0:FULL * P, :].rearrange("(t p) d -> p t d", p=P), m.X[:, 0:FULL, :]).then_inc(s_out, 16)
            sp.dma_start(out[FULL * P:N, :], m.X[0:TAIL, FULL, :]).then_inc(s_out, 16)
            sp.wait_ge(s_out, 32)


def build(nc, A, out, stages=4):
    with ExitStack() as ctx:
        m = allocate(nc, ctx)
        m.s_gather = [ctx.enter_context(nc.semaphore(f"gathered{k}")) for k in range(RING)]
        m.gathered = [0] * RING
        with semaphores(nc) as sem:
            load_constants(nc, m, A, sem)
            build_records(nc, m, A, sem)
            plan_chunks(nc, m, A, sem)
        with semaphores(nc) as sem:
            attention_layer(nc, sem, m)
        if stages > 1:
            appnp_layer(nc, m)
        if stages > 2:
            gat_layer(nc, m)
        if stages > 3:
            with semaphores(nc) as sem:
                relational_layer(nc, sem, m)
        with semaphores(nc) as sem:
            store_output(nc, sem, m, out)


_INS = ['x', 'src', 'dst', 'edge_attr_32', 'edge_type_8', 'L0_gnn_qW', 'L0_gnn_qb', 'L0_gnn_kW', 'L0_gnn_kb',
        'L0_gnn_vW', 'L0_gnn_vb', 'L0_gnn_eW', 'L0_gnn_eb', 'L0_gnn_oW', 'L0_gnn_ob', 'L0_gnn_ln1_g',
        'L0_gnn_ln1_b', 'L0_gnn_f1W', 'L0_gnn_f1b', 'L0_gnn_lnf_g', 'L0_gnn_lnf_b', 'L0_gnn_f2W', 'L0_gnn_f2b',
        'L0_gnn_ln2_g', 'L0_gnn_ln2_b', 'L2_gnn_W1', 'L2_gnn_a_src1', 'L2_gnn_a_dst1', 'L2_gnn_b1', 'L2_gnn_W2',
        'L2_gnn_a_src2', 'L2_gnn_a_dst2', 'L2_gnn_b2', 'L3_gnn_weight', 'L3_gnn_root', 'L3_gnn_bias']
_OUTS = [((N, D), 'float32')]


def kernel(**inputs):
    import numpy as _np
    import concourse.bacc as _bacc
    from concourse import mybir as _mybir
    from concourse.bass_utils import run_bass_kernel_spmd as _run

    nc = _bacc.Bacc("TRN2", target_bir_lowering=False, num_devices=1)
    arrays, args = {}, {}
    for name in _INS:
        a = _np.ascontiguousarray(inputs[name])
        arrays[f"in_{name}_dram"] = a
        args[name] = nc.dram_tensor(f"in_{name}_dram", a.shape, _mybir.dt.from_np(a.dtype), kind="ExternalInput").ap()
    outs = []
    for i, (shape, dtype) in enumerate(_OUTS):
        dt = _mybir.dt.from_np(_np.dtype(dtype))
        outs.append(nc.dram_tensor(f"out_{i}_dram", shape, dt, kind="ExternalOutput").ap())
    build(nc, args, outs[0])
    r = _run(nc, [arrays], core_ids=[0])
    got = tuple(r.results[0][f"out_{i}_dram"] for i in range(len(_OUTS)))
    return got[0]
```

```python
from contextlib import ExitStack, contextmanager

import concourse.bass as bass
from concourse import mybir
from concourse.alu_op_type import AluOpType as ALU

ACT = mybir.ActivationFunctionType
AX = mybir.AxisListType.X
F32 = mybir.dt.float32
BF16 = mybir.dt.bfloat16
I32 = mybir.dt.int32
ENG = mybir.EngineType

P = 128
N, E, D, FFN, EDIM, NREL = 6250, 100000, 128, 512, 32, 8
H0 = 8
SELF_LOOPS = 3750
FULL, TAIL = N // P, N % P
TILES = FULL + 1
NT = TILES + TILES % 2
NP = NT * P
U = 4
NCH = -(-((E + TILES * (P - 1)) // P) // (2 * U)) * (2 * U)
NG = NCH // U
RING = 4
EP, EC = 125, E // 125
RECW = 12
R_SRC, R_DST, R_TYP, R_NEXT, R_BIAS = 0, 1, 2, 3, 4
ROUND = 16
BIG = 1.0e30
EPS = 1e-5


class Core:
    pass


def after(eng, sem, value):
    if isinstance(value, int) and value <= 0:
        return
    eng.wait_ge(sem, value)


def apart(eng, sem, value):
    if isinstance(value, int) and value <= 0:
        return
    eng.wait_ge(sem, value)
    eng.nop(nofuse=True)


def in_pairs(eng, n, body):
    body(0, 0, 0)
    body(1, 1, 0)
    with eng.Fori(1, n // 2) as i:
        body(i * 2, 0, i)
        body(i * 2 + 1, 1, i)


def in_rounds(eng, n, ring, body):
    for s in range(ring):
        body(s, s, 0)
    with eng.Fori(1, n // ring - 1) as i:
        for s in range(ring):
            body(i * ring + s, s, i)
    for s in range(ring):
        body(n - ring + s, s, n // ring - 1)


def within(step, n=NG):
    return not isinstance(step, int) or step < n


def began(step):
    return not isinstance(step, int) or step >= 0


def count_gathers(m):
    m.gathered = [g + 16 * U * (NG // RING) for g in m.gathered]


def gathers_done(base, s8, i):
    return i * (32 * U) + (base + 16 * U * (s8 // RING + 1))


def one_hot(dve, m, to, chunks, n):
    return dve.tensor_tensor(to, m.node_ramp[:, :].unsqueeze(1).broadcast_to([P, n, P]),
                             m.dst_slot[:, chunks].unsqueeze(2).broadcast_to([P, n, P]), ALU.is_equal)


def one_hot_act(act, m, to, j):
    for u in range(U):
        act.activation(to[:, u, :], m.node_ramp[:, :], ACT.Abs, bias=m.dst_slot[:, bass.ds(j * U + u, 1)], scale=-1.0)
    act.drain()
    return act.activation(to, to, ACT.Relu, bias=m.ones[:, 0:1], scale=-1.0)


def kinds(dve, m, to, j):
    return dve.tensor_tensor(to, m.node_ramp[:, 0:NREL].unsqueeze(1).broadcast_to([P, U, NREL]),
                             m.etype[:, cols(j)].unsqueeze(2).broadcast_to([P, U, NREL]), ALU.is_equal)


def tiles_of_chunks(nc, m, engine, j):
    return tiles_at(nc, m, engine, cols(j))


def tiles_at(nc, m, engine, chunks):
    _, tiles = nc.values_load_multi_w_load_instructions(
        m.chunk_tile[0:1, chunks], engines=[engine], min_val=0, max_val=TILES - 1,
        skip_runtime_bounds_check_because="plan_chunks clamps the table")
    return tiles


def cols(j, n=U):
    return bass.ds(j * n, n)


@contextmanager
def semaphores(nc):
    with ExitStack() as ctx:
        handles = []

        def sem(name):
            handles.append(ctx.enter_context(nc.semaphore(name)))
            return handles[-1]

        yield sem
        with nc.Block() as block:
            @block.gpsimd
            def _(pool):
                for handle in handles:
                    pool.sem_clear(handle)


def load_constants(nc, m, A, sem):
    s_w, s_z, s_id = sem("weights_loaded"), sem("constants_zeroed"), sem("constants_made")
    s_i, s_row = sem("iota_done"), sem("rows_loaded")
    with nc.Block() as block:
        @block.sync
        def _(sp):
            n = 0

            def load(dst, src):
                nonlocal n
                sp.dma_start(dst, src).then_inc(s_w, 16)
                n += 16

            sp.wait_ge(s_z, 3)
            load(m.X[:, 0:FULL, :], A["x"][0:FULL * P, :].rearrange("(t p) d -> p t d", p=P))
            load(m.X[0:TAIL, FULL, :], A["x"][FULL * P:N, :])
            for e in range(P // EDIM):
                load(m.edge_w[e * EDIM:(e + 1) * EDIM, e * H0:(e + 1) * H0], A["L0_gnn_eW"])
            load(m.w_vqk[:, 0:D], A["L0_gnn_vW"])
            load(m.w_vqk[:, D:2 * D], A["L0_gnn_qW"])
            load(m.w_vqk[:, 2 * D:3 * D], A["L0_gnn_kW"])
            load(m.w_o[:, :], A["L0_gnn_oW"])
            load(m.w_f1[:, :], A["L0_gnn_f1W"])
            load(m.w_f2[:, :, :], A["L0_gnn_f2W"].rearrange("(c k) n -> k c n", k=P))
            load(m.w_g1[:, :], A["L2_gnn_W1"])
            load(m.w_g2[:, :], A["L2_gnn_W2"])
            load(m.w_rel[:, 0:NREL, :], A["L3_gnn_weight"].rearrange("r k n -> k r n"))
            load(m.w_rel[:, NREL, :], A["L3_gnn_root"])
            sp.wait_ge(s_w, n)

        @block.scalar
        def _(act):
            rows = [(m.b_vqk[:, 0:D], A["L0_gnn_vb"]), (m.b_vqk[:, D:2 * D], A["L0_gnn_qb"]),
                    (m.b_vqk[:, 2 * D:3 * D], A["L0_gnn_kb"]), (m.b_edge[:, :], A["L0_gnn_eb"]),
                    (m.b_o[:, :], A["L0_gnn_ob"]), (m.g_ln1[:, :], A["L0_gnn_ln1_g"]),
                    (m.b_ln1[:, :], A["L0_gnn_ln1_b"]), (m.b_f1[:, :], A["L0_gnn_f1b"]),
                    (m.b_f2[:, :], A["L0_gnn_f2b"]), (m.g_ln2[:, :], A["L0_gnn_ln2_g"]),
                    (m.b_ln2[:, :], A["L0_gnn_ln2_b"]), (m.b_g1[:, :], A["L2_gnn_b1"]),
                    (m.b_g2[:, :], A["L2_gnn_b2"]), (m.b_rel[:, :], A["L3_gnn_bias"]),
                    (m.a_src1[:, :], A["L2_gnn_a_src1"].rearrange("h c -> (h c)")),
                    (m.a_dst1[:, :], A["L2_gnn_a_dst1"].rearrange("h c -> (h c)")),
                    (m.a_src2[:, :], A["L2_gnn_a_src2"].rearrange("h c -> (h c)")),
                    (m.a_dst2[:, :], A["L2_gnn_a_dst2"].rearrange("h c -> (h c)"))]
            for dst, src in rows:
                act.dma_start(dst, src.partition_broadcast(P)).then_inc(s_row, 16)
            for dst, src in ((m.g_lnf, A["L0_gnn_lnf_g"]), (m.b_lnf, A["L0_gnn_lnf_b"])):
                act.dma_start(dst[:, :], src.rearrange("(c p) -> p c", p=P), allow_slow_non_contiguous=True
                              ).then_inc(s_row, 16)
            act.wait_ge(s_row, 16 * (len(rows) + 2))

        @block.vector
        def _(dve):
            dve.memset(m.X[:, :, :], 0.0).then_inc(s_z, 1)
            dve.memset(m.edge_w[:, :], 0.0).then_inc(s_z, 1)
            dve.memset(m.ident[:, :], 0.0).then_inc(s_z, 1)
            dve.memset(m.ones[:, :], 1.0).then_inc(s_z, 1)
            dve.memset(m.minus_half[:, :], -0.5)
            dve.wait_ge(s_i, 3)
            dve.tensor_copy(m.node_ramp[:, :], m.node_ramp_i[:, :]).then_inc(s_id, 1)
            dve.tensor_copy(m.node_id[:, :], m.node_i[:, :]).then_inc(s_id, 1)
            dve.tensor_copy(m.slot[:, :], m.slot_i[:, :]).then_inc(s_id, 1)
            dve.wait_ge(s_id, 5)
            dve.tensor_scalar(m.has_loop[:, :], m.node_id[:, :], float(SELF_LOOPS), None,
                              ALU.is_lt).then_inc(s_id, 1)

        @block.gpsimd
        def _(pool):
            pool.iota(m.node_ramp_i[:, :], [[1, P]], base=0, channel_multiplier=0).then_inc(s_i, 1)
            pool.iota(m.node_i[:, :], [[P, NT]], base=0, channel_multiplier=1).then_inc(s_i, 1)
            pool.iota(m.slot_i[:, :], [[0, 1]], base=0, channel_multiplier=1).then_inc(s_i, 1)
            pool.wait_ge(s_z, 4)
            pool.affine_select(out=m.ident[:, :], in_=m.ident[:, :], compare_op=ALU.not_equal, fill=1.0,
                               base=0, pattern=[[-1, P]], channel_multiplier=1).then_inc(s_id, 1)
            pool.affine_select(out=m.upto[:, :], in_=m.ones[:, 0:TILES], compare_op=ALU.is_ge, fill=0.0,
                               base=0, pattern=[[1, TILES]], channel_multiplier=-1).then_inc(s_id, 1)


def build_records(nc, m, A, sem):
    s_e, s_nextz = sem("edge_lists_loaded"), sem("next_dst_cleared")
    s_attr = [sem(f"attr_loaded{k}") for k in range(2)]
    s_rec_out = m.s_gather
    s_tr, s_trc, s_bias, s_rec = sem("attr_turned"), sem("attr_turned_copied"), sem("bias_made"), sem("record_made")
    s_pad, s_padout, s_cnt = sem("pad_made"), sem("pad_stored"), sem("edges_counted")
    s_ends = sem("tile_ends_made")
    rounds = EC // ROUND
    with ExitStack() as ctx:
        def sb(name, shape, dt=F32):
            return ctx.enter_context(nc.sbuf_tensor(name, shape, dt))

        room = m.scratch[0:EP, :]
        src_i, dst_i, typ_i, next_i = (room[:, k * EC:(k + 1) * EC].bitcast(I32) for k in range(4))
        dst_f, below = (room[:, k * EC:(k + 1) * EC] for k in (4, 5))
        assert rounds >= TILES
        edges_below = sb("edges_below", [EP, rounds + 1])
        tile_end_i, tile_end = sb("tile_end_i", [EP, rounds], I32), sb("tile_end", [EP, rounds])
        attr = sb("attr", [EP, 2, ROUND * EDIM])
        attr_t = sb("attr_t", [P, 2, 4, P])
        rec = sb("rec", [EP, 2, ROUND, RECW])
        pad = sb("pad", [P, RECW])
        rec_i = rec[:, :, :, :].bitcast(I32)
        attr_d = A["edge_attr_32"].rearrange("(p i) k -> p (i k)", p=EP)
        rec_d = m.rec_dram[0:E, :].rearrange("(p i) w -> p i w", p=EP)

        with nc.Block() as block:
            @block.sync
            def _(sp):
                flat = lambda a: a.rearrange("(p i) -> p i", p=EP)
                sp.dma_start(dst_i[:, :], flat(A["dst"])).then_inc(s_e, 16)
                sp.dma_start(src_i[:, :], flat(A["src"])).then_inc(s_e, 16)
                sp.dma_start(typ_i[:, :], flat(A["edge_type_8"])).then_inc(s_e, 16)
                sp.wait_ge(s_nextz, 1)
                sp.dma_start(next_i[0:EP - 1, :], A["dst"][1:1 + (EP - 1) * EC].rearrange(
                    "(p i) -> p i", i=EC)).then_inc(s_e, 16)
                sp.dma_start(next_i[EP - 1:EP, 0:EC - 1], A["dst"][1 + (EP - 1) * EC:E].rearrange(
                    "(a i) -> a i", a=1)).then_inc(s_e, 16)

                def load(r, k, i):
                    after(sp, s_tr, r - 1)
                    sp.dma_start(attr[:, k, :], attr_d[:, bass.ds(r * (ROUND * EDIM), ROUND * EDIM)]
                                 ).then_inc(s_attr[k], 16)
                in_pairs(sp, rounds, load)
                sp.wait_ge(s_pad, 2)
                sp.dma_start(m.rec_dram[E:E + P, :], pad[:, :]).then_inc(s_padout, 16)
                sp.wait_ge(s_padout, 16)

            @block.tensor
            def _(pe):
                def turn(r, k, i):
                    pe.wait_ge(s_attr[k], i * 16 + 16)
                    for q in range(4):
                        last = pe.transpose(m.ps_t[:, k, q * P:q * P + EP], attr[:, k, q * P:(q + 1) * P],
                                            m.ident[0:EP, 0:EP])
                    last.then_inc(s_tr, 1)
                    pe.wait_ge(s_trc, r + 1)
                    after(pe, s_rec, r - 1)
                    for q in range(4):
                        last = pe.matmul(m.ps_k[0:EP, k, q * EDIM:(q + 1) * EDIM], attr_t[:, k, q, 0:EP],
                                         m.edge_w[:, :], start=True, stop=True)
                    last.then_inc(s_bias, 1)
                in_pairs(pe, rounds, turn)

            @block.scalar
            def _(act):
                def copy(r, k, i):
                    after(act, s_bias, r - 1)
                    act.wait_ge(s_tr, r + 1)
                    act.copy(attr_t[:, k, :, 0:EP], m.ps_t[:, k, :].rearrange("p (q e) -> p q e", q=4)[:, :, 0:EP]
                             ).then_inc(s_trc, 1)
                in_pairs(act, rounds, copy)

            @block.vector
            def _(dve):
                dve.memset(next_i[:, :], -1).then_inc(s_nextz, 1)
                dve.memset(pad[:, :], 0.0).then_inc(s_pad, 1)
                dve.wait_ge(s_pad, 1)
                dve.memset(pad[:, R_DST:R_DST + 1], 1.0e7).then_inc(s_pad, 1)
                dve.wait_ge(s_e, 16 * 5)
                dve.tensor_copy(dst_f[:, :], dst_i[:, :]).then_inc(s_cnt, 1)
                dve.memset(edges_below[:, 0:1], 0.0).then_inc(s_cnt, 1)
                dve.wait_ge(s_cnt, 2)
                dve.wait_ge(s_ends, 1)
                dve.tensor_copy(tile_end[:, :], tile_end_i[:, :])
                dve.drain()

                def record(r, k, i):
                    dve.drain()
                    dve.tensor_scalar(below[:, :], dst_f[:, :], tile_end[:, bass.ds(r, 1)], None, ALU.is_lt)
                    after(dve, s_rec_out[k], i * 16)
                    dve.wait_ge(s_bias, r + 1)
                    at = bass.ds(r * ROUND, ROUND)
                    dve.tensor_copy(rec_i[:, k, :, R_SRC], src_i[:, at])
                    dve.tensor_copy(rec[:, k, :, R_DST], dst_i[:, at])
                    dve.tensor_copy(rec[:, k, :, R_TYP], typ_i[:, at])
                    dve.tensor_copy(rec[:, k, :, R_NEXT], next_i[:, at])
                    dve.drain()
                    dve.tensor_reduce(edges_below[:, bass.ds(r + 1, 1)], below[:, :], AX, ALU.add)
                    dve.tensor_tensor(rec[:, k, :, R_BIAS:R_BIAS + H0],
                                      m.ps_k[0:EP, k, 0:4 * EDIM].rearrange("p (e h) -> p e h", h=H0),
                                      m.b_edge[0:EP, :].unsqueeze(1).broadcast_to([EP, ROUND, H0]),
                                      ALU.add).then_inc(s_rec, 1)
                in_pairs(dve, rounds, record)
                dve.drain()
                dve.tensor_tensor(m.tile_edges[:, :], edges_below[:, 1:TILES + 1], edges_below[:, 0:TILES],
                                  ALU.subtract)

            @block.gpsimd
            def _(pool):
                pool.iota(tile_end_i[:, :], [[P, rounds]], base=P, channel_multiplier=0).then_inc(s_ends, 1)

                def store(r, k, i):
                    apart(pool, s_rec, r + 1)
                    pool.dma_start(rec_d[:, bass.ds(r * ROUND, ROUND), :], rec[:, k, :, :]).then_inc(s_rec_out[k], 16)
                in_pairs(pool, rounds, store)
                for k in range(2):
                    pool.wait_ge(s_rec_out[k], 16 * (rounds // 2))
    for k in range(2):
        m.gathered[k] += 16 * (rounds // 2)


def plan_chunks(nc, m, A, sem, meanwhile):
    s_pe, s_v, s_r = sem("plan_products"), sem("plan_steps"), [sem("records_in_sp"), sem("records_in_act")]
    by_pool = NCH * 11 // 26 // (2 * U) * (2 * U)
    by_other = (NCH - by_pool) // 2
    assert by_other % U == 0
    s_ramp, s_col = sem("chunk_ramp_made"), sem("columns_made")
    half = NCH // 2
    with ExitStack() as ctx:
        def sb(name, shape, dt=F32):
            return ctx.enter_context(nc.sbuf_tensor(name, shape, dt))

        cnt, cnt_i, nch = sb("cnt", [TILES, 1]), sb("cnt_i", [TILES, 1], I32), sb("nch", [TILES, 1])
        slack, last = sb("slack", [TILES, 1]), sb("last_chunk", [TILES, 1])
        past, first = sb("past", [TILES, NCH]), sb("first_edge", [1, NCH])
        first_i = sb("first_edge_i", [1, NCH], I32)
        tile_f = sb("tile_f", [P, NCH])
        ramp = sb("chunk_ramp", [TILES, NCH])
        with nc.Block() as block:
            @block.tensor
            def _(pe):
                pe.matmul(m.ps_t[0:TILES, 0, 0:1], m.tile_edges[:, :], m.ones[0:EP, 0:1], start=True, stop=True
                          ).then_inc(s_pe, 1)
                pe.wait_ge(s_v, 6)
                pe.matmul(m.ps_k[0:TILES, 0, 0:1], m.upto[0:TILES, :], nch[:, :], start=True, stop=True
                          ).then_inc(s_pe, 1)
                pe.wait_ge(s_v, 9)
                for h in range(2):
                    part = past[:, h * half:(h + 1) * half]
                    pe.matmul(m.ps_o[:, 0, h, 0:half], m.ones[0:TILES, :], part, start=True, stop=True)
                    pe.matmul(m.ps_o[0:1, 1, h, 0:half], slack[:, :], part, start=True, stop=True
                              ).then_inc(s_pe, 1)

            @block.vector
            def _(dve):
                n = 0

                def step(ins):
                    nonlocal n
                    n += 1
                    ins.then_inc(s_v, 1)
                    dve.wait_ge(s_v, n)

                dve.wait_ge(s_ramp, 1)
                step(dve.tensor_copy(ramp[:, :], m.dst_slot[0:TILES, 0:NCH].bitcast(I32)))
                dve.wait_ge(s_pe, 1)
                step(dve.tensor_copy(cnt[:, :], m.ps_t[0:TILES, 0, 0:1]))
                step(dve.tensor_scalar(cnt_i[:, :], cnt[:, :], float(P - 1), None, ALU.add))
                step(dve.tensor_scalar(cnt_i[:, :], cnt_i[:, :], 7, None, ALU.arith_shift_right))
                step(dve.tensor_copy(nch[:, :], cnt_i[:, :]))
                step(dve.scalar_tensor_tensor(slack[:, :], nch[:, :], -float(P), cnt[:, :], ALU.mult, ALU.add))
                dve.wait_ge(s_pe, 2)
                step(dve.tensor_copy(last[:, :], m.ps_k[0:TILES, 0, 0:1]))
                step(dve.tensor_scalar(past[:, :], ramp[:, :], last[:, 0:1], None, ALU.is_ge))
                step(dve.memset(m.dst_slot[:, :], -1.0))
                dve.wait_ge(s_pe, 4)
                step(dve.tensor_scalar(tile_f[:, :].rearrange("p (h c) -> p h c", h=2), m.ps_o[:, 0, :, 0:half],
                                       float(TILES - 1), None, ALU.min))
                step(dve.memset(m.chunk_tile[:, :], 0))
                step(dve.tensor_copy(m.chunk_tile[0:1, 0:NCH], tile_f[0:1, :]))
                step(dve.scalar_tensor_tensor(first[:, :].rearrange("p (h c) -> p h c", h=2),
                                              ramp[0:1, :].rearrange("p (h c) -> p h c", h=2), float(P),
                                              m.ps_o[0:1, 1, :, 0:half], ALU.mult, ALU.add))
                step(dve.tensor_scalar(first_i[:, :], first[:, :], float(E), None, ALU.min))

            @block.gpsimd
            def _(pool):
                pool.iota(m.dst_slot[0:TILES, 0:NCH].bitcast(I32), [[1, NCH]], base=0, channel_multiplier=0
                          ).then_inc(s_ramp, 1)

        def load(eng, engine, start, count, s, base=0):
            with eng.Fori(0, count // U) as i:
                _, at = nc.values_load_multi_w_load_instructions(
                    first_i[0:1, bass.ds(i * U + start, U)], engines=[engine], min_val=0, max_val=E,
                    skip_runtime_bounds_check_because="first_i is clamped where it is made")
                for u in range(U):
                    eng.dma_start(m.R[:, bass.ds(i * U + (start + u), 1), :],
                                  m.rec_dram[bass.ds(at[u], P), :].unsqueeze(1)).then_inc(s, 16)
            eng.wait_ge(s, base + 16 * count)

        pool_base = m.gathered[0]
        m.gathered[0] += 16 * by_pool
        meanwhile({
            "sync": lambda sp: load(sp, ENG.SP, by_pool, by_other, s_r[0]),
            "scalar": lambda act: load(act, ENG.Activation, by_pool + by_other, by_other, s_r[1]),
            "gpsimd": lambda pool: load(pool, ENG.Pool, 0, by_pool, m.s_gather[0], pool_base)})
        with nc.Block() as block:
            @block.vector
            def _(dve):
                n = 0

                def step(ins):
                    nonlocal n
                    n += 1
                    ins.then_inc(s_col, 1)
                    dve.wait_ge(s_col, n)

                step(dve.tensor_scalar(tile_f[:, :], tile_f[:, :], -float(P), None, ALU.mult))
                step(dve.tensor_tensor(m.dst_slot[:, 0:NCH], m.R[:, :, R_DST], tile_f[:, :], ALU.add))
                step(dve.memset(m.etype[:, :], 0.0))
                step(dve.memset(m.src_idx[:, :], 0))
                step(dve.memset(m.rel_idx[:, :], 0))
                step(dve.memset(m.rel_w[:, :], 0.0))
                step(dve.tensor_copy(m.etype[:, 0:NCH], m.R[:, :, R_TYP]))
                step(dve.tensor_copy(m.src_idx[:, 0:NCH], m.R[:, :, R_SRC].bitcast(I32)))
                step(dve.scalar_tensor_tensor(m.rel_idx[:, 0:NCH], m.src_idx[:, 0:NCH], float(NREL),
                                              m.etype[:, 0:NCH], ALU.mult, ALU.add))
                step(dve.tensor_tensor(m.is_last[:, :], m.R[:, :, R_DST], m.R[:, :, R_NEXT], ALU.not_equal))
                step(dve.tensor_scalar(m.at_end[:, :], m.slot[:, :], float(P - 1), None, ALU.is_equal))
                step(dve.tensor_scalar(m.is_last[:, :], m.is_last[:, :], m.at_end[:, 0:1], None, ALU.max))


def allocate(nc, ctx):
    def sb(name, shape, dt=F32):
        return ctx.enter_context(nc.sbuf_tensor(name, shape, dt))

    m = Core()
    m.ident, m.ones, m.upto = sb("ident", [P, P]), sb("ones", [P, P]), sb("upto", [P, TILES])
    m.node_i, m.node_id, m.has_loop = sb("node_i", [P, NT], I32), sb("node_id", [P, NT]), sb("has_loop", [P, NT])
    m.slot_i, m.slot, m.at_end = sb("slot_i", [P, 1], I32), sb("slot", [P, 1]), sb("at_end", [P, 1])
    m.edge_w = sb("edge_w", [P, EDIM])
    m.w_vqk, m.b_vqk = sb("w_vqk", [P, 3 * D]), sb("b_vqk", [P, 3 * D])
    m.b_edge = sb("b_edge", [P, H0])
    m.w_o, m.w_f1, m.w_f2 = sb("w_o", [P, D]), sb("w_f1", [P, FFN]), sb("w_f2", [P, FFN // P, D])
    m.w_g1, m.w_g2, m.w_rel = sb("w_g1", [P, D]), sb("w_g2", [P, D]), sb("w_rel", [P, NREL + 1, D])
    m.b_o, m.g_ln1, m.b_ln1, m.b_f2 = sb("b_o", [P, D]), sb("g_ln1", [P, D]), sb("b_ln1", [P, D]), sb("b_f2", [P, D])
    m.g_ln2, m.b_ln2, m.b_g1, m.b_g2 = sb("g_ln2", [P, D]), sb("b_ln2", [P, D]), sb("b_g1", [P, D]), sb("b_g2", [P, D])
    m.b_rel, m.a_src1, m.a_dst1 = sb("b_rel", [P, D]), sb("a_src1", [P, D]), sb("a_dst1", [P, D])
    m.a_src2, m.a_dst2 = sb("a_src2", [P, D]), sb("a_dst2", [P, D])
    m.b_f1, m.g_lnf, m.b_lnf = sb("b_f1", [P, FFN]), sb("g_lnf", [P, FFN // P]), sb("b_lnf", [P, FFN // P])
    m.X = sb("X", [P, NT, D])
    m.sums_odd = sb("own", [P, NT, D + H0 + NREL])
    m.own = m.sums_odd[:, :, 0:D]
    m.acc = sb("acc", [P, NT, D + H0 + NREL])
    m.R = sb("R", [P, NCH, RECW])
    m.top = sb("top", [P, NT, 2 * H0])
    m.dinv = sb("dinv", [P, NT])
    m.a_s, m.a_d, m.own_score = sb("a_s", [P, NT, 4]), sb("a_d", [P, NT, 4]), sb("own_score", [P, NT, 4])
    m.tile_edges = sb("tile_edges", [EP, TILES])
    m.dst_slot, m.etype, m.rel_w = sb("dst_slot", [P, NCH]), sb("etype", [P, NCH]), sb("rel_w", [P, NCH])
    m.src_idx, m.rel_idx = sb("src_idx", [P, NCH], I32), sb("rel_idx", [P, NCH], I32)
    m.is_last = sb("is_last", [P, NCH])
    m.chunk_tile = sb("chunk_tile", [1, NCH], I32)
    m.node_ramp_i, m.node_ramp = sb("node_ramp_i", [P, P], I32), sb("node_ramp", [P, P])
    m.minus_half = sb("minus_half", [P, NT])
    m.tmp = sb("tmp", [P, D])
    m.loop_off, m.dinv_part = sb("loop_off", [P, NT]), sb("dinv_part", [P, NT])
    m.ps_t = ctx.enter_context(nc.psum_tensor("ps_t", [P, 2, 512], F32))
    m.ps_k = ctx.enter_context(nc.psum_tensor("ps_k", [P, 2, 512], F32))
    m.ps_o = ctx.enter_context(nc.psum_tensor("ps_o", [P, 2, 2, 512], F32))
    m.scratch = m.acc[:, :, :].rearrange("p t w -> p (t w)")
    m.table_vq = nc.dram_tensor("table_vq", (NP, 2 * D), F32).ap()
    m.table_h = nc.dram_tensor("table_h", (NP, D), F32).ap()
    m.table_g = nc.dram_tensor("table_g", (NP, D + 4), F32).ap()
    m.table_r = nc.dram_tensor("table_r", (NP * NREL, D), F32).ap()
    m.rows_dram = nc.dram_tensor("rows_dram", (P, NCH, D), F32).ap()
    m.rec_dram = nc.dram_tensor("rec_dram", (E + P, RECW), F32).ap()
    return m


def project(nc, sem, m, tag, prepare, weight, width, finish, table=None, table_width=0, ends=None):
    s_in, s_tr, s_trc = sem(tag + "_staged"), sem(tag + "_turned"), sem(tag + "_turned_copied")
    s_mm, s_out = sem(tag + "_product"), sem(tag + "_out")
    s_store = [sem(f"{tag}_stored{k}") for k in range(2)]
    banks = -(-width // 512)
    step = width // banks
    with ExitStack() as ctx:
        staged = ctx.enter_context(nc.sbuf_tensor(tag + "_in", [P, 2, D], F32))
        rows_t = ctx.enter_context(nc.sbuf_tensor(tag + "_t", [P, 2, D], F32))
        out = ctx.enter_context(nc.sbuf_tensor(tag + "_o", [P, 2, width], F32))
        with nc.Block() as block:
            @block.vector
            def _(dve):
                def stage(t, k):
                    after(dve, s_tr, t - 1)
                    prepare(dve, staged[:, k, :], t)
                    dve.drain().then_inc(s_in, 1)

                def end(t, k, i):
                    if table is not None:
                        after(dve, s_store[k], i * 16)
                    dve.wait_ge(s_mm, t + 1)
                    finish(dve, out[:, k, :], m.ps_o[:, k, 0:banks, 0:step], t)
                    dve.drain().then_inc(s_out, 1)

                stage(0, 0)
                stage(1, 1)
                end(0, 0, 0)
                stage(2, 0)
                end(1, 1, 0)
                with dve.Fori(1, NT // 2 - 1) as i:
                    stage(i * 2 + 1, 1)
                    end(i * 2, 0, i)
                    stage(i * 2 + 2, 0)
                    end(i * 2 + 1, 1, i)
                stage(NT - 1, 1)
                end(NT - 2, 0, NT // 2 - 1)
                end(NT - 1, 1, NT // 2 - 1)

            @block.tensor
            def _(pe):
                def body(t, k, i):
                    pe.wait_ge(s_in, t + 1)
                    pe.transpose(m.ps_t[:, k, 0:P], staged[:, k, :], m.ident[:, :]).then_inc(s_tr, 1)
                    pe.wait_ge(s_trc, t + 1)
                    after(pe, s_out, t - 1)
                    for b in range(banks):
                        last = pe.matmul(m.ps_o[:, k, b, 0:step], rows_t[:, k, :],
                                         weight[:, b * step:(b + 1) * step], start=True, stop=True)
                    last.then_inc(s_mm, 1)
                in_pairs(pe, NT, body)

            @block.scalar
            def _(act):
                def body(t, k, i):
                    act.wait_ge(s_tr, t + 1)
                    after(act, s_mm, t - 1)
                    act.copy(rows_t[:, k, :], m.ps_t[:, k, 0:P]).then_inc(s_trc, 1)
                in_pairs(act, NT, body)
                if ends:
                    ends["scalar"](act)

            if ends:
                @block.gpsimd
                def _(pool):
                    ends["gpsimd"](pool)

            if table is not None:
                @block.sync
                def _(sp):
                    def body(t, k, i):
                        sp.wait_ge(s_out, t + 1)
                        sp.dma_start(table[bass.ds(t * P, P), :], out[:, k, 0:table_width]).then_inc(s_store[k], 16)
                    in_pairs(sp, NT, body)
                    if ends:
                        ends["sync"](sp)
                    for k in range(2):
                        sp.wait_ge(s_store[k], 16 * (NT // 2))


def project_rows(nc, sem, m, tag, prepare, weight, finish):
    B = 5
    s_in, s_tr, s_trc = sem(tag + "_staged"), sem(tag + "_turned"), sem(tag + "_turned_copied")
    s_mm, s_out = sem(tag + "_product"), sem(tag + "_out")
    turned = [m.ps_t, m.ps_k]
    with ExitStack() as ctx:
        staged = ctx.enter_context(nc.sbuf_tensor(tag + "_in", [P, 2, B, D], F32))
        rows_t = ctx.enter_context(nc.sbuf_tensor(tag + "_t", [P, 2, B, P], F32))
        with nc.Block() as block:
            @block.vector
            def _(dve):
                def stage(i, k):
                    after(dve, s_tr, i - 1)
                    prepare(dve, staged[:, k, :, :], bass.ds(i * B, B))
                    dve.drain().then_inc(s_in, 1)

                def body(i, k, _):
                    if within(i + 1, NT // B):
                        stage(i + 1, 1 - k)
                    apart(dve, s_mm, i + 1)
                    finish(dve, m.ps_o[:, k, 0, :].rearrange("p (b d) -> p b d", b=4), bass.ds(i * B, 4))
                    finish(dve, m.ps_o[:, k, 1, 0:D].unsqueeze(1), bass.ds(i * B + 4, 1))
                    dve.drain().then_inc(s_out, 1)
                stage(0, 0)
                in_rounds(dve, NT // B, 2, body)

            @block.tensor
            def _(pe):
                def body(i, k, _):
                    pe.wait_ge(s_in, i + 1)
                    for b in range(B):
                        last = pe.transpose(turned[k][:, b // 4, (b % 4) * P:(b % 4 + 1) * P], staged[:, k, b, :],
                                            m.ident[:, :])
                    last.then_inc(s_tr, 1)
                    pe.wait_ge(s_trc, i + 1)
                    after(pe, s_out, i - 1)
                    for b in range(B):
                        last = pe.matmul(m.ps_o[:, k, b // 4, (b % 4) * D:(b % 4 + 1) * D], rows_t[:, k, b, :],
                                         weight, start=True, stop=True)
                    last.then_inc(s_mm, 1)
                in_rounds(pe, NT // B, 2, body)

            @block.scalar
            def _(act):
                def body(i, k, _):
                    act.wait_ge(s_tr, i + 1)
                    after(act, s_mm, i - 1)
                    act.copy(rows_t[:, k, 0:4, :], turned[k][:, 0, :].rearrange("p (b n) -> p b n", b=4))
                    act.copy(rows_t[:, k, 4, :], turned[k][:, 1, 0:P]).then_inc(s_trc, 1)
                in_rounds(act, NT // B, 2, body)


def layer_norm(nc, sem, m, tag, rows, gain=None, shift=None, add=None):
    s_var, s_rstd = sem(tag + "_variance"), sem(tag + "_rstd")
    with ExitStack() as ctx:
        def sb(name, shape):
            return ctx.enter_context(nc.sbuf_tensor(tag + name, shape, F32))

        stats = sb("_stats", [P, NT, 6])
        mean, var, rstd, diff = (sb(n, [P, NT]) for n in ("_mean", "_var", "_rstd", "_diff"))
        with nc.Block() as block:
            @block.vector
            def _(dve):
                if add is not None:
                    dve.tensor_tensor(rows, rows, add, ALU.add)
                    dve.drain()
                with dve.Fori(0, NT // 10) as i:
                    for k in range(10):
                        dve.bn_stats(stats[:, bass.ds(i * 10 + k, 1), :], rows[:, bass.ds(i * 10 + k, 1), :])
                dve.drain()
                dve.tensor_tensor(mean[:, :], stats[:, :, 1], stats[:, :, 4], ALU.add)
                dve.tensor_tensor(diff[:, :], stats[:, :, 1], stats[:, :, 4], ALU.subtract)
                dve.tensor_tensor(var[:, :], stats[:, :, 2], stats[:, :, 5], ALU.add)
                dve.drain()
                dve.tensor_scalar(mean[:, :], mean[:, :], 0.5, None, ALU.mult)
                dve.tensor_tensor(diff[:, :], diff[:, :], diff[:, :], ALU.mult)
                dve.tensor_scalar(var[:, :], var[:, :], 1.0 / D, None, ALU.mult)
                dve.drain()
                dve.scalar_tensor_tensor(var[:, :], diff[:, :], 0.25, var[:, :], ALU.mult, ALU.add)
                dve.drain()
                dve.tensor_scalar(var[:, :], var[:, :], EPS, None, ALU.add).then_inc(s_var, 1)
                dve.wait_ge(s_rstd, 1)
                with dve.Fori(0, NT // 10) as i:
                    for k in range(10):
                        t = bass.ds(i * 10 + k, 1)
                        dve.tensor_scalar(rows[:, t, :], rows[:, t, :], mean[:, t], rstd[:, t], ALU.subtract, ALU.mult)
                if gain is not None:
                    dve.drain()
                    dve.tensor_tensor(rows, rows, gain.unsqueeze(1).broadcast_to([P, NT, D]), ALU.mult)
                    dve.drain()
                    dve.tensor_tensor(rows, rows, shift.unsqueeze(1).broadcast_to([P, NT, D]), ALU.add)

            @block.gpsimd
            def _(pool):
                pool.wait_ge(s_var, 1)
                pool.tensor_tensor(rstd[:, :], var[:, :], m.minus_half[:, 0:var.shape[1]], ALU.pow).then_inc(s_rstd, 1)


def score_pass(nc, sem, m, tag, table, width, heads, dot):
    s_idx, s_oh = sem(tag + "_indices"), sem(tag + "_one_hot")
    s_gather, base = m.s_gather, list(m.gathered)
    s_spill = [sem(f"{tag}_spilled{s}") for s in range(RING)]
    s_tr, s_trc, s_ex = sem(tag + "_turned"), sem(tag + "_turned_copied"), sem(tag + "_spread")
    s_used = sem(tag + "_used")
    s_st, s_st_tr, s_run, s_back = (sem(tag + n) for n in ("_scores_staged", "_scores_turned", "_run", "_run_back"))
    s_flag, s_sent = sem(tag + "_flagged"), sem(tag + "_sent")
    own = heads if not dot else D
    G = RING * U
    rows, w = G * heads, heads + 1
    HOTS = 2 * RING
    last_round = NG // RING - 1
    with ExitStack() as ctx:
        def sb(name, shape, dt=F32):
            return ctx.enter_context(nc.sbuf_tensor(tag + name, shape, dt))

        idx = sb("_idx", [P, RING, U], I32)
        got = sb("_got", [P, RING, U, width])
        hot = m.scratch[:, 0:HOTS * U * P].rearrange("p (s u n) -> p s u n", s=HOTS, u=U)
        hot_t = sb("_hot_t", [P, 2, U, P])
        dots = sb("_dots", [P, U, heads])
        value, last = sb("_value", [P, G, heads]), sb("_last", [P, G, heads])
        cut, run = sb("_cut", [rows, P]), sb("_run", [rows, P])
        sent, present, found = sb("_sent", [P, 2, G, w]), sb("_present", [P, G]), sb("_found", [P, G, heads])
        tops = m.scratch[:, HOTS * U * P:HOTS * U * P + U * NT * heads].rearrange("p (u t h) -> p u t h", u=U, t=NT)
        scores_t, scores_back = m.ps_o[0:rows, 0, 0, 0:2 * P], m.ps_o[:, 0, 1, 0:rows]
        with nc.Block() as block:
            @block.gpsimd
            def _(pool):
                def body(j, s8, i):
                    s = s8 % RING
                    apart(pool, s_idx, j + 1)
                    apart(pool, s_spill[s], i * 32 + 16 * (s8 // RING))
                    for u in range(U):
                        pool.indirect_dma_start(got[:, s, u, :], None, table, bass.IndirectOffsetOnAxis(
                            ap=idx[:, s, u:u + 1], axis=0)).then_inc(s_gather[s], 16)
                in_rounds(pool, NG, HOTS, body)

            @block.sync
            def _(sp):
                def body(j, s8, i):
                    s = s8 % RING
                    sp.wait_ge(s_gather[s], gathers_done(base[s], s8, i))
                    sp.dma_start(m.rows_dram[:, cols(j), :], got[:, s, :, 0:D]).then_inc(s_spill[s], 16)
                in_rounds(sp, NG, HOTS, body)
                for s in range(RING):
                    sp.wait_ge(s_spill[s], 16 * (NG // RING))

            @block.tensor
            def _(pe):
                def turn_scores(r):
                    apart(pe, s_st, r + 1)
                    apart(pe, s_run, r)
                    pe.transpose(scores_t[:, 0:P], value[:, :, :].rearrange("p g h -> p (g h)"), m.ident[:, :])
                    pe.transpose(scores_t[:, P:2 * P], last[:, :, :].rearrange("p g h -> p (g h)"), m.ident[:, :]
                                 ).then_inc(s_st_tr, 1)

                def turn_back(r):
                    apart(pe, s_run, r + 1)
                    apart(pe, s_flag, r)
                    pe.transpose(scores_back, run[:, :], m.ident[0:rows, 0:rows]).then_inc(s_back, 1)

                def send(r, k, q):
                    if q == 0:
                        apart(pe, s_flag, r + 1)
                    for u in range(U):
                        c = q * U + u
                        mm = pe.matmul(m.ps_o[:, 1, k, c * w:(c + 1) * w], hot[:, k * RING + q, u, :], sent[:, k, c, :],
                                       start=True, stop=True)
                    mm.then_inc(s_sent, 1)

                def turn(j, s8):
                    pe.wait_ge(s_oh, j + 1)
                    for u in range(U):
                        mm = pe.transpose(m.ps_t[:, s8 % 2, u * P:(u + 1) * P], hot[:, s8, u, :], m.ident[:, :])
                    mm.then_inc(s_tr, 1)

                def body(j, s8, i):
                    k, s, r, rk = s8 % 2, s8 % RING, i * 2 + (s8 // RING - 1), 1 - s8 // RING
                    tiles = tiles_of_chunks(nc, m, ENG.PE, j)
                    after(pe, s_used, j - 1)
                    pe.wait_ge(s_trc, j + 1)
                    for u in range(U):
                        to = (m.own if dot else m.a_d)[:, bass.ds(tiles[u], 1), 0:own]
                        mm = pe.matmul(m.ps_k[:, k, u * own:(u + 1) * own], hot_t[:, k, u, :], to,
                                       start=True, stop=True)
                    mm.then_inc(s_ex, 1)
                    if s == 1 and began(r):
                        turn_back(r)
                    if within(j + 1):
                        turn(j + 1, (s8 + 1) % HOTS)
                    if s == 0 and began(r - 1):
                        send(r - 1, 1 - rk, RING - 1)
                    if s == 0 and began(r):
                        turn_scores(r)
                    if s > 0 and began(r):
                        send(r, rk, s - 1)
                turn(0, 0)
                in_rounds(pe, NG, HOTS, body)
                send(last_round - 1, (last_round - 1) % 2, RING - 1)
                turn_scores(last_round)
                turn_back(last_round)
                for q in range(RING):
                    send(last_round, last_round % 2, q)

            @block.scalar
            def _(act):
                def stage_scores(r):
                    act.wait_ge(s_used, r * RING + RING)
                    after(act, s_st_tr, r)
                    here = bass.ds(r * G, G)
                    act.copy(value[:, :, :], m.R[:, here, R_BIAS:R_BIAS + heads])
                    act.copy(last[:, :, :], m.is_last[:, here].unsqueeze(2).broadcast_to([P, G, heads])
                             ).then_inc(s_st, 1)

                def body(j, s8, i):
                    r = i * 2 + (s8 // RING - 1)
                    if within(j + 1):
                        copy(j + 1, (s8 + 1) % 2)
                    if s8 % RING == 0 and began(r):
                        stage_scores(r)
                    if within(j + 2):
                        stage_one_hot(j + 2, (s8 + 2) % HOTS)

                def copy(j, k):
                    act.wait_ge(s_tr, j + 1)
                    after(act, s_ex, j - 1)
                    act.copy(hot_t[:, k, :, :], m.ps_t[:, k, :].rearrange("p (u e) -> p u e", u=U)).then_inc(s_trc, 1)

                def stage_one_hot(j, s8):
                    after(act, s_sent, j - 7)
                    one_hot_act(act, m, hot[:, s8, :, :], j).then_inc(s_oh, 1)
                stage_one_hot(0, 0)
                stage_one_hot(1, 1)
                copy(0, 0)
                in_rounds(act, NG, HOTS, body)
                stage_scores(last_round)

            @block.vector
            def _(dve):
                def stage_indices(j, s):
                    dve.tensor_copy(idx[:, s, :], m.src_idx[:, cols(j)]).then_inc(s_idx, 1)

                def score(j, s8, i):
                    k, s = s8 % 2, s8 % RING
                    dve.wait_ge(s_ex, j + 1)
                    dve.wait_ge(s_gather[s], gathers_done(base[s], s8, i))
                    at = m.R[:, cols(j), R_BIAS:R_BIAS + heads]
                    if not dot:
                        dve.tensor_tensor(dots[:, :, :], got[:, s, :, D:D + heads],
                                          m.ps_k[:, k, 0:U * own].rearrange("p (u h) -> p u h", u=U), ALU.add)
                        dve.drain()
                        dve.scalar_tensor_tensor(at, dots[:, :, :], 0.2, dots[:, :, :], ALU.mult, ALU.max)
                        dve.drain().then_inc(s_used, 1)
                        return
                    q = got[:, s, :, D:2 * D]
                    dve.tensor_tensor(q, q, m.ps_k[:, k, :].rearrange("p (u d) -> p u d", u=U), ALU.mult)
                    dve.drain()
                    dve.tensor_reduce(dots[:, :, :], q.rearrange("p u (h c) -> p u h c", h=heads), AX, ALU.add)
                    dve.drain()
                    dve.scalar_tensor_tensor(at, dots[:, :, :], float(D // heads) ** -0.5, at, ALU.mult, ALU.add)
                    dve.drain().then_inc(s_used, 1)

                def scan(r):
                    dve.wait_ge(s_st_tr, r + 1)
                    dve.tensor_scalar(cut[:, 1:P], scores_t[:, P:2 * P - 1], -BIG, None, ALU.mult)
                    dve.drain()
                    dve.tensor_tensor_scan(run[:, :], cut[:, :], scores_t[:, 0:P], -BIG, ALU.add, ALU.max)
                    dve.drain().then_inc(s_run, 1)

                def flag(r, k):
                    dve.wait_ge(s_back, r + 1)
                    flags = m.is_last[:, bass.ds(r * G, G)]
                    dve.tensor_tensor(sent[:, k, :, 0:heads], scores_back.rearrange("p (g h) -> p g h", g=G),
                                      flags.unsqueeze(2).broadcast_to([P, G, heads]), ALU.mult)
                    dve.tensor_copy(sent[:, k, :, heads], flags)
                    dve.drain().then_inc(s_flag, 1)

                def find(r, k):
                    dve.wait_ge(s_sent, r * RING + RING)
                    res = m.ps_o[:, 1, k, 0:G * w].rearrange("p (g w) -> p g w", g=G)
                    dve.tensor_scalar(present[:, :], res[:, :, heads], BIG, -BIG, ALU.mult, ALU.add)
                    dve.drain()
                    dve.tensor_tensor(found[:, :, :], res[:, :, 0:heads],
                                      present[:, :].unsqueeze(2).broadcast_to([P, G, heads]), ALU.add)
                    dve.drain()

                def take(r, q):
                    tiles = tiles_of_chunks(nc, m, ENG.DVE, r * RING + q)
                    for u in range(U):
                        top = tops[:, u, bass.ds(tiles[u], 1), :]
                        dve.tensor_tensor(top, top, found[:, q * U + u, :].unsqueeze(1), ALU.max)
                    dve.drain()

                def body(j, s8, i):
                    s, r, rk = s8 % RING, i * 2 + (s8 // RING - 1), 1 - s8 // RING
                    if s == 1 and began(r):
                        flag(r, rk)
                    score(j, s8, i)
                    if within(j + RING):
                        stage_indices(j + RING, s)
                    if s == 0 and began(r):
                        scan(r)
                    if s == 1 and began(r - 1):
                        find(r - 1, 1 - rk)
                    if s > 0 and began(r - 1):
                        take(r - 1, s - 1)
                    if s == RING - 1 and began(r - 1):
                        take(r - 1, s)

                dve.memset(cut[:, :], 0.0)
                dve.memset(tops[:, :, :, :], -BIG)
                for j in range(RING):
                    stage_indices(j, j)
                in_rounds(dve, NG, HOTS, body)
                scan(last_round)
                flag(last_round, last_round % 2)
                for r in (last_round - 1, last_round):
                    find(r, r % 2)
                    for q in range(RING):
                        take(r, q)
                dve.tensor_tensor(tops[:, 0:2, :, :], tops[:, 0:2, :, :], tops[:, 2:4, :, :], ALU.max)
                dve.drain()
                dve.tensor_tensor(tops[:, 0, :, :], tops[:, 0, :, :], tops[:, 1, :, :], ALU.max)
                dve.drain()
                dve.tensor_tensor(m.top[:, :, 0:heads], m.top[:, :, 0:heads], tops[:, 0, :, :], ALU.max)
    count_gathers(m)


def value_pass(nc, sem, m, tag, heads, count=False, pick=False):
    s_oh, s_rows = sem(tag + "_one_hot"), [sem(f"{tag}_rows{k}") for k in range(2)]
    s_tr, s_trc, s_ex = sem(tag + "_turned"), sem(tag + "_turned_copied"), sem(tag + "_spread")
    s_d, s_p, s_wr = sem(tag + "_differences"), sem(tag + "_weights"), sem(tag + "_weighted")
    s_sum, s_acc = sem(tag + "_summed"), sem(tag + "_added")
    W = D + heads + (NREL if count else 0)
    span = 2 * H0 if pick else heads
    with ExitStack() as ctx:
        def sb(name, shape):
            return ctx.enter_context(nc.sbuf_tensor(tag + name, shape, F32))

        hot = sb("_hot", [P, RING, U, P])
        hot_t = ctx.enter_context(nc.sbuf_tensor(tag + "_hot_t", [P, 2, U, P], BF16))
        parts = ctx.enter_context(nc.sbuf_tensor(tag + "_parts", [P, 3, NT, span], BF16))
        rest = sb("_rest", [P, NT, span])
        kind = sb("_kind", [P, RING, U, NREL])
        diff = sb("_diff", [P, 2, U, heads])
        rows = sb("_rows", [P, 2, U, D])
        weighted = sb("_weighted", [P, 2, U, W])
        with nc.Block() as block:
            @block.vector
            def _(dve):
                dve.memset(m.sums_odd[:, :, 0:W], 0.0)
                left = m.top[:, :, 0:span]
                for part in range(3):
                    dve.tensor_copy(parts[:, part, :, :], left)
                    dve.drain()
                    if part < 2:
                        dve.tensor_tensor(rest[:, :, :], left, parts[:, part, :, :], ALU.subtract)
                        dve.drain()
                        left = rest[:, :, :]
        with nc.Block() as block:
            @block.sync
            def _(sp):
                def body(j, s, i):
                    after(sp, s_wr, j - 1)
                    sp.dma_start(rows[:, s % 2, :, :], m.rows_dram[:, cols(j), :]).then_inc(s_rows[s % 2], 16)
                in_rounds(sp, NG, RING, body)

            @block.tensor
            def _(pe):
                def total(j, s):
                    k = s % 2
                    pe.wait_ge(s_wr, j + 1)
                    after(pe, s_acc, j - 1)
                    for u in range(U):
                        last = pe.matmul(m.ps_o[:, k, u // 2, (u % 2) * W:(u % 2 + 1) * W], hot[:, s, u, :],
                                         weighted[:, k, u, :], start=True, stop=True)
                    last.then_inc(s_sum, 1)

                def body(j, s, i):
                    k = s % 2
                    pe.wait_ge(s_oh, j + 1)
                    for u in range(U):
                        last = pe.transpose(m.ps_t[:, k, u * P:(u + 1) * P], hot[:, s, u, :], m.ident[:, :])
                    last.then_inc(s_tr, 1)
                    if began(j - 2):
                        total(j - 2, (s + 2) % RING)
                    tiles = tiles_of_chunks(nc, m, ENG.PE, j)
                    pe.wait_ge(s_trc, j + 1)
                    after(pe, s_d, j - 1)
                    for u in range(U):
                        for part in range(3):
                            last = pe.matmul(m.ps_k[:, k, u * span:(u + 1) * span], hot_t[:, k, u, :],
                                             parts[:, part, bass.ds(tiles[u], 1), :], start=(part == 0), stop=(part == 2))
                    last.then_inc(s_ex, 1)
                in_rounds(pe, NG, RING, body)
                total(NG - 2, RING - 2)
                total(NG - 1, RING - 1)

            @block.scalar
            def _(act):
                def copy(j, k):
                    act.wait_ge(s_tr, j + 1)
                    after(act, s_ex, j - 1)
                    act.copy(hot_t[:, k, :, :], m.ps_t[:, k, :].rearrange("p (u e) -> p u e", u=U)).then_inc(s_trc, 1)

                def body(j, s, i):
                    k = s % 2
                    if within(j + 1):
                        copy(j + 1, 1 - k)
                    after(act, s_sum, j - 1)
                    act.wait_ge(s_d, j + 1)
                    act.activation(weighted[:, k, :, D:D + heads], diff[:, k, :, :], ACT.Exp).then_inc(s_p, 1)
                    if within(j + 3):
                        stage(j + 3, (s + 3) % RING)

                def stage(j, s):
                    after(act, s_sum, j - 3)
                    one_hot_act(act, m, hot[:, s, :, :], j).then_inc(s_oh, 1)
                for j in range(3):
                    stage(j, j)
                copy(0, 0)
                in_rounds(act, NG, RING, body)

            @block.vector
            def _(dve):
                def add(j, k):
                    tiles = tiles_of_chunks(nc, m, ENG.DVE, j)
                    dve.wait_ge(s_sum, j + 1)
                    for u in range(U):
                        a = (m.acc, m.sums_odd)[u % 2][:, bass.ds(tiles[u], 1), 0:W]
                        dve.tensor_tensor(a, a, m.ps_o[:, k, u // 2, (u % 2) * W:(u % 2 + 1) * W].unsqueeze(1), ALU.add)
                        if u % 2 == 1 and u < U - 1:
                            dve.drain()

                def weigh(j, s, i):
                    k = s % 2
                    dve.wait_ge(s_rows[k], i * (16 * RING // 2) + 16 * (s // 2 + 1))
                    dve.wait_ge(s_p, j + 1)
                    if count:
                        kinds(dve, m, weighted[:, k, :, D + heads:W], j)
                    dve.tensor_tensor(weighted[:, k, :, 0:D].rearrange("p u (h c) -> p u h c", h=heads),
                                      rows[:, k, :, :].rearrange("p u (h c) -> p u h c", h=heads),
                                      weighted[:, k, :, D:D + heads].unsqueeze(3).broadcast_to([P, U, heads, D // heads]),
                                      ALU.mult)

                def differences(j, s):
                    k = s % 2
                    dve.wait_ge(s_ex, j + 1)
                    spread = m.ps_k[:, k, 0:U * span].rearrange("p (u h) -> p u h", u=U)
                    dve.tensor_tensor(diff[:, k, :, :], m.R[:, cols(j), R_BIAS:R_BIAS + heads], spread[:, :, 0:heads],
                                      ALU.subtract)
                    if pick:
                        dve.tensor_tensor(kind[:, s, :, :], kind[:, s, :, :], spread[:, :, H0:2 * H0], ALU.mult)

                def body(j, s, i):
                    if began(j - 2):
                        add(j - 2, s % 2)
                    weigh(j, s, i)
                    if within(j + 1):
                        differences(j + 1, (s + 1) % RING)
                    if pick:
                        dve.tensor_reduce(m.rel_w[:, cols(j)], kind[:, s, :, :], AX, ALU.add)
                        if within(j + 2):
                            kinds(dve, m, kind[:, (s + 2) % RING, :, :], j + 2)
                    dve.drain().then_inc(s_wr, 1)
                    if within(j + 1):
                        dve.sem_inc(s_d, 1)
                    if began(j - 2):
                        dve.sem_inc(s_acc, 1)

                if pick:
                    kinds(dve, m, kind[:, 0, :, :], 0)
                    kinds(dve, m, kind[:, 1, :, :], 1)
                    dve.drain()
                differences(0, 0)
                dve.drain().then_inc(s_d, 1)
                in_rounds(dve, NG, RING, body)
                for j in (NG - 2, NG - 1):
                    add(j, j % 2)
                    dve.drain()
                dve.tensor_tensor(m.acc[:, :, 0:W], m.acc[:, :, 0:W], m.sums_odd[:, :, 0:W], ALU.add)


def sum_pass(nc, sem, m, tag, table, indices, edge_weight=None):
    s_idx, s_oh, s_sum, s_acc = (sem(tag + n) for n in ("_indices", "_one_hot", "_summed", "_added"))
    s_gather, base = m.s_gather, list(m.gathered)
    with ExitStack() as ctx:
        def sb(name, shape, dt=F32):
            return ctx.enter_context(nc.sbuf_tensor(tag + name, shape, dt))

        idx, got, hot = sb("_idx", [P, RING, U], I32), sb("_got", [P, RING, U, D]), sb("_hot", [P, 2, U, P])
        with nc.Block() as block:
            @block.gpsimd
            def _(pool):
                def body(j, s, i):
                    apart(pool, s_idx, j + 1)
                    for u in range(U):
                        pool.indirect_dma_start(got[:, s, u, :], None, table, bass.IndirectOffsetOnAxis(
                            ap=idx[:, s, u:u + 1], axis=0)).then_inc(s_gather[s], 16)
                in_rounds(pool, NG, RING, body)

            @block.tensor
            def _(pe):
                def body(j, s, i):
                    k = s % 2
                    pe.wait_ge(s_oh, j + 1)
                    after(pe, s_acc, j - 1)
                    pe.wait_ge(s_gather[s], i * (16 * U) + (base[s] + 16 * U))
                    for u in range(U):
                        last = pe.matmul(m.ps_o[:, k, 0, u * D:(u + 1) * D], hot[:, k, u, :], got[:, s, u, :],
                                         start=True, stop=True)
                    last.then_inc(s_sum, 1)
                in_rounds(pe, NG, RING, body)

            @block.vector
            def _(dve):
                def stage_indices(j, s):
                    dve.tensor_copy(idx[:, s, :], indices[:, cols(j)]).then_inc(s_idx, 1)

                def stage_one_hot(j, k):
                    after(dve, s_sum, j - 1)
                    ins = one_hot(dve, m, hot[:, k, :, :], cols(j), U)
                    if edge_weight is not None:
                        dve.drain()
                        ins = dve.tensor_tensor(hot[:, k, :, :], hot[:, k, :, :],
                                                edge_weight[:, cols(j)].unsqueeze(2).broadcast_to([P, U, P]), ALU.mult)
                    ins.then_inc(s_oh, 1)

                def add(tiles, k):
                    for u in range(U):
                        a = m.acc[:, bass.ds(tiles[u], 1), 0:D]
                        dve.tensor_tensor(a, a, m.ps_o[:, k, 0, u * D:(u + 1) * D].unsqueeze(1), ALU.add)
                        dve.drain()
                    dve.sem_inc(s_acc, 1)

                def body(j, s, i):
                    if within(j + 1):
                        stage_one_hot(j + 1, (s + 1) % 2)
                    tiles = tiles_of_chunks(nc, m, ENG.DVE, j)
                    dve.wait_ge(s_sum, j + 1)
                    if within(j + RING):
                        stage_indices(j + RING, s)
                    add(tiles, s % 2)
                for j in range(RING):
                    stage_indices(j, j)
                stage_one_hot(0, 0)
                in_rounds(dve, NG, RING, body)
    count_gathers(m)


def feed_forward(nc, sem, m, rows, out):
    B = 5
    s_in, s_tr, s_trc, s_h = sem("ff_staged"), sem("ff_turned"), sem("ff_turned_copied"), sem("ff_hidden")
    s_var, s_rstd, s_n = sem("ff_variance"), sem("ff_rstd"), sem("ff_normed")
    s_gt, s_gtc, s_y, s_out = sem("ff_normed_turned"), sem("ff_gelu"), sem("ff_product"), sem("ff_out")
    C = FFN // P
    banks = [m.ps_o[:, 0, 0, :], m.ps_o[:, 0, 1, :], m.ps_o[:, 1, 0, :], m.ps_o[:, 1, 1, :], m.ps_k[:, 0, :]]
    with ExitStack() as ctx:
        def sb(name, shape):
            return ctx.enter_context(nc.sbuf_tensor("ff_" + name, shape, F32))

        x = sb("x", [P, 2, B, D])
        product, product_last = m.ps_k[:, 1, :].rearrange("p (b d) -> p b d", b=4), m.ps_t[:, 1, P:P + D]
        hid = m.scratch[:, 0:B * FFN].rearrange("p (b f) -> p b f", b=B)
        hid_t = m.scratch[:, B * FFN:2 * B * FFN].rearrange("p (c b n) -> p c b n", b=B, c=C)
        x_t = sb("x_t", [P, B, P])
        stats, mean, var, rstd, diff = sb("stats", [P, B, 6]), *(sb(n, [P, B]) for n in ("mean", "var", "rstd", "diff"))
        with nc.Block() as block:
            @block.vector
            def _(dve):
                def stage(i, k):
                    dve.tensor_copy(x[:, k, :, :], rows[:, bass.ds(i * B, B), :])
                    dve.drain().then_inc(s_in, 1)

                def residual(i, k):
                    at = x[:, k, :, :]
                    dve.tensor_tensor(at, at, m.b_f2[:, :].unsqueeze(1).broadcast_to([P, B, D]), ALU.add)
                    dve.drain()
                    dve.wait_ge(s_y, i + 1)
                    dve.tensor_tensor(out[:, bass.ds(i * B, 4), :], at[:, 0:4, :], product, ALU.add)
                    dve.tensor_tensor(out[:, bass.ds(i * B + 4, 1), :], at[:, 4:5, :], product_last.unsqueeze(1), ALU.add)
                    dve.drain().then_inc(s_out, 1)

                def body(i, k, _):
                    for b in range(B):
                        dve.wait_ge(s_h, i * B + (b + 1))
                        dve.tensor_tensor(hid[:, b, :], banks[b], m.b_f1[:, :], ALU.add)
                    dve.drain()
                    for b in range(B):
                        dve.bn_stats(stats[:, b, :], hid[:, b, :])
                    dve.drain()
                    dve.tensor_tensor(mean[:, :], stats[:, :, 1], stats[:, :, 4], ALU.add)
                    dve.tensor_tensor(diff[:, :], stats[:, :, 1], stats[:, :, 4], ALU.subtract)
                    dve.tensor_tensor(var[:, :], stats[:, :, 2], stats[:, :, 5], ALU.add)
                    dve.drain()
                    dve.tensor_scalar(mean[:, :], mean[:, :], 0.5, None, ALU.mult)
                    dve.tensor_tensor(diff[:, :], diff[:, :], diff[:, :], ALU.mult)
                    dve.tensor_scalar(var[:, :], var[:, :], 1.0 / FFN, None, ALU.mult)
                    dve.drain()
                    dve.scalar_tensor_tensor(var[:, :], diff[:, :], 0.25, var[:, :], ALU.mult, ALU.add)
                    dve.drain()
                    dve.tensor_scalar(var[:, :], var[:, :], EPS, None, ALU.add).then_inc(s_var, 1)
                    dve.wait_ge(s_rstd, i + 1)
                    for b in range(B):
                        dve.tensor_scalar(hid[:, b, :], hid[:, b, :], mean[:, b:b + 1], rstd[:, b:b + 1],
                                          ALU.subtract, ALU.mult)
                    dve.drain().then_inc(s_n, 1)
                    if began(i - 1):
                        residual(i - 1, 1 - k)
                    if within(i + 1, NT // B):
                        stage(i + 1, 1 - k)
                stage(0, 0)
                in_rounds(dve, NT // B, 2, body)
                residual(NT // B - 1, 1)

            @block.gpsimd
            def _(pool):
                with pool.Fori(0, NT // B) as i:
                    apart(pool, s_var, i + 1)
                    pool.tensor_tensor(rstd[:, :], var[:, :], m.minus_half[:, 0:var.shape[1]], ALU.pow).then_inc(s_rstd, 1)

            @block.tensor
            def _(pe):
                def second(i):
                    pe.wait_ge(s_gtc, i * C + C)
                    after(pe, s_out, i)
                    for b in range(B):
                        for c in range(C):
                            mm = pe.matmul(product[:, b, :] if b < 4 else product_last, hid_t[:, c, b, :],
                                           m.w_f2[:, c, :], start=(c == 0), stop=(c == C - 1))
                    mm.then_inc(s_y, 1)

                def body(i, k, _):
                    pe.wait_ge(s_in, i + 1)
                    for b in range(B):
                        mm = pe.transpose(m.ps_t[:, b // 4, (b % 4) * P:(b % 4 + 1) * P], x[:, k, b, :], m.ident[:, :])
                    mm.then_inc(s_tr, 1)
                    pe.wait_ge(s_trc, i * 2 + 2)
                    after(pe, s_gtc, i * C)
                    for b in range(B):
                        pe.matmul(banks[b], x_t[:, b, :], m.w_f1[:, :], start=True, stop=True).then_inc(s_h, 1)
                    if began(i - 1):
                        second(i - 1)
                    pe.wait_ge(s_n, i + 1)
                    for c in range(C):
                        for b in range(B):
                            to = banks[c][:, b * P:(b + 1) * P] if b < 4 else banks[4][:, c * P:(c + 1) * P]
                            mm = pe.transpose(to, hid[:, b, c * P:(c + 1) * P], m.ident[:, :])
                        mm.then_inc(s_gt, 1)
                in_rounds(pe, NT // B, 2, body)
                second(NT // B - 1)

            @block.scalar
            def _(act):
                with act.Fori(0, NT // B) as i:
                    act.wait_ge(s_tr, i + 1)
                    act.copy(x_t[:, 0:4, :], m.ps_t[:, 0, :].rearrange("p (b n) -> p b n", b=4)).then_inc(s_trc, 1)
                    act.copy(x_t[:, 4, :], m.ps_t[:, 1, 0:P]).then_inc(s_trc, 1)
                    for c in range(C):
                        act.wait_ge(s_gt, i * C + (c + 1))
                        act.activation(hid_t[:, c, 0:4, :], banks[c].rearrange("p (b n) -> p b n", b=4), ACT.Gelu,
                                       bias=m.b_lnf[:, c:c + 1], scale=m.g_lnf[:, c:c + 1])
                    for c in range(C):
                        act.activation(hid_t[:, c, 4, :], banks[4][:, c * P:(c + 1) * P], ACT.Gelu,
                                       bias=m.b_lnf[:, c:c + 1], scale=m.g_lnf[:, c:c + 1]).then_inc(s_gtc, 1)


def heads_of(rows, heads):
    return rows.rearrange("p t (h c) -> p t h c", h=heads)


def spread_heads(m, at, heads):
    return m.acc[:, at, D:D + heads].unsqueeze(3).broadcast_to([P, m.acc[:, at, D:D + heads].shape[1], heads, D // heads])


def project_attention(nc, sem, m, ends):
    def prepare(dve, staged, t):
        dve.tensor_copy(staged.unsqueeze(1), m.X[:, bass.ds(t, 1), :])

    def finish(dve, out, product, t):
        dve.tensor_tensor(out.unsqueeze(1), product, m.b_vqk[:, :].unsqueeze(1), ALU.add)
        dve.drain()
        dve.tensor_copy(m.own[:, bass.ds(t, 1), :], out[:, 2 * D:3 * D].unsqueeze(1))

    project(nc, sem, m, "vqk", prepare, m.w_vqk[:, :], 3 * D, finish, m.table_vq, 2 * D, ends)


def attention_layer(nc, sem, m):
    with nc.Block() as block:
        @block.vector
        def _(dve):
            dve.memset(m.top[:, :, :], -BIG)
    score_pass(nc, sem, m, "a0", m.table_vq, 2 * D, H0, True)

    with nc.Block() as block:
        @block.vector
        def _(dve):
            dve.memset(m.acc[:, :, :], 0.0)
    value_pass(nc, sem, m, "v0", H0, count=True)

    s_deg = sem("degrees")
    with nc.Block() as block:
        @block.vector
        def _(dve):
            counts = m.acc[:, :, D + H0:D + H0 + NREL]
            dve.tensor_reduce(m.dinv[:, :], counts, AX, ALU.add)
            dve.drain()
            dve.tensor_scalar(m.dinv[:, :], m.dinv[:, :], 1.0, None, ALU.add).then_inc(s_deg, 1)
            den = m.acc[:, :, D:D + H0]
            dve.tensor_scalar(den, den, 1e-8, None, ALU.max)
            dve.tensor_scalar(counts, counts, 1.0, None, ALU.max)
            dve.drain()
            dve.reciprocal(den, den)
            dve.reciprocal(m.top[:, :, H0:2 * H0], counts)

        @block.gpsimd
        def _(pool):
            pool.wait_ge(s_deg, 1)
            pool.tensor_tensor(m.dinv[:, :], m.dinv[:, :], m.minus_half[:, :], ALU.pow)

    def normalised(dve, staged, at):
        dve.tensor_tensor(heads_of(staged, H0), heads_of(m.acc[:, at, 0:D], H0), spread_heads(m, at, H0), ALU.mult)

    def residual(dve, product, at):
        rows = m.own[:, at, :]
        dve.tensor_tensor(rows, product, m.X[:, at, :], ALU.add)
        dve.drain()
        dve.tensor_tensor(rows, rows, m.b_o[:, :].unsqueeze(1).broadcast_to([P, rows.shape[1], D]), ALU.add)

    project_rows(nc, sem, m, "oproj", normalised, m.w_o[:, :], residual)
    layer_norm(nc, sem, m, "ln1", m.own[:, :, :], m.g_ln1[:, :], m.b_ln1[:, :])
    feed_forward(nc, sem, m, m.own, m.own)
    layer_norm(nc, sem, m, "ln2", m.own[:, :, :], m.g_ln2[:, :], m.b_ln2[:, :])
    layer_norm(nc, sem, m, "ln_l0", m.X[:, :, :], add=m.own[:, :, :])


def appnp_layer(nc, m):
    h = m.acc[:, :, 0:D]
    hops = 5
    parts = [(0, NT // 2), (NT // 2, NT)]
    rows = m.table_h.rearrange("(t p) d -> p t d", p=P)
    for hop in range(hops + 1):
        with semaphores(nc) as sem:
            s_own, s_tab = sem(f"hop{hop}_scaled"), sem(f"hop{hop}_stored")
            with nc.Block() as block:
                @block.vector
                def _(dve):
                    if hop == 0:
                        dve.tensor_scalar(m.dinv_part[:, :], m.dinv[:, :], 1.0 - 0.8, None, ALU.mult)
                    for a, b in parts:
                        dinv = m.dinv[:, a:b].unsqueeze(2).broadcast_to([P, b - a, D])
                        if hop > 0:
                            dve.tensor_tensor(h[:, a:b, :], h[:, a:b, :],
                                              m.dinv_part[:, a:b].unsqueeze(2).broadcast_to([P, b - a, D]), ALU.mult)
                            dve.drain()
                            dve.scalar_tensor_tensor(h[:, a:b, :], m.X[:, a:b, :], 0.8, h[:, a:b, :], ALU.mult, ALU.add)
                            dve.drain()
                        if hop < hops:
                            now = m.X if hop == 0 else h
                            dve.tensor_tensor(m.own[:, a:b, :], now[:, a:b, :], dinv, ALU.mult)
                            dve.drain().then_inc(s_own, 1)

                if hop < hops:
                    @block.scalar
                    def _(act):
                        for n, (a, b) in enumerate(parts):
                            act.wait_ge(s_own, n + 1)
                            act.copy(h[:, a:b, :], m.own[:, a:b, :])

                    @block.sync
                    def _(sp):
                        for n, (a, b) in enumerate(parts):
                            sp.wait_ge(s_own, n + 1)
                            sp.dma_start(rows[:, a:b, :], m.own[:, a:b, :]).then_inc(s_tab, 16)
                        sp.wait_ge(s_tab, 16 * len(parts))
            if hop < hops:
                sum_pass(nc, sem, m, f"p{hop}", m.table_h, m.src_idx)
            else:
                layer_norm(nc, sem, m, "ln_l1", m.X[:, :, :], add=h)


def gat_conv(nc, sem, m, tag, prepare, weight, a_src, a_dst, heads, pick):
    def finish(dve, product, at):
        dve.tensor_copy(m.own[:, at, :], product)

    project_rows(nc, sem, m, tag + "w", prepare, weight[:, :], finish)
    s_tab, s_exp, s_self = sem(tag + "_table"), sem(tag + "_self_exp"), sem(tag + "_self")
    s_a = sem(tag + "_source_scores")
    own_score = m.own_score[:, :, 0:heads]
    loop = m.has_loop[:, :].unsqueeze(2).broadcast_to([P, NT, heads])
    with nc.Block() as block:
        @block.sync
        def _(sp):
            rows = m.table_g.rearrange("(t p) d -> p t d", p=P)
            sp.dma_start(rows[:, :, 0:D], m.own[:, :, :]).then_inc(s_tab, 16)
            sp.wait_ge(s_a, 1)
            sp.dma_start(rows[:, :, D:D + 4], m.a_s[:, :, :]).then_inc(s_tab, 16)
            sp.wait_ge(s_tab, 32)

        @block.vector
        def _(dve):
            products = m.acc[:, :, 0:D]
            for a, to in ((a_src, m.a_s), (a_dst, m.a_d)):
                dve.tensor_tensor(products, m.own[:, :, :], a[:, :].unsqueeze(1).broadcast_to([P, NT, D]), ALU.mult)
                dve.drain()
                dve.tensor_reduce(to[:, :, 0:heads], heads_of(products, heads), AX, ALU.add)
                dve.drain().then_inc(s_a, 1)
            top = m.top[:, :, 0:heads]
            dve.tensor_tensor(top, m.a_s[:, :, 0:heads], m.a_d[:, :, 0:heads], ALU.add)
            dve.drain()
            dve.scalar_tensor_tensor(own_score, top, 0.2, top, ALU.mult, ALU.max)
            dve.tensor_scalar(m.loop_off[:, :], m.has_loop[:, :], BIG, -BIG, ALU.mult, ALU.add)
            dve.drain()
            dve.tensor_tensor(top, own_score, loop, ALU.mult)
            dve.drain()
            dve.tensor_tensor(top, top, m.loop_off[:, :].unsqueeze(2).broadcast_to([P, NT, heads]), ALU.add)
    score_pass(nc, sem, m, tag + "s", m.table_g, D + 4, heads, False)
    with nc.Block() as block:
        @block.vector
        def _(dve):
            den = m.acc[:, :, D:D + heads]
            dve.tensor_tensor(own_score, own_score, m.top[:, :, 0:heads], ALU.subtract)
            dve.drain()
            dve.tensor_scalar(own_score, own_score, 0.0, None, ALU.min)
            dve.drain().then_inc(s_self, 1)
            dve.wait_ge(s_exp, 1)
            dve.tensor_tensor(den, own_score, loop, ALU.mult)
            dve.drain()
            dve.tensor_tensor(heads_of(m.acc[:, :, 0:D], heads), heads_of(m.own[:, :, :], heads),
                              spread_heads(m, bass.ds(0, NT), heads), ALU.mult)

        @block.scalar
        def _(act):
            act.wait_ge(s_self, 1)
            act.activation(own_score, own_score, ACT.Exp).then_inc(s_exp, 1)
    value_pass(nc, sem, m, tag + "v", heads, pick=pick)
    with nc.Block() as block:
        @block.vector
        def _(dve):
            den = m.acc[:, :, D:D + heads]
            dve.tensor_scalar(den, den, 1e-16, None, ALU.add)
            dve.drain()
            dve.reciprocal(den, den)


def gat_layer(nc, m):
    def prepare_x(dve, staged, at):
        dve.tensor_copy(staged, m.X[:, at, :])

    def prepare_h(dve, staged, at):
        dve.tensor_copy(staged, m.own[:, at, :])

    def rows_of_sums(dve, to, heads, bias):
        dve.tensor_tensor(heads_of(to, heads), heads_of(m.acc[:, :, 0:D], heads),
                          spread_heads(m, bass.ds(0, NT), heads), ALU.mult)
        dve.drain()
        dve.tensor_tensor(to, to, bias[:, :].unsqueeze(1).broadcast_to([P, NT, D]), ALU.add)
        dve.drain()

    with semaphores(nc) as sem:
        gat_conv(nc, sem, m, "g1", prepare_x, m.w_g1, m.a_src1, m.a_dst1, 4, True)
        s_m, s_e = sem("elu_min"), sem("elu_exp")
        with nc.Block() as block:
            @block.vector
            def _(dve):
                low = m.acc[:, :, 0:D]
                rows_of_sums(dve, m.own[:, :, :], 4, m.b_g1)
                dve.tensor_scalar(low, m.own[:, :, :], 0.0, None, ALU.min).then_inc(s_m, 1)
                dve.wait_ge(s_e, 1)
                dve.scalar_tensor_tensor(m.own[:, :, :], low, -1.0, m.own[:, :, :], ALU.add, ALU.max)

            @block.scalar
            def _(act):
                act.wait_ge(s_m, 1)
                act.activation(m.acc[:, :, 0:D], m.acc[:, :, 0:D], ACT.Exp).then_inc(s_e, 1)

    with semaphores(nc) as sem:
        gat_conv(nc, sem, m, "g2", prepare_h, m.w_g2, m.a_src2, m.a_dst2, 1, False)
        with nc.Block() as block:
            @block.vector
            def _(dve):
                rows_of_sums(dve, m.acc[:, :, 0:D], 1, m.b_g2)
        layer_norm(nc, sem, m, "ln_l2", m.X[:, :, :], add=m.acc[:, :, 0:D])


def relational_layer(nc, sem, m):
    def prepare(dve, staged, t):
        dve.tensor_copy(staged.unsqueeze(1), m.X[:, bass.ds(t, 1), :])

    def per_relation(dve, out, product, t):
        dve.tensor_copy(out.rearrange("p (b n) -> p b n", b=2), product)

    def prepare_root(dve, staged, at):
        dve.tensor_copy(staged, m.X[:, at, :])

    def root(dve, product, at):
        rows = m.acc[:, at, 0:D]
        dve.tensor_tensor(rows, product, m.b_rel[:, :].unsqueeze(1).broadcast_to([P, rows.shape[1], D]), ALU.add)

    project(nc, sem, m, "rel", prepare, m.w_rel[:, 0:NREL, :].rearrange("k r n -> k (r n)"), NREL * D, per_relation,
            m.table_r.rearrange("(n r) d -> n (r d)", r=NREL), NREL * D)
    project_rows(nc, sem, m, "root", prepare_root, m.w_rel[:, NREL, :], root)
    sum_pass(nc, sem, m, "r", m.table_r, m.rel_idx, m.rel_w)
    layer_norm(nc, sem, m, "ln_l3", m.X[:, :, :], add=m.acc[:, :, 0:D])


def store_output(nc, sem, m, out):
    s_out = sem("output_stored")
    with nc.Block() as block:
        @block.sync
        def _(sp):
            sp.dma_start(out[0:FULL * P, :].rearrange("(t p) d -> p t d", p=P), m.X[:, 0:FULL, :]).then_inc(s_out, 16)
            sp.dma_start(out[FULL * P:N, :], m.X[0:TAIL, FULL, :]).then_inc(s_out, 16)
            sp.wait_ge(s_out, 32)


def build(nc, A, out, stages=4):
    with ExitStack() as ctx:
        m = allocate(nc, ctx)
        m.s_gather = [ctx.enter_context(nc.semaphore(f"gathered{k}")) for k in range(RING)]
        m.gathered = [0] * RING
        with semaphores(nc) as sem:
            load_constants(nc, m, A, sem)
            build_records(nc, m, A, sem)
            plan_chunks(nc, m, A, sem, lambda ends: project_attention(nc, sem, m, ends))
        with semaphores(nc) as sem:
            attention_layer(nc, sem, m)
        if stages > 1:
            appnp_layer(nc, m)
        if stages > 2:
            gat_layer(nc, m)
        if stages > 3:
            with semaphores(nc) as sem:
                relational_layer(nc, sem, m)
        with semaphores(nc) as sem:
            store_output(nc, sem, m, out)


_INS = ['x', 'src', 'dst', 'edge_attr_32', 'edge_type_8', 'L0_gnn_qW', 'L0_gnn_qb', 'L0_gnn_kW', 'L0_gnn_kb',
        'L0_gnn_vW', 'L0_gnn_vb', 'L0_gnn_eW', 'L0_gnn_eb', 'L0_gnn_oW', 'L0_gnn_ob', 'L0_gnn_ln1_g',
        'L0_gnn_ln1_b', 'L0_gnn_f1W', 'L0_gnn_f1b', 'L0_gnn_lnf_g', 'L0_gnn_lnf_b', 'L0_gnn_f2W', 'L0_gnn_f2b',
        'L0_gnn_ln2_g', 'L0_gnn_ln2_b', 'L2_gnn_W1', 'L2_gnn_a_src1', 'L2_gnn_a_dst1', 'L2_gnn_b1', 'L2_gnn_W2',
        'L2_gnn_a_src2', 'L2_gnn_a_dst2', 'L2_gnn_b2', 'L3_gnn_weight', 'L3_gnn_root', 'L3_gnn_bias']
_OUTS = [((N, D), 'float32')]


def kernel(**inputs):
    import numpy as _np
    import concourse.bacc as _bacc
    from concourse import mybir as _mybir
    from concourse.bass_utils import run_bass_kernel_spmd as _run

    nc = _bacc.Bacc("TRN2", target_bir_lowering=False, num_devices=1)
    arrays, args = {}, {}
    for name in _INS:
        a = _np.ascontiguousarray(inputs[name])
        arrays[f"in_{name}_dram"] = a
        args[name] = nc.dram_tensor(f"in_{name}_dram", a.shape, _mybir.dt.from_np(a.dtype), kind="ExternalInput").ap()
    outs = []
    for i, (shape, dtype) in enumerate(_OUTS):
        dt = _mybir.dt.from_np(_np.dtype(dtype))
        outs.append(nc.dram_tensor(f"out_{i}_dram", shape, dt, kind="ExternalOutput").ap())
    build(nc, args, outs[0])
    r = _run(nc, [arrays], core_ids=[0])
    got = tuple(r.results[0][f"out_{i}_dram"] for i in range(len(_OUTS)))
    return got[0]
```
